# Optimizing a Trainium2 kernel written in Bass

```python
import numpy as np
import jax
import jax.numpy as jnp

def _softmax(x, axis=-1):
    return jax.nn.softmax(x, axis=axis)

def _gelu(x):
    return jax.nn.gelu(x, approximate=True)

def _silu(x):
    return jax.nn.silu(x)

def _sigmoid(x):
    return jax.nn.sigmoid(x)

def _layernorm(x, axis=-1, eps=1e-05):
    m = jnp.mean(x, axis=axis, keepdims=True)
    v = jnp.var(x, axis=axis, keepdims=True)
    return (x - m) / jnp.sqrt(v + eps)

def _scatter_add(tgt, idx, src, axis=0):
    return tgt.at[idx].add(src)

def _segment_sum(src, seg, n):
    return jax.ops.segment_sum(src, seg, n)
kernel_name = 'mk_recurrent_d1_jaxref_r4_035958'

def setup_inputs(seed: int=0):
    np.random.seed(seed)
    _w = jnp.asarray

    def _L0_attn_setup():
        import jax, jax.numpy as jnp
        import numpy as np
        D_MODEL = 256
        N_HEADS = 16
        D_HEAD = D_MODEL // N_HEADS
        EPS = 1e-05

        @jax.custom_vjp
        def spike(x):
            return (x >= 0).astype(x.dtype)

        def _spike_fwd(x):
            return (spike(x), x)

        def _spike_bwd(x, g):
            return (g / (1.0 + (jnp.pi * x) ** 2),)
        spike.defvjp(_spike_fwd, _spike_bwd)

        def lif(x, v_th):
            return spike(x - v_th)

        def layer_norm(x, g, b):
            mu = jnp.mean(x, axis=-1, keepdims=True)
            var = jnp.mean((x - mu) ** 2, axis=-1, keepdims=True)
            return (x - mu) * jax.lax.rsqrt(var + EPS) * g + b

        def log_pe_bias(n_q, n_k):
            pos_q = jnp.arange(n_q)[:, None]
            pos_k = jnp.arange(n_k)[None, :]
            dist = jnp.abs(pos_q - pos_k).astype(jnp.float32)
            max_len = max(n_q, n_k)
            bias = jnp.ceil(jnp.log2((max_len - 1) / (dist + 1.0)))
            return jnp.maximum(bias, 0.0)
        key = jax.random.key(seed)
        ks = jax.random.split(key, 16)
        D = D_MODEL
        std = 1.0 / np.sqrt(D)
        inp = {'query': jax.random.normal(ks[0], (2, 512, D), dtype=jnp.float32), 'Wq': jax.random.normal(ks[1], (D, D), dtype=jnp.float32) * std, 'bq': jnp.zeros((D,), jnp.float32), 'Wk': jax.random.normal(ks[2], (D, D), dtype=jnp.float32) * std, 'bk': jnp.zeros((D,), jnp.float32), 'Wv': jax.random.normal(ks[3], (D, D), dtype=jnp.float32) * std, 'bv': jnp.zeros((D,), jnp.float32), 'Wo': jax.random.normal(ks[4], (D, D), dtype=jnp.float32) * std, 'bo': jnp.zeros((D,), jnp.float32), 'gq': jnp.ones((D,), jnp.float32), 'betaq': jnp.zeros((D,), jnp.float32), 'gk': jnp.ones((D,), jnp.float32), 'betak': jnp.zeros((D,), jnp.float32), 'gv': jnp.ones((D,), jnp.float32), 'betav': jnp.zeros((D,), jnp.float32), 'go': jnp.ones((D,), jnp.float32), 'betao': jnp.zeros((D,), jnp.float32), 'scale': jnp.asarray(np.sqrt(1.0 / D_HEAD), jnp.float32)}
        return inp
    _L0_attn_in = _L0_attn_setup()

    def _L0_ffn_setup():
        import jax, jax.numpy as jnp
        import numpy as np
        EPS = 1e-06
        N_EXPERTS = 8

        def _rms_norm(x, scale, eps=EPS):
            mean_sq = jnp.mean(x.astype(jnp.float32) ** 2, axis=-1, keepdims=True)
            s = scale.astype(jnp.float32) * jax.lax.rsqrt(mean_sq + eps)
            return x * s.astype(x.dtype)

        def _dist2(x, y):
            nx = jnp.sum(x ** 2, axis=-1)[..., :, None]
            ny = jnp.sum(y ** 2, axis=-1)[..., None, :]
            return nx + ny - 2.0 * (x @ y.T)
        key = jax.random.key(seed)
        ks = jax.random.split(key, 5)
        dim, hidden, E = (256, 512, N_EXPERTS)
        x = jax.random.normal(ks[0], (4, 512, dim), dtype=jnp.float32)
        scale = jnp.ones((dim,), dtype=jnp.float32)
        centroids = jax.random.normal(ks[1], (E, dim), dtype=jnp.float32)
        up_w = jax.random.normal(ks[2], (E, dim, hidden * 2), dtype=jnp.float32) * dim ** (-0.5)
        down_w = jax.random.normal(ks[3], (E, hidden, dim), dtype=jnp.float32) * hidden ** (-0.5)
        return {'x': x, 'scale': scale, 'centroids': centroids, 'up_w': up_w, 'down_w': down_w}
    _L0_ffn_in = _L0_ffn_setup()
    _d = {'L0_attn_query': _L0_attn_in['query'], 'L0_attn_Wq': _L0_attn_in['Wq'], 'L0_attn_bq': _L0_attn_in['bq'], 'L0_attn_Wk': _L0_attn_in['Wk'], 'L0_attn_bk': _L0_attn_in['bk'], 'L0_attn_Wv': _L0_attn_in['Wv'], 'L0_attn_bv': _L0_attn_in['bv'], 'L0_attn_Wo': _L0_attn_in['Wo'], 'L0_attn_bo': _L0_attn_in['bo'], 'L0_attn_gq': _L0_attn_in['gq'], 'L0_attn_betaq': _L0_attn_in['betaq'], 'L0_attn_gk': _L0_attn_in['gk'], 'L0_attn_betak': _L0_attn_in['betak'], 'L0_attn_gv': _L0_attn_in['gv'], 'L0_attn_betav': _L0_attn_in['betav'], 'L0_attn_go': _L0_attn_in['go'], 'L0_attn_betao': _L0_attn_in['betao'], 'L0_attn_scale': _L0_attn_in['scale'], 'L0_ffn_scale': _L0_ffn_in['scale'], 'L0_ffn_centroids': _L0_ffn_in['centroids'], 'L0_ffn_up_w': _L0_ffn_in['up_w'], 'L0_ffn_down_w': _L0_ffn_in['down_w']}
    _x0 = _d['L0_attn_query']
    _d['L0_attn_query'] = jax.random.normal(jax.random.fold_in(jax.random.key(seed), 1), (1, 4096, 256), dtype=_x0.dtype)
    del _x0
    return _d

def reference(L0_attn_query, L0_attn_Wq, L0_attn_bq, L0_attn_Wk, L0_attn_bk, L0_attn_Wv, L0_attn_bv, L0_attn_Wo, L0_attn_bo, L0_attn_gq, L0_attn_betaq, L0_attn_gk, L0_attn_betak, L0_attn_gv, L0_attn_betav, L0_attn_go, L0_attn_betao, L0_attn_scale, L0_ffn_scale, L0_ffn_centroids, L0_ffn_up_w, L0_ffn_down_w):

    def _L0_attn_ref(query, Wq, bq, Wk, bk, Wv, bv, Wo, bo, gq, betaq, gk, betak, gv, betav, go, betao, scale):
        import jax, jax.numpy as jnp
        import numpy as np
        D_MODEL = 256
        N_HEADS = 16
        D_HEAD = D_MODEL // N_HEADS
        EPS = 1e-05

        @jax.custom_vjp
        def spike(x):
            return (x >= 0).astype(x.dtype)

        def _spike_fwd(x):
            return (spike(x), x)

        def _spike_bwd(x, g):
            return (g / (1.0 + (jnp.pi * x) ** 2),)
        spike.defvjp(_spike_fwd, _spike_bwd)

        def lif(x, v_th):
            return spike(x - v_th)

        def layer_norm(x, g, b):
            mu = jnp.mean(x, axis=-1, keepdims=True)
            var = jnp.mean((x - mu) ** 2, axis=-1, keepdims=True)
            return (x - mu) * jax.lax.rsqrt(var + EPS) * g + b

        def log_pe_bias(n_q, n_k):
            pos_q = jnp.arange(n_q)[:, None]
            pos_k = jnp.arange(n_k)[None, :]
            dist = jnp.abs(pos_q - pos_k).astype(jnp.float32)
            max_len = max(n_q, n_k)
            bias = jnp.ceil(jnp.log2((max_len - 1) / (dist + 1.0)))
            return jnp.maximum(bias, 0.0)
        B, N, D = query.shape
        H, Dh = (N_HEADS, D_HEAD)
        Q = lif(layer_norm(query @ Wq.T + bq, gq, betaq), 1.0)
        K = lif(layer_norm(query @ Wk.T + bk, gk, betak), 1.0)
        V = lif(layer_norm(query @ Wv.T + bv, gv, betav), 1.0)
        Q = Q.reshape(B, N, H, Dh).transpose(0, 2, 1, 3)
        K = K.reshape(B, N, H, Dh).transpose(0, 2, 1, 3)
        V = V.reshape(B, N, H, Dh).transpose(0, 2, 1, 3)
        qk = jnp.einsum('bhld,bhmd->bhlm', Q, K)
        q_sum = Q.sum(-1, keepdims=True)
        k_sum = K.sum(-1, keepdims=True)
        hamming = q_sum + jnp.swapaxes(k_sum, 2, 3) - 2.0 * qk
        attn = Dh - hamming + log_pe_bias(N, N)[None, None]
        out = jnp.einsum('bhlm,bhmd->bhld', attn * scale, V)
        out = lif(out, 0.5)
        out = out.transpose(0, 2, 1, 3).reshape(B, N, D)
        out = lif(layer_norm(out @ Wo.T + bo, go, betao), 1.0)
        return out

    def _L0_ffn_ref(x, scale, centroids, up_w, down_w):
        import jax, jax.numpy as jnp
        import numpy as np
        EPS = 1e-06
        N_EXPERTS = 8

        def _rms_norm(x, scale, eps=EPS):
            mean_sq = jnp.mean(x.astype(jnp.float32) ** 2, axis=-1, keepdims=True)
            s = scale.astype(jnp.float32) * jax.lax.rsqrt(mean_sq + eps)
            return x * s.astype(x.dtype)

        def _dist2(x, y):
            nx = jnp.sum(x ** 2, axis=-1)[..., :, None]
            ny = jnp.sum(y ** 2, axis=-1)[..., None, :]
            return nx + ny - 2.0 * (x @ y.T)
        skip = x
        xn = _rms_norm(x, scale)
        ids = jnp.argmin(_dist2(xn, centroids), axis=-1)
        out = jnp.zeros_like(x)
        for e in range(N_EXPERTS):
            h = jnp.einsum('bsd,dh->bsh', xn, up_w[e])
            a, g = jnp.split(h, 2, axis=-1)
            y = jnp.einsum('bsh,hd->bsd', a * jax.nn.silu(g), down_w[e])
            out = jnp.where((ids == e)[..., None], y, out)
        return out + skip
    x = L0_attn_query
    xn = _layernorm(x, axis=-1)
    s = _L0_attn_ref(xn, L0_attn_Wq, L0_attn_bq, L0_attn_Wk, L0_attn_bk, L0_attn_Wv, L0_attn_bv, L0_attn_Wo, L0_attn_bo, L0_attn_gq, L0_attn_betaq, L0_attn_gk, L0_attn_betak, L0_attn_gv, L0_attn_betav, L0_attn_go, L0_attn_betao, L0_attn_scale)
    g = _silu(_L0_ffn_ref(xn, L0_ffn_scale, L0_ffn_centroids, L0_ffn_up_w, L0_ffn_down_w))
    x = x + s * g
    return x

_drawn_inputs = setup_inputs


def setup_inputs(seed=0):
    import zlib

    import numpy as np

    out = dict(_drawn_inputs(seed))
    spreads = {'L0_attn_bq': (0.0, 0.1),
     'L0_attn_bk': (0.0, 0.1),
     'L0_attn_bv': (0.0, 0.1),
     'L0_attn_bo': (0.0, 0.1),
     'L0_attn_gq': (1.0, 0.2),
     'L0_attn_betaq': (0.0, 0.1),
     'L0_attn_gk': (1.0, 0.2),
     'L0_attn_betak': (0.0, 0.1),
     'L0_attn_gv': (1.0, 0.2),
     'L0_attn_betav': (0.0, 0.1),
     'L0_attn_go': (1.0, 0.2),
     'L0_attn_betao': (0.0, 0.1),
     'L0_ffn_scale': (1.0, 0.2)}
    factors = {}
    for name, (base, spread) in spreads.items():
        noise = np.random.default_rng([zlib.crc32(name.encode()), seed]).standard_normal(out[name].shape)
        drawn = base * np.exp(spread * noise) if base else spread * noise
        out[name] = jnp.asarray(drawn.astype(out[name].dtype))
    for name, factor in factors.items():
        out[name] = (out[name] * factor).astype(out[name].dtype)
    return out
```

```python
from contextlib import ExitStack

import concourse.bass as bass
from concourse import mybir

ALU = mybir.AluOpType
ACT = mybir.ActivationFunctionType
AX = mybir.AxisListType
F32 = mybir.dt.float32
F32R = mybir.dt.float32r
BF16 = mybir.dt.bfloat16
I32 = mybir.dt.int32
U16 = mybir.dt.uint16

P = 128
N = 4096
D = 256
DC = D // P
NT = N // P
E = 8
HID = 512
HC = HID // P
ST = NT + E - 1
PAD = 16
CH = 4
CT = CH * P
NCH = NT // CH
YW = 3 * D + E
ROWA = 2 * D + 1
LN_EPS = 1e-5
RMS_EPS = 1e-6

G_, B_, BETA_, FS_, SCALE_ = 0, 8, 16, 24, 26
NV = 27

C_NEAR, C_TRI, C_PICK, C_SCAN, C_HEAD, C_SUM, C_END = 0, 384, 640, 896, 1024, 1152, 1280


def build(nc, x, wq, wk, wv, wo, vectors, centroids, up_w, down_w, consts, blocks, eye, out):
    with ExitStack() as ctx:
        sem = lambda name: ctx.enter_context(nc.semaphore(name))
        block_arena = [(nc.sbuf_base + 63) // 64 * 64]

        def place(name, shape, dt, at=None):
            size = 4 if dt in (F32, F32R, I32) else 2
            for n in shape[1:]:
                size *= n
            size = (size + 31) // 32 * 32
            if at is None:
                at = block_arena[0]
                block_arena[0] += size
            return nc.alloc_sbuf_tensor_at(name, shape, dt, offset=at), at

        up_sb, at_up = place("up_sb", [P, E, DC, 2 * HID], F32)
        down_sb, at_down = place("down_sb", [P, E, HC, D], F32)
        xs, _ = place("xs", [P, NT, D], F32, at=at_up)
        q_sp, _ = place("q_sp", [P, NT, D], BF16, at=at_up + 4 * NT * D)
        k_sp, _ = place("k_sp", [P, NT, D], BF16, at=at_up + 6 * NT * D)
        w_raw, _ = place("w_raw", [P, 4, DC, D], F32, at=at_down)
        diag, _ = place("diag", [P, 8, P], F32, at=at_down + 8192)
        w_cen, _ = place("w_cen", [P, DC, YW + D], F32, at=at_down + 12288)
        diag16, _ = place("diag16", [P, 3, 8, P], BF16, at=at_down + 20736)
        sgn_row, _ = place("sgn_row", [P, 4, D], F32, at=at_down + 26880)

        v_sp, at_v = place("v_sp", [P, PAD + NT + PAD, D], BF16)
        q_t, at_q = place("q_t", [P, DC, N], BF16)
        blk_tab, _ = place("blk_tab", [P, N], BF16)
        w_hi, at_w = place("w_hi", [P, DC, YW], F32R)
        w_lo, at_w2 = place("w_lo", [P, DC, YW], F32R)
        a_sp = [place(f"a_sp{k}", [P, DC, CT], F32R, at=at_w + 4096 * k)[0] for k in range(2)]
        s_out = [place(f"s_out{k}", [P, CH, D], BF16, at=at_w + 8192 + 2048 * k)[0] for k in range(2)]
        assert at_w2 + 4 * DC * YW - at_w >= 12288
        wo_hi, _ = place("wo_hi", [P, DC, D], F32R)
        wo_lo, _ = place("wo_lo", [P, DC, D], F32R)
        thr, _ = place("thr", [P, 4 * D], F32)
        fs_row, _ = place("fs_row", [P, D], F32)
        b_row, _ = place("b_row", [P, 4 * D], BF16)
        b_pick, _ = place("b_pick", [P, P], BF16)
        xn, at_xn = zip(*[place(f"xn{k}", [P, D + 2], F32) for k in range(4)])
        x_hi, at_xh = zip(*[place(f"x_hi{k}", [P, DC, P], F32R) for k in range(2)])
        x_lo, at_xl = zip(*[place(f"x_lo{k}", [P, DC, P], F32R) for k in range(2)])
        junk = [place(f"junk{k}", [P, D], BF16)[0] for k in range(4)]
        sq, at_sq = zip(*[place(f"sq{k}", [P, D], F32) for k in range(2)])

        cst, _ = place("cst", [P, C_END], BF16)
        ident, _ = place("ident", [P, P], F32)
        ident16, _ = place("ident16", [P, P], BF16)
        ones16, _ = place("ones16", [P, P], BF16)
        mean_w, _ = place("mean_w", [P, P], F32)
        ones32, _ = place("ones32", [P, P], F32)
        zeros16, _ = place("zeros16", [P, CT], BF16, at=at_q)
        vec_raw, _ = place("vec_raw", [NV, P], F32, at=at_q + 1024)
        vc, _ = place("vc", [P, NV], F32)
        cen_raw, _ = place("cen_raw", [E, D], F32, at=at_q + 2048)
        small, _ = place("small", [P, 128], F32)
        b16, _ = place("b16", [P, 24], BF16)
        eps4, _ = place("eps4", [P, 4, 4], F32)
        half_neg, _ = place("half_neg", [P, 4], F32)
        st6, _ = place("st6", [P, 2, 6], F32)
        mv2, _ = place("mv2", [P, 2, 2], F32)
        mv, _ = place("mv", [P, NT, 2], F32)
        pw, _ = place("pw", [P, 6, 4], F32)
        pv, _ = place("pv", [P, 4], F32)
        rstd, _ = place("rstd", [P, NT], F32)
        nmr, _ = place("nmr", [P, NT], F32)
        rms, _ = place("rms", [P, NT], F32)
        ss, _ = place("ss", [P, NT, 4], F32)
        rs, _ = place("rs", [P, NT, 4], F32)
        nx, _ = place("nx", [P, NT], F32)
        ny, _ = place("ny", [P, E], F32)
        dots, _ = place("dots", [P, NT, E], F32)
        ra, _ = place("ra", [P, NT, E], F32, at=at_xh[0])
        rb, _ = place("rb", [P, NT, E], F32, at=at_xh[1])
        hot, _ = place("hot", [P, NT, E], F32, at=at_xl[0])
        hot16, _ = place("hot16", [P, NT, E], BF16)
        eidx, _ = place("eidx", [P, E], F32)
        lev, _ = place("lev", [P, NT], F32)
        rt, _ = place("rt", [P, 4, NT], F32)
        r8, _ = place("r8", [P, 6, E], F32)
        pos, _ = place("pos", [P, NT], I32)
        ids, _ = place("ids", [P, NT], I32)
        tile_no, _ = place("tile_no", [P, ST], F32)
        tcmp, _ = place("tcmp", [1, ST, E], F32)
        tex, _ = place("tex", [1, ST], F32)
        expert, _ = place("expert", [1, ST], I32)
        none, _ = place("none", [ST, P], I32)
        slot_id, _ = place("slot_id", [P, ST], I32)
        from_id = [place(f"from_id{k}", [P, 1], I32)[0] for k in range(4)]
        to_id = [place(f"to_id{k}", [P, 1], I32)[0] for k in range(4)]
        from_n, to_n = sem("from_n"), sem("to_n")
        pool_passed, dve_passed = sem("pool_passed"), sem("dve_passed")
        sc16, _ = place("sc16", [P, D], BF16)
        sv_row, _ = place("sv_row", [P, D], F32, at=at_sq[0])
        m_f, _ = place("m_f", [P, D], F32, at=at_xl[1])
        m_hi, _ = place("m_hi", [P, D], BF16, at=at_sq[1])
        m_lo, _ = place("m_lo", [P, D], BF16, at=at_sq[1] + 2 * D)
        neg16, _ = place("neg16", [P, 2], BF16)
        thr2, _ = place("thr2", [P, 2], F32)

        row_a = [place(f"row_a{k}", [P, ROWA], F32, at=at_xn[2 * k] if k < 2 else None)[0] for k in range(4)]
        row_s = [place(f"row_s{k}", [P, D], BF16)[0] for k in range(4)]
        e_xt = [place(f"e_xt{k}", [P, DC, P], F32, at=at_v + 1024 * k)[0] for k in range(2)]
        e_ht = [place(f"e_ht{k}", [P, HC, P], F32, at=at_v + 2048 + 2048 * k)[0] for k in range(2)]
        e_gate = [place(f"e_gate{k}", [P, HID], F32, at=at_v + 6144 + 2048 * k)[0] for k in range(2)]
        e_act = [place(f"e_act{k}", [P, HID], F32, at=at_v + 10240 + 2048 * k)[0] for k in range(2)]
        e_z = [place(f"e_z{k}", [P, D], F32, at=at_v + 14336 + 1024 * k)[0] for k in range(2)]
        e_g = [place(f"e_g{k}", [P, D], F32, at=at_v + 16384 + 1024 * k)[0] for k in range(2)]
        e_o = [place(f"e_o{k}", [P, D], F32, at=at_v + 18432 + 1024 * k)[0] for k in range(4)]
        assert block_arena[0] <= nc.sbuf_usable_end, (block_arena[0], nc.sbuf_usable_end)

        bank = [ctx.enter_context(nc.psum_tensor(f"bank{k}", [P, 512], F32)) for k in range(8)]
        rows_a = nc.dram_tensor("rows_a", (N, ROWA), F32, kind="Internal").ap()
        rows_s = nc.dram_tensor("rows_s", (N, D), BF16, kind="Internal").ap()
        slots = nc.dram_tensor("slots", (ST * P, 1), I32, kind="Internal").ap()

        near = cst[:, C_NEAR:C_TRI]
        tri = cst[:, C_TRI:C_PICK].rearrange("p (a b) -> p a b", a=2)
        pick = cst[:, C_PICK:C_SCAN]
        scan_tri = cst[:, C_SCAN:C_HEAD]
        head = cst[:, C_HEAD:C_SUM]
        sum_rows = cst[:, C_SUM:C_END]

        ld_w, ld_c, ld_b, x_loaded = sem("ld_w"), sem("ld_c"), sem("ld_b"), sem("x_loaded")
        x_copied, up_loaded, down_loaded = sem("x_copied"), sem("up_loaded"), sem("down_loaded")
        consts_set = sem("consts_set")
        vec_turned, w_turned, vec_kept, bias_mean = sem("vec_turned"), sem("w_turned"), sem("vec_kept"), sem("bias_mean")
        diag_made, rows_made, w_centred, w_high = sem("diag_made"), sem("rows_made"), sem("w_centred"), sem("w_high")
        setup_done, none_made, tables_made = sem("setup_done"), sem("none_made"), sem("tables_made")
        dve_n, pool_n = sem("dve_n"), sem("pool_n")
        group_n, aggr_done, norm_n, sq_done, out_n, fs_made, neg_made, rows_clear = sem("group_n"), sem("aggr_done"), sem("norm_n"), sem("sq_done"), sem("out_n"), sem("fs_made"), sem("neg_made"), sem("rows_clear")
        stats_done, rstd_done, xn_done, rms_put = sem("stats_done"), sem("rstd_done"), sem("xn_done"), sem("rms_put")
        xt_done, hi_done, lo_done = sem("xt_done"), sem("hi_done"), sem("lo_done")
        row_put = [sem(f"row_put{k}") for k in range(4)]
        qk_done, v_done, squared, qk_rs, v_rs = (sem("qk_done"), sem("v_done"), sem("squared"),
                                                     sem("qk_rs"), sem("v_rs"))
        spiked, dots_done, nx_done, st_n = sem("spiked"), sem("dots_done"), sem("nx_done"), sem("st_n")
        sums_done, qt_done, qt_kept = sem("sums_done"), sem("qt_done"), sem("qt_kept")
        hot_done, ranks_done, pos_done, none_put, id_put, ids_back = (
            sem("hot_done"), sem("ranks_done"), sem("pos_done"), sem("none_put"), sem("id_put"), sem("ids_back"))
        m_done, cvec_done, sv_done = sem("m_done"), sem("cvec_done"), sem("sv_done")
        at_done, at_spiked, wo_done, wo_sq, wo_rs, s_made = (sem("at_done"), sem("at_spiked"), sem("wo_done"),
                                                            sem("wo_sq"), sem("wo_rs"), sem("s_made"))
        s_put = [sem(f"s_put{k}") for k in range(2)]
        got = [sem(f"got{k}") for k in range(4)]
        sent = [sem(f"sent{k}") for k in range(4)]
        ext_done, ext_kept, up_done, gate_done, act_done = (sem("ext_done"), sem("ext_kept"), sem("up_done"),
                                                          sem("gate_done"), sem("act_done"))
        eht_done, eht_kept, down_done, z_done, g_done, sg_done, o_done = (
            sem("eht_done"), sem("eht_kept"), sem("down_done"), sem("z_done"), sem("g_done"), sem("sg_done"), sem("o_done"))

        def after(eng, s, count):
            if not isinstance(count, int) or count > 0:
                eng.wait_ge(s, count)

        def tile_of(buffer, t):
            return buffer[:, bass.ds(t, 1), :].rearrange("p a n -> p (a n)")

        def chain(eng, s):
            count = [0]

            def step(ins):
                count[0] += 1
                ins.then_inc(s, 1)
                eng.wait_ge(s, count[0])
            return step

        block = ctx.enter_context(nc.Block())

        @block.sync
        def _(sp):
            for p, w in enumerate((wq, wk, wv, wo)):
                sp.dma_start(w_raw[:, p, :, :], w.rearrange("(c p) n -> p c n", p=P)).then_inc(ld_w, 16)
            for g in range(NT // 4):
                if g:
                    sp.wait_ge(x_loaded, 16 * g)
                sp.dma_start(xs[:, 4 * g:4 * g + 4, :],
                             x[512 * g:512 * g + 512, :].rearrange("(t p) n -> p t n", p=P)).then_inc(x_loaded, 16)
            sp.dma_start(blk_tab[:, :].bitcast(U16), blocks).then_inc(ld_b, 16)
            sp.dma_start(rows_a[:, D + 1:2 * D + 1], x).then_inc(x_copied, 16)
            sp.wait_ge(none_made, 1)
            sp.dma_start(slots.rearrange("(s p) a -> s (p a)", p=P), none[:, :]).then_inc(none_put, 16)
            sp.wait_ge(setup_done, 1)
            for e in range(0, E, 2):
                sp.dma_start(down_sb[:, e:e + 2, :, :],
                             down_w[e:e + 2].rearrange("e (c p) n -> p e c n", p=P)).then_inc(down_loaded, 16)
            sp.wait_ge(xn_done, NT)
            sp.wait_ge(stats_done, NT)
            sp.wait_ge(sums_done, NT)
            sp.wait_ge(qt_done, NT)
            for e in range(E):
                sp.dma_start(up_sb[:, e, :, :], up_w[e].rearrange("(c p) n -> p c n", p=P)).then_inc(up_loaded, 16)
            sp.wait_ge(id_put, 16 * NT)
            sp.dma_start(slot_id[:, :], slots.rearrange("(s p) a -> p (s a)", p=P),
                         allow_slow_non_contiguous=True).then_inc(ids_back, 16)

        @block.tensor
        def _(pe):
            pe.wait_ge(consts_set, 5)
            pe.wait_ge(ld_c, 16 * 4)
            pe.transpose(bank[4][0:P, 0:NV], vec_raw[:, :], ident[0:NV, 0:NV])
            for c in range(DC):
                last = pe.transpose(bank[4][:, 64 + E * c:64 + E * c + E], cen_raw[:, c * P:(c + 1) * P],
                                    ident[0:E, 0:E])
            last.then_inc(vec_turned, 1)
            pe.wait_ge(ld_w, 64)
            for p in range(4):
                for ic in range(DC):
                    for oc in range(DC):
                        last = pe.transpose(bank[p][:, ic * D + oc * P:ic * D + (oc + 1) * P],
                                            w_raw[:, p, oc, ic * P:(ic + 1) * P], ident[:, :])
                last.then_inc(w_turned, 1)
            pe.wait_ge(vec_kept, 1)
            pe.matmul(bank[5][:, 0:8], mean_w[:, :], vc[:, B_:B_ + 8], start=True, stop=True).then_inc(bias_mean, 1)
            for mark, where in ((1, 6), (2, 4)):
                pe.wait_ge(diag_made, mark)
                for h in range(2):
                    last = pe.matmul(bank[where + h][:, :], ones32[:, :], diag[:, 4 * h:4 * h + 4, :],
                                     start=True, stop=True)
                last.then_inc(rows_made, 1)
            pe.wait_ge(diag_made, 3)
            pe.matmul(bank[7][:, 0:D], ones32[:, :], diag[:, 0:2, :], start=True, stop=True)
            for c in range(DC):
                last = pe.matmul(bank[7][:, D:D + E], ones32[:, :], small[:, 64 + E * c:64 + E * c + E],
                                 start=(c == 0), stop=(c == DC - 1))
            last.then_inc(rows_made, 1)
            pe.wait_ge(diag_made, 4)
            for h in range(2):
                for part in range(3):
                    last = pe.matmul(bank[4 + h][32 * part:32 * part + 32, :], ones16[:, 0:32],
                                     diag16[:, part, 4 * h:4 * h + 4, :], start=True, stop=True)
            last.then_inc(rows_made, 1)
            pe.matmul(bank[6][:, :], zeros16[:, 0:P], zeros16[:, :], start=True, stop=True)

            def transpose_x(k, i):
                t, s = k + 4 * i, k % 2
                pe.wait_ge(xn_done, t + 1)
                for c in range(DC):
                    last = pe.transpose(bank[s][:, c * P:(c + 1) * P], xn[k % 4][:, c * P:(c + 1) * P], ident[:, :])
                last.then_inc(xt_done, 1)

            def project(k, i):
                t, s = k + 4 * i, k % 2
                pe.wait_ge(lo_done, t + 1)
                after(pe, spiked, 3 * (t - 1))
                after(pe, dots_done, t - 1)
                for b, c0, c1, done in ((2 + s, 0, 2 * D, qk_done), (4 + s, 2 * D, YW, v_done)):
                    first = True
                    for left, right in ((x_hi, w_hi), (x_hi, w_lo), (x_lo, w_hi)):
                        for c in range(DC):
                            pe.matmul(bank[b][:, 0:c1 - c0], left[s][:, c, :], right[:, c, c0:c1],
                                      start=first, stop=False)
                            first = False
                    cb = min(c1, 3 * D)
                    pe.matmul(bank[b][:, 0:cb - c0], b_pick[0:96, :], b_row[0:96, c0:cb],
                              start=False, stop=True).then_inc(done, 1)

            def accumulate(k, i):
                t = k + 4 * i
                pe.wait_ge(spiked, 3 * (t + 1))
                after(pe, qt_kept, t)
                for c in range(DC):
                    last = pe.transpose(bank[7][:, 64 * c:64 * c + 64].bitcast(BF16),
                                        tile_of(q_sp, t)[:, c * P:(c + 1) * P], ident16[:, :])
                last.then_inc(qt_done, 1)
                for c in range(DC):
                    pe.matmul(bank[6][:, c * P:(c + 1) * P], tile_of(k_sp, t)[:, c * P:(c + 1) * P],
                              tile_of(v_sp, t + PAD)[:, c * P:(c + 1) * P], start=False, stop=False,
                              skip_group_check=True)
                pe.matmul(bank[6][:, D:2 * D], pick[:, bass.ds(4 * t, P)], tile_of(v_sp, t + PAD),
                          start=False, stop=False, skip_group_check=True).then_inc(sums_done, 1)

            def step_a(k, i):
                if k < NT:
                    transpose_x(k, i)
                if 0 <= k - 1 < NT:
                    project(k - 1, i)
                if 0 <= k - 3 < NT:
                    accumulate(k - 3, i)

            for k in range(4):
                step_a(k, 0)
            with pe.Fori(0, NT // 4 - 1) as i:
                for k in range(4, 8):
                    step_a(k, i)
            for k in range(NT, NT + 3):
                step_a(k, 0)

            pe.wait_ge(m_done, 1)
            pe.wait_ge(qt_kept, NT)
            pe.matmul(bank[7][:, 0:D], sum_rows, sc16[:, :], start=True, stop=True).then_inc(sv_done, 1)
            pe.wait_ge(m_done, 2)
            pe.wait_ge(neg_made, 1)
            for c in range(DC):
                cs = slice(c * P, (c + 1) * P)
                pe.matmul(bank[7][:, c:c + 1], m_hi[:, cs], ones16[:, 0:1], start=True, stop=False)
                pe.matmul(bank[7][:, c:c + 1], m_lo[:, cs], ones16[:, 0:1], start=False, stop=False)
                last = pe.matmul(bank[7][:, c:c + 1], sc16[:, cs], neg16[:, 0:1], start=False, stop=True)
            last.then_inc(cvec_done, 1)

            def attend(k, i):
                c = k + 2 * i
                pe.wait_ge(blk_ready, 16)
                for h in range(DC):
                    hs = slice(h * P, (h + 1) * P)
                    ps = bank[h]
                    after(pe, at_spiked, DC * (c - 1) + h + 1)
                    pe.matmul(ps[:, :], sc16[:, hs], blk_tab[:, bass.ds(c * CT, CT)], start=True, stop=False)
                    for part in (m_hi, m_lo):
                        pe.matmul(ps[:, :], part[:, hs], q_t[:, h, bass.ds(c * CT, CT)], start=False, stop=False)
                    for j in range(-1, CH + 1):
                        a, b = max(0, j - 1), min(CH, j + 2)
                        pe.matmul(ps[:, a * P:b * P], tile_of(v_sp, CH * c + (PAD + j))[:, hs],
                                  near[:, (a - j + 1) * P:(b - j + 1) * P], start=False, stop=False)
                    for b in range(CH):
                        for n, d in enumerate((2, 4, 8, 16)):
                            for side in range(2):
                                at = PAD + b + (d if side else -d)
                                last = pe.matmul(ps[:, b * P:(b + 1) * P], tile_of(v_sp, CH * c + at)[:, hs],
                                                 tri[:, side, :], start=False,
                                                 stop=(b == CH - 1 and n == 3 and side == 1))
                    last.then_inc(at_done, 1)

            def project_out(k, i):
                c, s = k + 2 * i, k % 2
                pe.wait_ge(at_spiked, DC * (c + 1))
                for pair in range(2):
                    ps = bank[2 + 2 * s + pair]
                    after(pe, s_made, CH * (c - 2) + 2 * pair + 2)
                    for n in range(2):
                        tl = 2 * pair + n
                        o = ps[:, n * D:(n + 1) * D]
                        for m, w in enumerate((wo_hi, wo_lo)):
                            for h in range(DC):
                                pe.matmul(o, a_sp[s][:, h, tl * P:(tl + 1) * P], w[:, h, :],
                                          start=(m == 0 and h == 0), stop=False)
                        last = pe.matmul(o, b_pick[0:96, :], b_row[0:96, 3 * D:4 * D], start=False, stop=True)
                    last.then_inc(wo_done, 1)

            blk_ready = ld_b
            attend(0, 0)
            pe.wait_ge(hot_done, 1)
            pe.matmul(bank[6][:, 0:NT * E], scan_tri, hot16[:, :, :], start=True, stop=True)
            pe.matmul(bank[6][:, NT * E:2 * NT * E], ones16[:, :], hot16[:, :, :], start=True, stop=True) \
                .then_inc(ranks_done, 1)
            for k in range(1, 4):
                attend(k, 0)
                project_out(k - 1, 0)
            with pe.Fori(0, NCH // 2 - 2) as i:
                for k in range(4, 6):
                    attend(k, i)
                    project_out(k - 1, i)
            project_out(NCH - 1, 0)

            def turn_rows(k, i):
                s = k + 4 * i
                pe.wait_ge(got[k % 4], 32 * (k // 4 + i + 1))
                after(pe, ext_kept, s)
                for c in range(DC):
                    last = pe.transpose(bank[4][:, c * P:(c + 1) * P], row_a[k % 4][:, c * P:(c + 1) * P], ident[:, :])
                last.then_inc(ext_done, 1)

            def turn_hidden(k, i):
                s = k + 4 * i
                pe.wait_ge(act_done, s + 1)
                after(pe, eht_kept, s)
                for c in range(HC):
                    last = pe.transpose(bank[5][:, c * P:(c + 1) * P], e_act[k % 2][:, c * P:(c + 1) * P], ident[:, :])
                last.then_inc(eht_done, 1)

            def expert_up(k, i):
                s = k + 4 * i
                e = pe.value_load(expert[0:1, bass.ds(s, 1)], min_val=0, max_val=E - 1)
                pe.wait_ge(ext_kept, s + 1)
                after(pe, act_done, s)
                w = up_sb[:, bass.ds(e, 1), :, :].rearrange("p a c n -> p (a c) n")
                for half in (1, 0):
                    for c in range(DC):
                        last = pe.matmul(bank[2 + half][:, :], e_xt[k % 2][:, c, :],
                                         w[:, c, half * HID:(half + 1) * HID], start=(c == 0), stop=(c == DC - 1))
                    last.then_inc(up_done, 1)

            def expert_down(k, i):
                s = k + 4 * i
                e = pe.value_load(expert[0:1, bass.ds(s, 1)], min_val=0, max_val=E - 1)
                pe.wait_ge(eht_kept, s + 1)
                after(pe, z_done, s - 1)
                w = down_sb[:, bass.ds(e, 1), :, :].rearrange("p a c n -> p (a c) n")
                for c in range(HC):
                    last = pe.matmul(bank[k % 2][:, 0:D], e_ht[k % 2][:, c, :], w[:, c, :],
                                     start=(c == 0), stop=(c == HC - 1))
                last.then_inc(down_done, 1)

            def step_c(k, i):
                if k < ST:
                    turn_rows(k, i)
                if 0 <= k - 2 < ST:
                    expert_down(k - 2, i)
                if 0 <= k - 1 < ST:
                    turn_hidden(k - 1, i)
                if k < ST:
                    expert_up(k, i)

            pe.wait_ge(pos_done, 2)
            pe.wait_ge(s_made, NT)
            pe.wait_ge(up_loaded, 16 * E)
            pe.wait_ge(down_loaded, 16 * E // 2)
            for k in range(4):
                step_c(k, 0)
            with pe.Fori(0, (ST - 4) // 4) as i:
                for k in range(4, 8):
                    step_c(k, i)
            for k in range(ST // 4 * 4, ST + 2):
                step_c(k, 0)

        @block.scalar
        def _(act):
            act.dma_start(cst[:, :].bitcast(U16), consts).then_inc(ld_c, 16)
            act.dma_start(ident[:, :], eye).then_inc(ld_c, 16)
            act.dma_start(vec_raw[:, :], vectors).then_inc(ld_c, 16)
            act.dma_start(cen_raw[:, :], centroids).then_inc(ld_c, 16)
            act.wait_ge(w_centred, 1)
            act.activation(w_hi[:, :, :], w_cen[:, :, 0:YW], ACT.Copy).then_inc(w_high, 1)
            act.activation(wo_hi[:, :, :], w_cen[:, :, YW:YW + D], ACT.Copy).then_inc(w_high, 1)

            def normalize(k, i):
                t = k + 4 * i
                act.wait_ge(rstd_done, k // 4 + i + 1)
                act.wait_ge(x_loaded, 16 * (k // 4 + i + 1))
                if k >= 4:
                    act.wait_ge(xt_done, t - 3)
                    act.wait_ge(nx_done, t - 3)
                    act.wait_ge(row_put[k % 4], 16 * (k // 4 + i))
                act.activation(xn[k % 4][:, 0:D], tile_of(xs, t), ACT.Identity, bias=nmr[:, bass.ds(t, 1)],
                               scale=rstd[:, bass.ds(t, 1)]).then_inc(xn_done, 1)

            def step_a(k, i):
                t, s = k + 4 * i, k % 2
                if k < NT:
                    act.wait_ge(xt_done, t + 1)
                    act.activation(x_hi[s][:, :, :], bank[s][:, 0:D].rearrange("p (c n) -> p c n", c=DC),
                                   ACT.Copy).then_inc(hi_done, 1)
                if k + 1 < NT:
                    normalize(k + 1, i)
                if k >= 1:
                    u, su = t - 1, (k - 1) % 2
                    act.wait_ge(qk_done, u + 1)
                    for n in range(3):
                        if n == 2:
                            act.wait_ge(v_done, u + 1)
                        after(act, squared, 3 * (u - 1) + n + 1)
                        src = bank[2 + su][:, n * D:(n + 1) * D] if n < 2 else bank[4 + su][:, 0:D]
                        act.activation(junk[n][:, :], src, ACT.Square,
                                       accum_out=tile_of(ss, u)[:, n:n + 1]).then_inc(squared, 1)
                    act.wait_ge(sq_done, u + 1)
                    after(act, nx_done, u)
                    act.activation(junk[3][:, :], sq[su][:, :], ACT.Square,
                                   accum_out=nx[:, bass.ds(u, 1)]).then_inc(nx_done, 1)
                    act.wait_ge(rms_put, u + 1)
                    act.dma_start(rows_a[bass.ds(u * P, P), 0:D + 1],
                                  xn[(k - 1) % 4][:, 0:D + 1]).then_inc(row_put[(k - 1) % 4], 16)

            normalize(0, 0)
            for k in range(4):
                step_a(k, 0)
            with act.Fori(0, NT // 4 - 2) as i:
                for k in range(4, 8):
                    step_a(k, i)
            for k in range(NT - 4, NT + 1):
                step_a(k, 0)

            def squares_out(k, i):
                c, s = k + 2 * i, k % 2
                for pair in range(2):
                    act.wait_ge(wo_done, 2 * c + pair + 1)
                    for n in range(2):
                        m = 2 * pair + n
                        after(act, wo_sq, CH * (c - 1) + m + 1)
                        act.activation(junk[m][:, :], bank[2 + 2 * s + pair][:, n * D:(n + 1) * D], ACT.Square,
                                       accum_out=ss_out(c, m)).then_inc(wo_sq, 1)

            def put_s(k, i):
                c, s = k + 2 * i, k % 2
                act.wait_ge(s_made, CH * (c + 1))
                act.dma_start(rows_s[bass.ds(c * CT, CT), :].rearrange("(t p) n -> p t n", p=P),
                              s_out[s][:, :, :]).then_inc(s_put[s], 16)

            def ss_out(c, n):
                return ss[:, bass.ds(c * CH + n, 1), 3:4].rearrange("p a b -> p (a b)")

            squares_out(0, 0)
            for k in range(1, 3):
                squares_out(k, 0)
                put_s(k - 1, 0)
            with act.Fori(0, NCH // 2 - 2) as i:
                for k in range(3, 5):
                    squares_out(k, i)
                    put_s(k - 1, i)
            squares_out(NCH - 1, 0)
            put_s(NCH - 2, 0)
            put_s(NCH - 1, 0)

            def step_c(k, i):
                s, b = k + 4 * i, k % 2
                if k < ST:
                    act.wait_ge(ext_done, s + 1)
                    after(act, up_done, 2 * (s - 1))
                    for c in range(DC):
                        last = act.activation(e_xt[b][:, c, :], bank[4][:, c * P:(c + 1) * P], ACT.Copy,
                                              scale=vc[:, FS_ + c:FS_ + c + 1])
                    last.then_inc(ext_kept, 1)
                if k >= 2:
                    act.wait_ge(z_done, s - 1)
                    after(act, sg_done, s - 3)
                    act.activation(e_g[b][:, :], e_z[b][:, :], ACT.Silu).then_inc(g_done, 1)
                if k < ST:
                    act.wait_ge(up_done, 2 * s + 1)
                    after(act, act_done, s - 1)
                    act.activation(e_gate[b][:, :], bank[3][:, :], ACT.Silu,
                                   scale=row_a[k % 4][:, D:D + 1]).then_inc(gate_done, 1)

            for k in range(4):
                step_c(k, 0)
            with act.Fori(0, (ST - 4) // 4) as i:
                for k in range(4, 8):
                    step_c(k, i)
            for k in range(ST // 4 * 4, ST + 2):
                step_c(k, 0)

        @block.vector
        def _(dve):
            V = nc.vector
            step = chain(dve, dve_n)
            for m, val in ((ones32, 1.0), (ones16, 1.0), (mean_w, 1.0 / D), (zeros16, 0.0)):
                V.memset(m[:, :], val).then_inc(consts_set, 1)
            step(V.memset(b_pick[:, :], 0.0))
            for part in range(3):
                last = V.memset(b_pick[32 * part:32 * part + 1, :], 1.0)
            last.then_inc(consts_set, 1)

            def stats(k, i):
                t = k + 4 * i
                dve.wait_ge(x_loaded, 16 * (k // 4 + i + 1))
                V.bn_stats(st6[:, k % 2, :], tile_of(xs, t)).then_inc(st_n, 1)
                dve.wait_ge(st_n, t + 1)
                dve.sem_inc(dve_passed, 1)
                V.bn_aggr(mv2[:, k % 2, :], st6[:, k % 2, :]).then_inc(aggr_done, 1)
                dve.wait_ge(aggr_done, t + 1)
                V.tensor_copy(tile_of(mv, t), mv2[:, k % 2, :]).then_inc(stats_done, 1)

            dve.wait_ge(vec_turned, 1)
            step(V.tensor_copy(small[:, 48:64], bank[4][:, 64:80]))
            V.tensor_copy(vc[:, :], bank[4][:, 0:NV]).then_inc(vec_kept, 1)
            dve.wait_ge(vec_kept, 1)
            for c in range(DC):
                V.tensor_scalar(w_cen[:, c, 3 * D:YW], small[:, 48 + E * c:56 + E * c],
                                vc[:, FS_ + c:FS_ + c + 1], None, ALU.mult)
            step(V.tensor_tensor(small[:, 64:80], small[:, 48:64], small[:, 48:64], ALU.mult))
            gain, beta = vc[:, G_:G_ + 8], vc[:, BETA_:BETA_ + 8]
            sgn, mag, inv, lim, dead = (small[:, 8 * n:8 * n + 8] for n in range(5))
            spread = lambda col: col.unsqueeze(2).broadcast_to([P, col.shape[1], P])
            eye8 = lambda m, n: m[:, :].unsqueeze(1).broadcast_to([P, n, P])
            step(V.tensor_scalar(sgn, gain, 0.0, 2.0, ALU.is_ge, ALU.mult))
            step(V.tensor_scalar(sgn, sgn, -1.0, None, ALU.add))
            V.tensor_tensor(diag[:, :, :], eye8(ident, 8), spread(sgn), ALU.mult).then_inc(diag_made, 1)
            step(V.tensor_tensor(mag, gain, sgn, ALU.mult))
            step(V.tensor_scalar(mag, mag, 1e-30, None, ALU.max))
            step(V.reciprocal(inv, mag))
            step(V.tensor_scalar(lim, beta, -1.0, 1.0, ALU.mult, ALU.add))
            step(V.tensor_tensor(lim, lim, inv, ALU.mult))
            step(V.tensor_scalar(dead, gain, 0.0, 1e20, ALU.is_equal, ALU.mult))
            step(V.tensor_tensor(lim, lim, dead, ALU.subtract))
            step(V.tensor_scalar(lim, lim, 1.0 / 16, None, ALU.mult))
            dve.wait_ge(bias_mean, 1)
            step(V.tensor_copy(small[:, 88:96], bank[5][:, 0:8]))
            dve.wait_ge(rows_made, 1)
            V.tensor_tensor(diag[:, :, :], eye8(ident, 8), spread(lim), ALU.mult).then_inc(diag_made, 1)
            for h in range(2):
                last = V.tensor_copy(sgn_row[:, 2 * h:2 * h + 2, :].rearrange("p a n -> p (a n)"), bank[6 + h][:, :])
            step(last)
            for p in range(4):
                dve.wait_ge(w_turned, p + 1)
                last = V.tensor_reduce(small[:, 96 + 2 * p:98 + 2 * p],
                                       bank[p][:, :].rearrange("p (c n) -> p c n", c=DC), AX.X, ALU.add)
            step(last)
            step(V.tensor_scalar(small[:, 96:104], small[:, 96:104], 1.0 / D, None, ALU.mult))
            for p in range(4):
                at = p * D if p < 3 else YW
                for c in range(DC):
                    last = V.scalar_tensor_tensor(w_cen[:, c, at:at + D], bank[p][:, c * D:(c + 1) * D],
                                                  small[:, 96 + 2 * p + c:97 + 2 * p + c], sgn_row[:, p, :],
                                                  ALU.subtract, ALU.mult)
            last.then_inc(w_centred, 1)
            dve.wait_ge(rows_made, 2)
            for h in range(2):
                V.tensor_copy(thr[:, 512 * h:512 * h + 512], bank[4 + h][:, :])
            V.tensor_tensor(diag[:, 0:2, :], eye8(ident, 2), spread(vc[:, FS_:FS_ + 2]), ALU.mult).then_inc(diag_made, 1)
            bm, bc = small[:, 104:108], small[:, 112:120]
            step(V.tensor_tensor(bm, small[:, 88:96:2], small[:, 89:96:2], ALU.add))
            step(V.tensor_tensor(bc.rearrange("p (a b) -> p a b", b=2),
                                 vc[:, B_:B_ + 8].rearrange("p (a b) -> p a b", b=2),
                                 bm.unsqueeze(2).broadcast_to([P, 4, 2]), ALU.subtract))
            step(V.tensor_tensor(bc, bc, sgn, ALU.mult))
            for part in range(3):
                step(V.tensor_copy(b16[:, 8 * part:8 * part + 8], bc))
                if part < 2:
                    step(V.tensor_tensor(bc, bc, b16[:, 8 * part:8 * part + 8], ALU.subtract))
            step(V.tensor_copy(ident16[:, :], ident[:, :]))
            for part in range(3):
                last = V.tensor_tensor(diag16[:, part, :, :], eye8(ident16, 8), spread(b16[:, 8 * part:8 * part + 8]),
                                       ALU.mult)
            last.then_inc(diag_made, 1)
            dve.wait_ge(rows_made, 3)
            V.tensor_copy(fs_row[:, :], bank[7][:, 0:D]).then_inc(fs_made, 1)
            step(V.tensor_copy(ny[:, :], bank[7][:, D:D + E]))
            dve.wait_ge(w_high, 2)
            V.tensor_tensor(w_lo[:, :, :], w_cen[:, :, 0:YW], w_hi[:, :, :].bitcast(F32), ALU.subtract)
            V.tensor_tensor(wo_lo[:, :, :], w_cen[:, :, YW:YW + D], wo_hi[:, :, :].bitcast(F32), ALU.subtract)
            dve.wait_ge(rows_made, 4)
            for h in range(2):
                last = V.tensor_copy(b_row[0:96, 512 * h:512 * h + 512], bank[4 + h][0:96, :])
            last.then_inc(setup_done, 1)

            V.memset(v_sp[:, 0:PAD, :], 0.0)
            step(V.memset(v_sp[:, PAD + NT:PAD + NT + PAD, :], 0.0))
            for k in range(8):
                stats(k, 0)

            def low_part(k, i):
                t, s = k + 4 * i, k % 2
                dve.wait_ge(hi_done, t + 1)
                V.tensor_tensor(x_lo[s][:, :, :], bank[s][:, 0:D].rearrange("p (c n) -> p c n", c=DC),
                                x_hi[s][:, :, :].bitcast(F32), ALU.subtract).then_inc(lo_done, 1)

            def spikes(k, i):
                t, s = k + 4 * i, k % 2
                dve.wait_ge(qk_rs, t + 1)
                r = tile_of(rs, t)
                V.scalar_tensor_tensor(tile_of(q_sp, t), bank[2 + s][:, 0:D], r[:, 0:1], thr[:, 0:D],
                                       ALU.mult, ALU.is_ge).then_inc(spiked, 1)
                V.scalar_tensor_tensor(tile_of(k_sp, t), bank[2 + s][:, D:2 * D], r[:, 1:2], thr[:, D:2 * D],
                                       ALU.mult, ALU.is_ge).then_inc(spiked, 1)
                dve.wait_ge(v_rs, t + 1)
                V.scalar_tensor_tensor(tile_of(v_sp, t + PAD), bank[4 + s][:, 0:D], r[:, 2:3], thr[:, 2 * D:3 * D],
                                       ALU.mult, ALU.is_ge).then_inc(spiked, 1)
                V.tensor_copy(tile_of(dots, t), bank[4 + s][:, D:D + E]).then_inc(dots_done, 1)

            def keep_qt(k, i):
                t = k + 4 * i
                dve.wait_ge(qt_done, t + 1)
                V.tensor_copy(q_t[:, :, bass.ds(t * P, P)],
                              bank[7][:, 0:P].bitcast(BF16).rearrange("p (c n) -> p c n", c=DC)).then_inc(qt_kept, 1)

            def step_a(k, i, ahead):
                if k < NT:
                    low_part(k, i)
                if 0 <= k - 1 < NT:
                    spikes(k - 1, i)
                if 0 <= k - 3 < NT:
                    keep_qt(k - 3, i)
                if ahead:
                    stats(k + 8, i)

            for k in range(4):
                step_a(k, 0, True)
            with dve.Fori(0, NT // 4 - 3) as i:
                for k in range(4, 8):
                    step_a(k, i, True)
            for k in range(NT - 8, NT + 3):
                step_a(k, 0, False)

            dve.wait_ge(sums_done, NT)
            V.tensor_copy(sc16[:, :], bank[6][:, D:2 * D]).then_inc(m_done, 1)
            dve.wait_ge(sv_done, 1)
            dve.wait_ge(nx_done, NT)
            step(V.tensor_copy(sv_row[:, :], bank[7][:, 0:D]))
            step(V.scalar_tensor_tensor(m_f[:, :], bank[6][:, 0:D], 2.0, sv_row[:, :], ALU.mult, ALU.subtract))
            step(V.tensor_tensor(m_f[:, :].rearrange("p (c n) -> p c n", c=DC),
                                 m_f[:, :].rearrange("p (c n) -> p c n", c=DC),
                                 head.unsqueeze(1).broadcast_to([P, DC, P]), ALU.mult))
            step(V.tensor_copy(m_hi[:, :], m_f[:, :]))
            V.tensor_tensor(m_lo[:, :], m_f[:, :], m_hi[:, :], ALU.subtract).then_inc(m_done, 1)
            scale = vc[:, SCALE_:SCALE_ + 1]
            dve.wait_ge(cvec_done, 1)
            step(V.tensor_scalar(thr2[:, :], bank[7][:, 0:DC], scale, 0.5, ALU.mult, ALU.mult))
            step(V.tensor_scalar(thr2[:, :], thr2[:, :], 0.5, None, ALU.add))

            over_e = lambda m: m.unsqueeze(2).broadcast_to([P, NT, E])
            over_t = lambda m: m.unsqueeze(1).broadcast_to([P, NT, E])
            A, B, HOT = ra[:, :, :], rb[:, :, :], hot[:, :, :]
            dve.wait_ge(nx_done, NT)
            dve.wait_ge(dots_done, NT)
            dve.wait_ge(tables_made, 4)
            step(V.tensor_tensor(A, dots[:, :, :], over_e(rms[:, :]), ALU.mult))
            step(V.tensor_tensor(rt[:, 0, :], nx[:, :], rms[:, :], ALU.mult))
            step(V.tensor_tensor(rt[:, 0, :], rt[:, 0, :], rms[:, :], ALU.mult))
            step(V.scalar_tensor_tensor(A, A, -2.0, over_t(ny[:, :]), ALU.mult, ALU.add))
            step(V.tensor_tensor(A, A, over_e(rt[:, 0, :]), ALU.add))
            step(V.tensor_reduce(rt[:, 1, :], A, AX.X, ALU.min))
            step(V.tensor_tensor(B, A, over_e(rt[:, 1, :]), ALU.is_equal))
            step(V.scalar_tensor_tensor(B, B, -float(E), over_t(eidx[:, :]), ALU.mult, ALU.add))
            step(V.tensor_reduce(rt[:, 1, :], B, AX.X, ALU.min))
            step(V.tensor_scalar(rt[:, 1, :], rt[:, 1, :], float(E), None, ALU.add))
            step(V.tensor_tensor(HOT, over_t(eidx[:, :]), over_e(rt[:, 1, :]), ALU.is_equal))
            V.tensor_copy(hot16[:, :, :], HOT).then_inc(hot_done, 1)
            dve.wait_ge(ranks_done, 1)
            step(V.tensor_copy(A, bank[6][:, NT * E:2 * NT * E].rearrange("p (t e) -> p t e", e=E)))
            for e in range(E):
                last = V.tensor_tensor_scan(rb[:, :, e], ones32[:, 0:NT], ra[:, :, e], 0.0, ALU.mult, ALU.add)
            step(last)
            step(V.tensor_tensor(A, B, A, ALU.subtract))
            step(V.tensor_copy(r8[:, 0, :], rb[:, NT - 1, :]))
            step(V.tensor_tensor(A, bank[6][:, 0:NT * E].rearrange("p (t e) -> p t e", e=E), A, ALU.add))
            by_e = rb[:, :, :].rearrange("p t e -> p (t e)").rearrange("p (e t) -> p e t", e=E)
            step(V.tensor_tensor(by_e, r8[:, 0, :].unsqueeze(2).broadcast_to([P, E, NT]),
                                 lev[:, :].unsqueeze(1).broadcast_to([P, E, NT]), ALU.is_gt))
            step(V.tensor_reduce(r8[:, 1, :], by_e, AX.X, ALU.add))
            step(V.tensor_tensor_scan(r8[:, 2, :], ones32[:, 0:E], r8[:, 1, :], 0.0, ALU.mult, ALU.add))
            step(V.tensor_tensor(r8[:, 3, :], r8[:, 2, :], r8[:, 1, :], ALU.subtract))
            step(V.tensor_scalar(r8[:, 3, :], r8[:, 3, :], float(P), None, ALU.mult))
            step(V.tensor_tensor(A, A, over_t(r8[:, 3, :]), ALU.add))
            step(V.tensor_tensor(A, A, HOT, ALU.mult))
            step(V.tensor_reduce(rt[:, 2, :], A, AX.X, ALU.add))
            V.tensor_copy(pos[:, :], rt[:, 2, :]).then_inc(pos_done, 1)
            step(V.tensor_tensor(tcmp[:, :, :], r8[0:1, 2, :].unsqueeze(1).broadcast_to([1, ST, E]),
                                 tile_no[0:1, :].unsqueeze(2).broadcast_to([1, ST, E]), ALU.is_le))
            step(V.tensor_reduce(tex[:, :], tcmp[:, :, :], AX.X, ALU.add))
            V.tensor_scalar(expert[:, :], tex[:, :], float(E - 1), None, ALU.min).then_inc(pos_done, 1)

            def attention_spikes(k, i):
                c, s = k + 2 * i, k % 2
                after(dve, wo_done, 2 * (c - 1))
                for h in range(DC):
                    dve.wait_ge(at_done, DC * c + h + 1)
                    V.tensor_scalar(a_sp[s][:, h, :], bank[h][:, :], scale, thr2[:, h:h + 1], ALU.mult,
                                    ALU.is_ge).then_inc(at_spiked, 1)

            def output_spikes(k, i):
                c, s = k + 2 * i, k % 2
                if k >= 2:
                    dve.wait_ge(s_put[s], 16 * (k // 2 + i))
                for pair in range(2):
                    dve.wait_ge(wo_rs, 2 * c + pair + 1)
                    for n in range(2):
                        tl = 2 * pair + n
                        V.scalar_tensor_tensor(s_out[s][:, tl, :], bank[2 + 2 * s + pair][:, n * D:(n + 1) * D],
                                               tile_of(rs, c * CH + tl)[:, 3:4], thr[:, 3 * D:4 * D],
                                               ALU.mult, ALU.is_ge).then_inc(s_made, 1)

            for k in range(4):
                attention_spikes(k, 0)
                if k >= 1:
                    output_spikes(k - 1, 0)
            with dve.Fori(0, NCH // 2 - 2) as i:
                for k in range(4, 6):
                    attention_spikes(k, i)
                    output_spikes(k - 1, i)
            output_spikes(NCH - 1, 0)

            def step_c(k, i):
                s, b = k + 4 * i, k % 2
                if 0 <= k - 2 < ST:
                    dve.wait_ge(down_done, s - 1)
                    after(dve, g_done, s - 3)
                    V.tensor_tensor(e_z[b][:, :], bank[b][:, 0:D], row_a[(k - 2) % 4][:, 0:D], ALU.add).then_inc(z_done, 1)
                if 0 <= k - 1 < ST:
                    dve.wait_ge(eht_done, s)
                    after(dve, down_done, s - 2)
                    V.tensor_copy(e_ht[1 - b][:, :, :], bank[5][:, :].rearrange("p (c n) -> p c n", c=HC)).then_inc(eht_kept, 1)
                if 0 <= k - 2 < ST:
                    dve.wait_ge(g_done, s - 1)
                    if k - 2 >= 4:
                        dve.wait_ge(sent[(k - 2) % 4], 16 * ((k - 2) // 4 + i))
                    o = e_o[(k - 2) % 4]
                    V.tensor_tensor(o[:, :], e_g[b][:, :], row_s[(k - 2) % 4][:, :], ALU.mult).then_inc(sg_done, 1)
                    dve.wait_ge(sg_done, s - 1)
                    V.tensor_tensor(o[:, :], o[:, :], row_a[(k - 2) % 4][:, D + 1:2 * D + 1], ALU.add).then_inc(o_done, 1)
                if k < ST:
                    dve.wait_ge(gate_done, s + 1)
                    dve.wait_ge(up_done, 2 * s + 2)
                    after(dve, eht_done, s - 1)
                    V.scalar_tensor_tensor(e_act[b][:, :], bank[2][:, :], row_a[k % 4][:, D:D + 1], e_gate[b][:, :],
                                           ALU.mult, ALU.mult).then_inc(act_done, 1)

            for k in range(4):
                step_c(k, 0)
            with dve.Fori(0, (ST - 4) // 4) as i:
                for k in range(4, 8):
                    step_c(k, i)
            for k in range(ST // 4 * 4, ST + 2):
                step_c(k, 0)

        @block.gpsimd
        def _(pool):
            G = nc.gpsimd
            step = chain(pool, pool_n)

            def held(s, count):
                after(pool, s, count)
                pool.sem_inc(pool_passed, 1)

            G.iota(none[:, :], [[0, P]], base=N, channel_multiplier=0).then_inc(none_made, 1)
            for n, val in enumerate((LN_EPS, RMS_EPS, D * LN_EPS, -1.0)):
                G.memset(eps4[:, n, :], val)
            step(G.memset(half_neg[:, :], -0.5))
            G.iota(ids[:, :], [[P, NT]], base=0, channel_multiplier=1).then_inc(tables_made, 1)
            G.iota(eidx[:, :], [[1, E]], base=E, channel_multiplier=0, allow_small_or_imprecise_dtypes=True).then_inc(tables_made, 1)
            G.iota(lev[:, :], [[P, NT]], base=0, channel_multiplier=0, allow_small_or_imprecise_dtypes=True).then_inc(tables_made, 1)
            G.iota(tile_no[:, :], [[1, ST]], base=0, channel_multiplier=0, allow_small_or_imprecise_dtypes=True).then_inc(tables_made, 1)
            pool.wait_ge(ld_c, 16 * 4)
            G.tensor_scalar(neg16[:, :], sum_rows[:, 0:2], -16.0, None, ALU.mult).then_inc(neg_made, 1)

            GROUP_STEPS = 6

            def group(g):
                def step(n, ins):
                    ins.then_inc(group_n, 1)
                    held(group_n, GROUP_STEPS * g + n)

                held(stats_done, 4 * (g + 1))
                m, v = (mv[:, bass.ds(4 * g, 4), n:n + 1].rearrange("p a b -> p (a b)") for n in range(2))
                into = lambda buffer: buffer[:, bass.ds(4 * g, 4)]
                t0, t1, t2, t3, t4, t5 = (pw[:, n, :] for n in range(6))
                step(1, G.tensor_tensor(t0, v, eps4[:, 0, :], ALU.add))
                step(2, G.tensor_tensor(t1, t0, half_neg[:, :], ALU.pow))
                G.tensor_copy(into(rstd), t1)
                step(3, G.tensor_tensor(t5, t1, m, ALU.mult))
                step(4, G.tensor_tensor(t2, t1, t1, ALU.mult))
                step(5, G.tensor_tensor(t3, t2, v, ALU.mult))
                step(6, G.tensor_tensor(t4, t3, eps4[:, 1, :], ALU.add))
                G.tensor_tensor(into(rms), t4, half_neg[:, :], ALU.pow)
                G.tensor_tensor(into(nmr), t5, eps4[:, 3, :], ALU.mult).then_inc(rstd_done, 1)

            def put_rms(k, i):
                t = k + 4 * i
                held(xn_done, t + 1)
                held(rstd_done, k // 4 + i + 1)
                G.tensor_copy(xn[k % 4][:, D:D + 1], rms[:, bass.ds(t, 1)]).then_inc(rms_put, 1)

            def norms(k, i):
                t = k + 4 * i
                for n, (a, b, ready) in enumerate(((0, 2, qk_rs), (2, 3, v_rs))):
                    held(squared, 3 * t + b)
                    G.tensor_tensor(pv[:, a:b], tile_of(ss, t)[:, a:b], eps4[:, 2, a:b], ALU.add).then_inc(norm_n, 1)
                    held(norm_n, 2 * t + n + 1)
                    G.tensor_tensor(tile_of(rs, t)[:, a:b], pv[:, a:b], half_neg[:, a:b], ALU.pow).then_inc(ready, 1)

            def scaled(k, i):
                t = k + 4 * i
                held(nx_done, t - 1)
                G.tensor_tensor(sq[k % 2][:, :], xn[k % 4][:, 0:D], fs_row[:, :], ALU.mult).then_inc(sq_done, 1)

            def step_a(k, i, ahead):
                if k >= 1:
                    norms(k - 1, i)
                if k < NT:
                    put_rms(k, i)
                    scaled(k, i)
                if ahead and k % 4 == 3:
                    group(k // 4 + i + 2)

            group(0)
            group(1)
            pool.wait_ge(fs_made, 1)
            for k in range(4):
                step_a(k, 0, True)
            with pool.Fori(0, NT // 4 - 3) as i:
                for k in range(4, 8):
                    step_a(k, i, True)
            for k in range(NT - 8, NT + 1):
                step_a(k, 0, False)

            def number(c0, c1):
                for t in range(c0, c1):
                    G.indirect_dma_start(slots, bass.IndirectOffsetOnAxis(ap=pos[:, t:t + 1], axis=0),
                                         ids[:, t:t + 1], None, bounds_check=ST * P - 1,
                                         oob_is_err=False).then_inc(id_put, 16)

            def norms_out(k, i):
                c = k + 2 * i
                for pair in range(2):
                    q = slice(2 * pair, 2 * pair + 2)
                    of = lambda buffer: buffer[:, bass.ds(c * CH + 2 * pair, 2), 3:4].rearrange("p a b -> p (a b)")
                    held(wo_sq, CH * c + 2 * pair + 2)
                    G.tensor_tensor(pv[:, q], of(ss), eps4[:, 2, q], ALU.add).then_inc(out_n, 1)
                    held(out_n, 2 * c + pair + 1)
                    G.tensor_tensor(of(rs), pv[:, q], half_neg[:, q], ALU.pow).then_inc(wo_rs, 1)

            for k in range(4):
                pool.wait_ge(row_put[k], 16 * NT // 4)
            pool.wait_ge(xt_done, NT)
            for k in range(4):
                G.memset(row_a[k][:, :], 0.0)
                last = G.memset(row_s[k][:, :], 0.0)
            last.then_inc(rows_clear, 1)
            pool.wait_ge(pos_done, 1)
            pool.wait_ge(none_put, 16)
            number(0, NT // 2)
            norms_out(0, 0)
            number(NT // 2, NT)
            with pool.Fori(0, (NCH - 2) // 2) as i:
                for k in range(1, 3):
                    norms_out(k, i)
            norms_out(NCH - 1, 0)

            def gather(k, i):
                s = k + 4 * i
                held(o_done, s - 3)
                G.tensor_copy(from_id[k % 4][:, :], slot_id[:, bass.ds(s, 1)]).then_inc(from_n, 1)
                held(from_n, s + 1)
                for rows, table in ((row_a, rows_a), (row_s, rows_s)):
                    G.indirect_dma_start(rows[k % 4][:, :], None, table,
                                         bass.IndirectOffsetOnAxis(ap=from_id[k % 4][:, :], axis=0),
                                         bounds_check=N - 1, oob_is_err=False).then_inc(got[k % 4], 16)

            def scatter(k, i):
                s = k + 4 * i
                if k >= 4:
                    held(sent[k % 4], 16 * (k // 4 + i))
                G.tensor_copy(to_id[k % 4][:, :], slot_id[:, bass.ds(s, 1)]).then_inc(to_n, 1)
                held(to_n, s + 1)
                held(o_done, s + 1)
                G.indirect_dma_start(out, bass.IndirectOffsetOnAxis(ap=to_id[k % 4][:, :], axis=0),
                                     e_o[k % 4][:, :], None, bounds_check=N - 1,
                                     oob_is_err=False).then_inc(sent[k % 4], 16)

            pool.wait_ge(ids_back, 16)
            pool.wait_ge(x_copied, 16)
            pool.wait_ge(rows_clear, 1)
            for k in range(2):
                pool.wait_ge(s_put[k], 16 * NCH // 2)
            for k in range(4):
                gather(k, 0)
            for k in range(4, 8):
                scatter(k - 4, 0)
                gather(k, 0)
            with pool.Fori(0, (ST - 11) // 4) as i:
                for k in range(8, 12):
                    scatter(k - 4, i)
                    gather(k, i)
            for k in range(36, ST):
                scatter(k - 4, 0)
                gather(k, 0)
            for k in range(ST - 4, ST):
                scatter(k, 0)
            for k in range(4):
                pool.wait_ge(sent[k], 16 * ((ST - k + 3) // 4))


_NAMES = {"x": "L0_attn_query", "wq": "L0_attn_Wq", "wk": "L0_attn_Wk", "wv": "L0_attn_Wv", "wo": "L0_attn_Wo",
          "centroids": "L0_ffn_centroids", "up_w": "L0_ffn_up_w", "down_w": "L0_ffn_down_w"}
_VECTORS = ["L0_attn_gq", "L0_attn_gk", "L0_attn_gv", "L0_attn_go", "L0_attn_bq", "L0_attn_bk", "L0_attn_bv",
            "L0_attn_bo", "L0_attn_betaq", "L0_attn_betak", "L0_attn_betav", "L0_attn_betao", "L0_ffn_scale"]


def _shape_constants():
    import numpy as np

    def bias(dist):
        n = dist + 1
        level = 12 - np.floor(np.log2(n)).astype(np.int64)
        return np.where(n >= N - 1, 0, level)

    a, b = np.arange(P)[None, :], np.arange(P)[:, None]
    col = np.arange(3 * P)[None, :]
    near = bias(np.abs(col - P - b))
    tri = np.stack([(a - b <= -2), (b - a <= -2)], 1).reshape(P, 2 * P)
    pick = np.zeros((P, 64, 4))
    pick[:, 31, 0] = 1
    pick[0, 31, 1] = 1
    pick[P - 1, 31, 2] = 1
    pick[1, 0, 3] = 1
    pick[P - 2, 62, 3] = 1
    scan = (b < a)
    head = (a // 16 == b // 16)
    sums = np.broadcast_to(b % 4 == 0, (P, P))
    consts = np.concatenate([near, tri, pick.reshape(P, 256), scan, head, sums], 1)

    blocks = np.zeros((4, 32, NT, P))
    for r in range(32):
        j = 31 - r
        for t in range(NT):
            k = abs(t - j)
            if k >= 2:
                blocks[0, r, t, :] = 12 - int(np.floor(np.log2(P * k)))
            if k >= 2 and (k + 1) & k == 0:
                if t > j:
                    blocks[1, r, t, P - 1] = -1
                else:
                    blocks[2, r, t, 0] = -1
    blocks[1, 31, NT - 1, P - 2] = -1
    blocks[3, 0, NT - 1, P - 1] = -1
    blocks[2, 0, 0, 1] = -1
    blocks[3, 31, 0, 0] = -1
    bits = lambda m: np.ascontiguousarray(np.ascontiguousarray(m, np.float32).view(np.uint16)[:, 1::2])
    return bits(consts), bits(blocks.transpose(1, 0, 2, 3).reshape(P, N)), np.eye(P, dtype=np.float32)


def kernel(**inputs):
    import numpy as _np
    import concourse.bacc as _bacc
    from concourse import mybir as _mybir
    from concourse.bass_utils import run_bass_kernel_spmd as _run

    nc = _bacc.Bacc("TRN2", target_bir_lowering=False, num_devices=1)
    arrays = {k: _np.ascontiguousarray(inputs[v]) for k, v in _NAMES.items()}
    arrays["x"] = arrays["x"].reshape(N, D)
    rows = [_np.asarray(inputs[n]).reshape(DC, P) for n in _VECTORS]
    rows.append(_np.broadcast_to(_np.asarray(inputs["L0_attn_scale"]).reshape(1, 1), (1, P)))
    arrays["vectors"] = _np.ascontiguousarray(_np.concatenate(rows, 0))
    arrays["consts"], arrays["blocks"], arrays["eye"] = _shape_constants()
    order = ["x", "wq", "wk", "wv", "wo", "vectors", "centroids", "up_w", "down_w", "consts", "blocks", "eye"]
    args = [nc.dram_tensor(f"in_{k}", arrays[k].shape, _mybir.dt.from_np(arrays[k].dtype), kind="ExternalInput").ap()
            for k in order]
    out = nc.dram_tensor("out_x", (N, D), F32, kind="ExternalOutput").ap()
    build(nc, *args, out)
    r = _run(nc, [{f"in_{k}": arrays[k] for k in order}], core_ids=[0])
    return r.results[0]["out_x"].reshape(1, N, D)
```

```python
from contextlib import ExitStack

import concourse.bass as bass
from concourse import mybir

ALU = mybir.AluOpType
ACT = mybir.ActivationFunctionType
AX = mybir.AxisListType
F32 = mybir.dt.float32
F32R = mybir.dt.float32r
BF16 = mybir.dt.bfloat16
I32 = mybir.dt.int32
U16 = mybir.dt.uint16

P = 128
N = 4096
D = 256
DC = D // P
NT = N // P
E = 8
HID = 512
HC = HID // P
ST = NT + E - 1
PAD = 16
CH = 4
CT = CH * P
NCH = NT // CH
YW = 3 * D + E
ROWA = 2 * D + 1
LN_EPS = 1e-5
RMS_EPS = 1e-6

G_, B_, BETA_, FS_, SCALE_ = 0, 8, 16, 24, 26
NV = 27

C_NEAR, C_TRI, C_PICK, C_SCAN, C_HEAD, C_SUM, C_END = 0, 384, 640, 896, 1024, 1152, 1280


SPLITS = {4: [(0, 0), (0, 1), (1, 0)], 5: [(1, 1), (5, 0), (6, 0)], 6: [(7, 0), (2, 0)], 7: [(2, 1), (3, 0)],
          8: [(7, 1), (3, 1), (6, 1), (4, 0), (4, 1), (5, 1)]}
SPLIT_ORDER = [unit for c in sorted(SPLITS) for unit in SPLITS[c]]
BY_POOL = [(7, 1), (6, 1)]


def build(nc, x, wq, wk, wv, wo, vectors, centroids, up_w, down_w, consts, blocks, eye, out):
    with ExitStack() as ctx:
        sem = lambda name: ctx.enter_context(nc.semaphore(name))
        block_arena = [(nc.sbuf_base + 63) // 64 * 64]

        def place(name, shape, dt, at=None):
            size = 4 if dt in (F32, F32R, I32) else 2
            for n in shape[1:]:
                size *= n
            size = (size + 31) // 32 * 32
            if at is None:
                at = block_arena[0]
                block_arena[0] += size
            return nc.alloc_sbuf_tensor_at(name, shape, dt, offset=at), at

        up_raw, at_up = place("up_raw", [P, E, DC, 2 * HID], F32)
        up_lo, _ = place("up_lo", [P, E, DC, 2 * HID], F32R, at=at_up)
        down_sb, at_down = place("down_sb", [P, E, HC, D], F32)
        xs, _ = place("xs", [P, NT, D], F32, at=at_up)
        q_sp, _ = place("q_sp", [P, NT, D], BF16, at=at_up + 4 * NT * D)
        k_sp, _ = place("k_sp", [P, NT, D], BF16, at=at_up + 6 * NT * D)
        w_raw, _ = place("w_raw", [P, 4, DC, D], F32, at=at_down)
        diag, _ = place("diag", [P, 8, P], F32, at=at_down + 8192)
        w_cen, _ = place("w_cen", [P, DC, YW + D], F32, at=at_down + 12288)
        diag16, _ = place("diag16", [P, 3, 8, P], BF16, at=at_down + 20736)
        sgn_row, _ = place("sgn_row", [P, 4, D], F32, at=at_down + 26880)

        up_hi, at_hi = place("up_hi", [P, E, DC, 2 * HID], F32R)
        block_arena[0] = at_hi + 8 * DC * HID
        assert (PAD * 2 * D, at_hi % 64) == (8 * DC * HID, 0)
        v_sp, at_v = place("v_sp", [P, PAD + NT + PAD, D], BF16)
        q_t, at_q = place("q_t", [P, DC, N], BF16)
        blk_tab, at_blk = place("blk_tab", [P, N], BF16)
        assert at_blk + 2 * N == at_hi + E * 8 * DC * HID
        w_hi, at_w = place("w_hi", [P, DC, YW], F32R)
        w_lo, at_w2 = place("w_lo", [P, DC, YW], F32R)
        a_sp = [place(f"a_sp{k}", [P, DC, CT], F32R, at=at_w + 4096 * k)[0] for k in range(2)]
        s_out = [place(f"s_out{k}", [P, CH, D], BF16, at=at_w + 8192 + 2048 * k)[0] for k in range(2)]
        assert at_w2 + 4 * DC * YW - at_w >= 12288
        wo_hi, _ = place("wo_hi", [P, DC, D], F32R)
        wo_lo, _ = place("wo_lo", [P, DC, D], F32R)
        thr, _ = place("thr", [P, 4 * D], F32)
        b_row, _ = place("b_row", [P, 4 * D], BF16)
        b_pick, _ = place("b_pick", [P, P], BF16)
        at_xh = [at_hi, at_hi + 1024]
        at_xl = [at_hi + 2048, at_hi + 3072]
        x_hi = [place(f"x_hi{k}", [P, DC, P], F32R, at=at_xh[k])[0] for k in range(2)]
        x_lo = [place(f"x_lo{k}", [P, DC, P], F32R, at=at_xl[k])[0] for k in range(2)]
        junk = [place(f"junk{k}", [P, D], BF16)[0] for k in range(4)]
        at_w_end = block_arena[0]
        sq, at_sq = zip(*[place(f"sq{k}", [P, DC, P], F32) for k in range(2)])

        xn, at_xn = zip(*[place(f"xn{k}", [P, D + 2], F32) for k in range(4)])

        cst, _ = place("cst", [P, C_END], BF16)
        ident, _ = place("ident", [P, P], F32)
        ident16, _ = place("ident16", [P, P], BF16)
        ones16, _ = place("ones16", [P, P], BF16)
        mean_w, _ = place("mean_w", [P, P], F32, at=at_hi + 4096)
        ones32, _ = place("ones32", [P, P], F32)
        zeros16, _ = place("zeros16", [P, CT], BF16, at=at_q)
        vec_raw, _ = place("vec_raw", [NV, P], F32, at=at_q + 1024)
        vc, _ = place("vc", [P, NV], F32)
        cen_raw, _ = place("cen_raw", [E, D], F32, at=at_q + 2048)
        small, _ = place("small", [P, 128], F32)
        b16, _ = place("b16", [P, 24], BF16)
        eps3, _ = place("eps3", [P, 3], F32)
        half_neg, _ = place("half_neg", [P, 2, 2], F32)
        st6, _ = place("st6", [P, 2, 6], F32)
        mv2, _ = place("mv2", [P, 2, 2], F32)
        neg_mean, _ = place("neg_mean", [P, NT], F32)
        inv_var, _ = place("inv_var", [P, NT], F32)
        var_in, _ = place("var_in", [P, NT, 2], F32)
        inv_std, _ = place("inv_std", [P, NT, 2], F32)
        pv, _ = place("pv", [P, 2, 4], F32)
        nmr, _ = place("nmr", [P, NT], F32)
        ss, _ = place("ss", [P, NT, 4], F32)
        rs, _ = place("rs", [P, NT, 4], F32)
        ny, _ = place("ny", [P, E], F32)
        dots, _ = place("dots", [P, NT, E + 1], F32, at=at_hi + 6912)
        ra, _ = place("ra", [P, NT, E], F32, at=at_xh[0])
        rb, _ = place("rb", [P, NT, E], F32, at=at_xh[1])
        hot, _ = place("hot", [P, NT, E], F32, at=at_xl[0])
        hot16, _ = place("hot16", [P, NT, E], BF16, at=at_hi + 4608)
        eidx, _ = place("eidx", [P, E], F32)
        lev, _ = place("lev", [P, NT], F32)
        rt, _ = place("rt", [P, 4, NT], F32)
        r8, _ = place("r8", [P, 6, E], F32)
        pos, _ = place("pos", [P, NT], I32)
        ids, _ = place("ids", [P, NT], I32)
        tile_no, _ = place("tile_no", [P, ST], F32)
        tcmp, _ = place("tcmp", [1, ST, E], F32, at=at_hi + 5632)
        tex, _ = place("tex", [1, ST], F32)
        expert, _ = place("expert", [1, ST], I32)
        none, _ = place("none", [ST, P], I32, at=at_hi + 5120)
        slot_id, _ = place("slot_id", [P, ST], I32)
        from_id = [place(f"from_id{k}", [P, 1], I32)[0] for k in range(4)]
        to_id = [place(f"to_id{k}", [P, 1], I32)[0] for k in range(4)]
        from_n, to_n = sem("from_n"), sem("to_n")
        pool_passed, dve_passed = sem("pool_passed"), sem("dve_passed")
        sc16, _ = place("sc16", [P, D], BF16)
        sv_row, _ = place("sv_row", [P, D], F32, at=at_sq[0])
        m_f, _ = place("m_f", [P, D], F32, at=at_xl[1])
        m_hi, _ = place("m_hi", [P, D], BF16, at=at_sq[1])
        m_lo, _ = place("m_lo", [P, D], BF16, at=at_sq[1] + 2 * D)
        neg16, _ = place("neg16", [P, 2], BF16)
        thr2, _ = place("thr2", [P, 2], F32)

        row_a = [place(f"row_a{k}", [P, ROWA], F32, at=at_xn[2 * k] if k < 2 else None)[0] for k in range(4)]
        row_s = [place(f"row_s{k}", [P, D], BF16)[0] for k in range(4)]
        over = [at_w]

        def over_weights(name, n, shape, dt=F32):
            made = []
            for k in range(n):
                made.append(place(f"{name}{k}", shape, dt, at=over[0])[0])
                over[0] += 4 * shape[1] * (shape[2] if len(shape) > 2 else 1)
            return made

        e_xh, e_xl = over_weights("e_xh", 2, [P, DC, P], F32R), over_weights("e_xl", 2, [P, DC, P], F32R)
        e_ht = over_weights("e_ht", 2, [P, HC, P])
        e_o = over_weights("e_o", 4, [P, D])
        e_gate, e_act = over_weights("e_gate", 2, [P, HID]), over_weights("e_act", 2, [P, HID])
        e_g, e_z = over_weights("e_g", 2, [P, D]), over_weights("e_z", 2, [P, D])
        assert over[0] <= at_w_end, (over[0], at_w_end)
        assert block_arena[0] <= nc.sbuf_usable_end, (block_arena[0], nc.sbuf_usable_end)

        bank = [ctx.enter_context(nc.psum_tensor(f"bank{k}", [P, 512], F32)) for k in range(8)]
        rows_a = nc.dram_tensor("rows_a", (N, ROWA), F32, kind="Internal").ap()
        rows_s = nc.dram_tensor("rows_s", (N, D), BF16, kind="Internal").ap()
        slots = nc.dram_tensor("slots", (ST * P, 1), I32, kind="Internal").ap()

        near = cst[:, C_NEAR:C_TRI]
        tri = cst[:, C_TRI:C_PICK].rearrange("p (a b) -> p a b", a=2)
        pick = cst[:, C_PICK:C_SCAN]
        scan_tri = cst[:, C_SCAN:C_HEAD]
        head = cst[:, C_HEAD:C_SUM]
        sum_rows = cst[:, C_SUM:C_END]

        ld_w, ld_c, ld_b, x_loaded = sem("ld_w"), sem("ld_c"), sem("ld_b"), sem("x_loaded")
        x_copied, up_loaded, down_loaded = sem("x_copied"), sem("up_loaded"), sem("down_loaded")
        consts_set = sem("consts_set")
        vec_turned, w_turned, vec_kept, bias_mean = sem("vec_turned"), sem("w_turned"), sem("vec_kept"), sem("bias_mean")
        diag_made, rows_made, w_centred, w_high = sem("diag_made"), sem("rows_made"), sem("w_centred"), sem("w_high")
        setup_done, none_made, tables_made = sem("setup_done"), sem("none_made"), sem("tables_made")
        dve_n, pool_n = sem("dve_n"), sem("pool_n")
        group_n, aggr_done, norm_n, sq_done, out_n, neg_made, rows_clear = sem("group_n"), sem("aggr_done"), sem("norm_n"), sem("sq_done"), sem("out_n"), sem("neg_made"), sem("rows_clear")
        stats_done, rstd_done, xn_done, rms_put = sem("stats_done"), sem("rstd_done"), sem("xn_done"), sem("rms_put")
        xt_done, hi_done, lo_done = sem("xt_done"), sem("hi_done"), sem("lo_done")
        row_put = [sem(f"row_put{k}") for k in range(4)]
        qk_done, v_done, squared, rs_done = sem("qk_done"), sem("v_done"), sem("squared"), sem("rs_done")
        spiked, dots_done, var_n, st_n = sem("spiked"), sem("dots_done"), sem("var_n"), sem("st_n")
        sums_done, qt_done, qt_kept = sem("sums_done"), sem("qt_done"), sem("qt_kept")
        hot_done, ranks_done, pos_done, none_put, id_put, ids_back = (
            sem("hot_done"), sem("ranks_done"), sem("pos_done"), sem("none_put"), sem("id_put"), sem("ids_back"))
        m_done, cvec_done, sv_done = sem("m_done"), sem("cvec_done"), sem("sv_done")
        at_done, at_spiked, wo_done, wo_sq, wo_rs, s_made = (sem("at_done"), sem("at_spiked"), sem("wo_done"),
                                                            sem("wo_sq"), sem("wo_rs"), sem("s_made"))
        s_put = [sem(f"s_put{k}") for k in range(2)]
        got_a, got_s = ([sem(f"{name}{k}") for k in range(4)] for name in ("got_a", "got_s"))
        sent = [sem(f"sent{k}") for k in range(4)]
        ext_done, ext_kept, up_done, gate_done, act_done = (sem("ext_done"), sem("ext_kept"), sem("up_done"),
                                                          sem("gate_done"), sem("act_done"))
        up_high, up_split, pool_split, ext_high = sem("up_high"), sem("up_split"), sem("pool_split"), sem("ext_high")
        eht_done, eht_kept, down_done, z_done, g_done, sg_done, o_done = (
            sem("eht_done"), sem("eht_kept"), sem("down_done"), sem("z_done"), sem("g_done"), sem("sg_done"), sem("o_done"))

        def after(eng, s, count):
            if not isinstance(count, int) or count > 0:
                eng.wait_ge(s, count)

        def tile_of(buffer, t):
            return buffer[:, bass.ds(t, 1), :].rearrange("p a n -> p (a n)")

        def chain(eng, s):
            count = [0]

            def step(ins):
                count[0] += 1
                ins.then_inc(s, 1)
                eng.wait_ge(s, count[0])
            return step

        block = ctx.enter_context(nc.Block())

        @block.sync
        def _(sp):
            for p, w in enumerate((wq, wk, wv, wo)):
                sp.dma_start(w_raw[:, p, :, :], w.rearrange("(c p) n -> p c n", p=P)).then_inc(ld_w, 16)
            for g in range(NT // 4):
                if g:
                    sp.wait_ge(x_loaded, 16 * g)
                sp.dma_start(xs[:, 4 * g:4 * g + 4, :],
                             x[512 * g:512 * g + 512, :].rearrange("(t p) n -> p t n", p=P)).then_inc(x_loaded, 16)
            sp.dma_start(blk_tab[:, :].bitcast(U16), blocks).then_inc(ld_b, 16)
            sp.dma_start(rows_a[:, D + 1:2 * D + 1], x).then_inc(x_copied, 16)
            sp.wait_ge(none_made, 1)
            sp.dma_start(slots.rearrange("(s p) a -> s (p a)", p=P), none[:, :]).then_inc(none_put, 16)
            sp.wait_ge(setup_done, 1)
            for e in range(0, E, 2):
                sp.dma_start(down_sb[:, e:e + 2, :, :],
                             down_w[e:e + 2].rearrange("e (c p) n -> p e c n", p=P)).then_inc(down_loaded, 16)
            for t in range(NT):
                sp.wait_ge(rms_put, t + 1)
                sp.dma_start(rows_a[t * P:(t + 1) * P, 0:D + 1], xn[t % 4][:, 0:D + 1]).then_inc(row_put[t % 4], 16)
            sp.wait_ge(xn_done, NT)
            sp.wait_ge(stats_done, NT)
            sp.wait_ge(sums_done, NT)
            sp.wait_ge(qt_done, NT)
            for e in range(E):
                sp.dma_start(up_raw[:, e, :, :], up_w[e].rearrange("(c p) n -> p c n", p=P)).then_inc(up_loaded, 16)
            for c in range(NCH):
                if c == NCH // 2:
                    sp.wait_ge(id_put, 16 * NT)
                    sp.dma_start(slot_id[:, :], slots.rearrange("(s p) a -> p (s a)", p=P),
                                 allow_slow_non_contiguous=True).then_inc(ids_back, 16)
                sp.wait_ge(s_made, CH * (c + 1))
                sp.dma_start(rows_s[c * CT:(c + 1) * CT, :].rearrange("(t p) n -> p t n", p=P),
                             s_out[c % 2][:, :, :]).then_inc(s_put[c % 2], 16)

        @block.tensor
        def _(pe):
            pe.wait_ge(consts_set, 5)
            pe.wait_ge(ld_c, 16 * 4)
            pe.transpose(bank[4][0:P, 0:NV], vec_raw[:, :], ident[0:NV, 0:NV])
            for c in range(DC):
                last = pe.transpose(bank[4][:, 64 + E * c:64 + E * c + E], cen_raw[:, c * P:(c + 1) * P],
                                    ident[0:E, 0:E])
            last.then_inc(vec_turned, 1)
            pe.wait_ge(ld_w, 64)
            for p in range(4):
                for ic in range(DC):
                    for oc in range(DC):
                        last = pe.transpose(bank[p][:, ic * D + oc * P:ic * D + (oc + 1) * P],
                                            w_raw[:, p, oc, ic * P:(ic + 1) * P], ident[:, :])
                last.then_inc(w_turned, 1)
            pe.wait_ge(vec_kept, 1)
            pe.matmul(bank[5][:, 0:8], mean_w[:, :], vc[:, B_:B_ + 8], start=True, stop=True).then_inc(bias_mean, 1)
            for mark, where in ((1, 6), (2, 4)):
                pe.wait_ge(diag_made, mark)
                for h in range(2):
                    last = pe.matmul(bank[where + h][:, :], ones32[:, :], diag[:, 4 * h:4 * h + 4, :],
                                     start=True, stop=True)
                last.then_inc(rows_made, 1)
            pe.wait_ge(diag_made, 3)
            for c in range(DC):
                last = pe.matmul(bank[7][:, D:D + E], ones32[:, :], small[:, 64 + E * c:64 + E * c + E],
                                 start=(c == 0), stop=(c == DC - 1))
            last.then_inc(rows_made, 1)
            for h in range(2):
                for part in range(3):
                    last = pe.matmul(bank[4 + h][32 * part:32 * part + 32, :], ones16[:, 0:32],
                                     diag16[:, part, 4 * h:4 * h + 4, :], start=True, stop=True)
            last.then_inc(rows_made, 1)
            pe.matmul(bank[6][:, :], zeros16[:, 0:P], zeros16[:, :], start=True, stop=True)

            def transpose_x(k, i):
                t, s = k + 4 * i, k % 2
                pe.wait_ge(xn_done, t + 1)
                for c in range(DC):
                    last = pe.transpose(bank[s][:, c * P:(c + 1) * P], xn[k % 4][:, c * P:(c + 1) * P], ident[:, :])
                last.then_inc(xt_done, 1)

            def project(k, i):
                t, s = k + 4 * i, k % 2
                pe.wait_ge(lo_done, t + 1)
                pe.wait_ge(sq_done, t + 1)
                for b, c0, c1, done in ((2 + s, 0, 2 * D, qk_done), (4 + s, 2 * D, YW, v_done)):
                    if done is qk_done:
                        after(pe, spiked, 3 * (t - 1) - 1)
                    else:
                        after(pe, dots_done, t - 1)
                        for c in range(DC):
                            pe.matmul(bank[b][:, D + E:D + E + 1], sq[s][:, c, :], ones32[:, 0:1],
                                      start=(c == 0), stop=(c == DC - 1))
                    first = True
                    for left, right in ((x_hi, w_hi), (x_hi, w_lo), (x_lo, w_hi)):
                        for c in range(DC):
                            pe.matmul(bank[b][:, 0:c1 - c0], left[s][:, c, :], right[:, c, c0:c1],
                                      start=first, stop=False)
                            first = False
                    cb = min(c1, 3 * D)
                    pe.matmul(bank[b][:, 0:cb - c0], b_pick[0:96, :], b_row[0:96, c0:cb],
                              start=False, stop=True).then_inc(done, 1)

            def accumulate(k, i):
                t = k + 4 * i
                pe.wait_ge(spiked, 3 * (t + 1))
                after(pe, qt_kept, t)
                for c in range(DC):
                    last = pe.transpose(bank[7][:, 64 * c:64 * c + 64].bitcast(BF16),
                                        tile_of(q_sp, t)[:, c * P:(c + 1) * P], ident16[:, :])
                last.then_inc(qt_done, 1)
                for c in range(DC):
                    pe.matmul(bank[6][:, c * P:(c + 1) * P], tile_of(k_sp, t)[:, c * P:(c + 1) * P],
                              tile_of(v_sp, t + PAD)[:, c * P:(c + 1) * P], start=False, stop=False,
                              skip_group_check=True)
                pe.matmul(bank[6][:, D:2 * D], pick[:, bass.ds(4 * t, P)], tile_of(v_sp, t + PAD),
                          start=False, stop=False, skip_group_check=True).then_inc(sums_done, 1)

            def step_a(k, i):
                if k < NT:
                    transpose_x(k, i)
                if 0 <= k - 1 < NT:
                    project(k - 1, i)
                if 0 <= k - 3 < NT:
                    accumulate(k - 3, i)

            for k in range(4):
                step_a(k, 0)
            with pe.Fori(0, NT // 4 - 1) as i:
                for k in range(4, 8):
                    step_a(k, i)
            for k in range(NT, NT + 3):
                step_a(k, 0)

            pe.wait_ge(m_done, 1)
            pe.wait_ge(qt_kept, NT)
            pe.matmul(bank[7][:, 0:D], sum_rows, sc16[:, :], start=True, stop=True).then_inc(sv_done, 1)
            pe.wait_ge(m_done, 2)
            pe.wait_ge(neg_made, 1)
            for c in range(DC):
                cs = slice(c * P, (c + 1) * P)
                pe.matmul(bank[7][:, c:c + 1], m_hi[:, cs], ones16[:, 0:1], start=True, stop=False)
                pe.matmul(bank[7][:, c:c + 1], m_lo[:, cs], ones16[:, 0:1], start=False, stop=False)
                last = pe.matmul(bank[7][:, c:c + 1], sc16[:, cs], neg16[:, 0:1], start=False, stop=True)
            last.then_inc(cvec_done, 1)

            def attend(k, i):
                c = k + 2 * i
                pe.wait_ge(blk_ready, 16)
                for h in range(DC):
                    hs = slice(h * P, (h + 1) * P)
                    ps = bank[h]
                    after(pe, at_spiked, DC * (c - 1) + h + 1)
                    pe.matmul(ps[:, :], sc16[:, hs], blk_tab[:, bass.ds(c * CT, CT)], start=True, stop=False)
                    for part in (m_hi, m_lo):
                        pe.matmul(ps[:, :], part[:, hs], q_t[:, h, bass.ds(c * CT, CT)], start=False, stop=False)
                    for j in range(-1, CH + 1):
                        a, b = max(0, j - 1), min(CH, j + 2)
                        pe.matmul(ps[:, a * P:b * P], tile_of(v_sp, CH * c + (PAD + j))[:, hs],
                                  near[:, (a - j + 1) * P:(b - j + 1) * P], start=False, stop=False)
                    for b in range(CH):
                        for n, d in enumerate((2, 4, 8, 16)):
                            for side in range(2):
                                at = PAD + b + (d if side else -d)
                                last = pe.matmul(ps[:, b * P:(b + 1) * P], tile_of(v_sp, CH * c + at)[:, hs],
                                                 tri[:, side, :], start=False,
                                                 stop=(b == CH - 1 and n == 3 and side == 1))
                    last.then_inc(at_done, 1)

            def project_out(k, i):
                c, s = k + 2 * i, k % 2
                pe.wait_ge(at_spiked, DC * (c + 1))
                for pair in range(2):
                    ps = bank[2 + 2 * s + pair]
                    after(pe, s_made, CH * (c - 2) + 2 * pair + 2)
                    for n in range(2):
                        tl = 2 * pair + n
                        o = ps[:, n * D:(n + 1) * D]
                        for m, w in enumerate((wo_hi, wo_lo)):
                            for h in range(DC):
                                pe.matmul(o, a_sp[s][:, h, tl * P:(tl + 1) * P], w[:, h, :],
                                          start=(m == 0 and h == 0), stop=False)
                        last = pe.matmul(o, b_pick[0:96, :], b_row[0:96, 3 * D:4 * D], start=False, stop=True)
                    last.then_inc(wo_done, 1)

            blk_ready = ld_b
            attend(0, 0)
            pe.wait_ge(hot_done, 1)
            pe.matmul(bank[6][:, 0:NT * E], scan_tri, hot16[:, :, :], start=True, stop=True)
            pe.matmul(bank[6][:, NT * E:2 * NT * E], ones16[:, :], hot16[:, :, :], start=True, stop=True) \
                .then_inc(ranks_done, 1)
            for k in range(1, 4):
                attend(k, 0)
                project_out(k - 1, 0)
            with pe.Fori(0, NCH // 2 - 2) as i:
                for k in range(4, 6):
                    attend(k, i)
                    project_out(k - 1, i)
            project_out(NCH - 1, 0)

            def turn_rows(k, i):
                s = k + 4 * i
                pe.wait_ge(got_a[k % 4], 16 * (k // 4 + i + 1))
                after(pe, ext_kept, s)
                for c in range(DC):
                    last = pe.transpose(bank[4][:, c * P:(c + 1) * P], row_a[k % 4][:, c * P:(c + 1) * P], ident[:, :])
                last.then_inc(ext_done, 1)

            def turn_hidden(k, i):
                s = k + 4 * i
                pe.wait_ge(act_done, s + 1)
                after(pe, eht_kept, s)
                for c in range(HC):
                    last = pe.transpose(bank[5][:, c * P:(c + 1) * P], e_act[k % 2][:, c * P:(c + 1) * P], ident[:, :])
                last.then_inc(eht_done, 1)

            def expert_up(k, i):
                s = k + 4 * i
                e = pe.value_load(expert[0:1, bass.ds(s, 1)], min_val=0, max_val=E - 1)
                pe.wait_ge(ext_kept, s + 1)
                after(pe, act_done, s)
                hi, lo = (w[:, bass.ds(e, 1), :, :].rearrange("p a c n -> p (a c) n") for w in (up_hi, up_lo))
                for half in (1, 0):
                    for n, (left, w) in enumerate(((e_xh, hi), (e_xh, lo), (e_xl, hi))):
                        for c in range(DC):
                            last = pe.matmul(bank[2 + half][:, :], left[k % 2][:, c, :],
                                             w[:, c, half * HID:(half + 1) * HID],
                                             start=(n == 0 and c == 0), stop=(n == 2 and c == DC - 1))
                    last.then_inc(up_done, 1)

            def expert_down(k, i):
                s = k + 4 * i
                e = pe.value_load(expert[0:1, bass.ds(s, 1)], min_val=0, max_val=E - 1)
                pe.wait_ge(eht_kept, s + 1)
                after(pe, z_done, s - 1)
                w = down_sb[:, bass.ds(e, 1), :, :].rearrange("p a c n -> p (a c) n")
                for c in range(HC):
                    last = pe.matmul(bank[k % 2][:, 0:D], e_ht[k % 2][:, c, :], w[:, c, :],
                                     start=(c == 0), stop=(c == HC - 1))
                last.then_inc(down_done, 1)

            def step_c(k, i):
                if k < ST:
                    turn_rows(k, i)
                if 0 <= k - 2 < ST:
                    expert_down(k - 2, i)
                if 0 <= k - 1 < ST:
                    turn_hidden(k - 1, i)
                if k < ST:
                    expert_up(k, i)

            pe.wait_ge(pos_done, 2)
            pe.wait_ge(s_made, NT)
            pe.wait_ge(up_split, 2 * E - len(BY_POOL))
            pe.wait_ge(pool_split, len(BY_POOL))
            pe.wait_ge(down_loaded, 16 * E // 2)
            for k in range(4):
                step_c(k, 0)
            with pe.Fori(0, (ST - 4) // 4) as i:
                for k in range(4, 8):
                    step_c(k, i)
            for k in range(ST // 4 * 4, ST + 2):
                step_c(k, 0)

        @block.scalar
        def _(act):
            act.dma_start(cst[:, :].bitcast(U16), consts).then_inc(ld_c, 16)
            act.dma_start(ident[:, :], eye).then_inc(ld_c, 16)
            act.dma_start(vec_raw[:, :], vectors).then_inc(ld_c, 16)
            act.dma_start(cen_raw[:, :], centroids).then_inc(ld_c, 16)
            act.wait_ge(w_centred, 1)
            act.activation(w_hi[:, :, :], w_cen[:, :, 0:YW], ACT.Copy).then_inc(w_high, 1)
            act.activation(wo_hi[:, :, :], w_cen[:, :, YW:YW + D], ACT.Copy).then_inc(w_high, 1)

            def normalize(k, i):
                t = k + 4 * i
                act.wait_ge(rstd_done, k // 2 + 2 * i + 1)
                act.wait_ge(x_loaded, 16 * (k // 4 + i + 1))
                if k >= 4:
                    act.wait_ge(xt_done, t - 3)
                    act.wait_ge(row_put[k % 4], 16 * (k // 4 + i))
                act.activation(xn[k % 4][:, 0:D], tile_of(xs, t), ACT.Identity, bias=nmr[:, bass.ds(t, 1)],
                               scale=inv_std[:, bass.ds(t, 1), 0:1].rearrange("p a b -> p (a b)")).then_inc(xn_done, 1)

            def step_a(k, i):
                t, s = k + 4 * i, k % 2
                if k < NT:
                    act.wait_ge(xt_done, t + 1)
                    act.activation(x_hi[s][:, :, :], bank[s][:, 0:D].rearrange("p (c n) -> p c n", c=DC),
                                   ACT.Copy).then_inc(hi_done, 1)
                    for c in range(DC):
                        last = act.activation(sq[s][:, c, :], bank[s][:, c * P:(c + 1) * P], ACT.Square,
                                              scale=vc[:, FS_ + c:FS_ + c + 1])
                    last.then_inc(sq_done, 1)
                if k + 1 < NT:
                    normalize(k + 1, i)
                if k >= 1:
                    u, su = t - 1, (k - 1) % 2
                    act.wait_ge(qk_done, u + 1)
                    for n in range(3):
                        if n == 2:
                            act.wait_ge(v_done, u + 1)
                        after(act, squared, 3 * (u - 1) + n + 1)
                        src = bank[2 + su][:, n * D:(n + 1) * D] if n < 2 else bank[4 + su][:, 0:D]
                        act.activation(junk[n][:, :], src, ACT.Square,
                                       accum_out=tile_of(ss, u)[:, n:n + 1]).then_inc(squared, 1)

            normalize(0, 0)
            for k in range(4):
                step_a(k, 0)
            with act.Fori(0, NT // 4 - 2) as i:
                for k in range(4, 8):
                    step_a(k, i)
            for k in range(NT - 4, NT + 1):
                step_a(k, 0)

            def squares_out(k, i):
                c, s = k + 2 * i, k % 2
                for pair in range(2):
                    act.wait_ge(wo_done, 2 * c + pair + 1)
                    for n in range(2):
                        m = 2 * pair + n
                        after(act, wo_sq, CH * (c - 1) + m + 1)
                        act.activation(junk[m][:, :], bank[2 + 2 * s + pair][:, n * D:(n + 1) * D], ACT.Square,
                                       accum_out=ss_out(c, m)).then_inc(wo_sq, 1)

            def ss_out(c, n):
                return ss[:, bass.ds(c * CH + n, 1), 3:4].rearrange("p a b -> p (a b)")

            def high_parts(c):
                for e, half in SPLITS[c]:
                    act.activation(up_hi[:, e, half, :], up_raw[:, e, half, :], ACT.Copy).then_inc(up_high, 1)

            for c in range(NCH):
                squares_out(c % 2, c // 2)
                if c == 3:
                    act.wait_ge(up_loaded, 16 * E)
                    act.wait_ge(pos_done, 2)
                    act.wait_ge(none_put, 16)
                if c + 1 in SPLITS and c < NCH - 1:
                    act.wait_ge(at_done, DC * (c + 1) if c + 1 < 7 else DC * NCH)
                    high_parts(c + 1)
            high_parts(NCH)

            def step_c(k, i):
                s, b = k + 4 * i, k % 2
                if k < ST:
                    act.wait_ge(ext_done, s + 1)
                    after(act, up_done, 2 * (s - 1))
                    for c in range(DC):
                        last = act.activation(e_xh[b][:, c, :], bank[4][:, c * P:(c + 1) * P], ACT.Copy,
                                              scale=vc[:, FS_ + c:FS_ + c + 1])
                    last.then_inc(ext_high, 1)
                if k >= 2:
                    act.wait_ge(z_done, s - 1)
                    after(act, sg_done, s - 3)
                    act.activation(e_g[b][:, :], e_z[b][:, :], ACT.Silu).then_inc(g_done, 1)
                if k < ST:
                    act.wait_ge(up_done, 2 * s + 1)
                    after(act, act_done, s - 1)
                    act.activation(e_gate[b][:, :], bank[3][:, :], ACT.Silu,
                                   scale=row_a[k % 4][:, D:D + 1]).then_inc(gate_done, 1)

            for k in range(4):
                step_c(k, 0)
            with act.Fori(0, (ST - 4) // 4) as i:
                for k in range(4, 8):
                    step_c(k, i)
            for k in range(ST // 4 * 4, ST + 2):
                step_c(k, 0)

        @block.vector
        def _(dve):
            V = nc.vector
            step = chain(dve, dve_n)
            for m, val in ((ones32, 1.0), (ones16, 1.0), (mean_w, 1.0 / D), (zeros16, 0.0)):
                V.memset(m[:, :], val).then_inc(consts_set, 1)
            step(V.memset(b_pick[:, :], 0.0))
            for part in range(3):
                last = V.memset(b_pick[32 * part:32 * part + 1, :], 1.0)
            last.then_inc(consts_set, 1)

            def stats(k, i, part=None):
                t = k + 4 * i
                m, v, into = mv2[:, k % 2, 0:1], mv2[:, k % 2, 1:2], tile_of(var_in, t)
                if part in (None, 0):
                    dve.wait_ge(x_loaded, 16 * (k // 4 + i + 1))
                    V.bn_stats(st6[:, k % 2, :], tile_of(xs, t)).then_inc(st_n, 1)
                if part in (None, 1):
                    dve.wait_ge(st_n, t + 1)
                    dve.sem_inc(dve_passed, 1)
                    V.bn_aggr(mv2[:, k % 2, :], st6[:, k % 2, :]).then_inc(aggr_done, 1)
                if part in (None, 2):
                    dve.wait_ge(aggr_done, t + 1)
                    V.tensor_scalar(into[:, 0:1], v, LN_EPS, None, ALU.add).then_inc(var_n, 1)
                    V.tensor_scalar(neg_mean[:, bass.ds(t, 1)], m, -1.0, None, ALU.mult)
                if part in (None, 3):
                    dve.wait_ge(var_n, 2 * t + 1)
                    V.reciprocal(inv_var[:, bass.ds(t, 1)], into[:, 0:1]).then_inc(var_n, 1)
                if part in (None, 4):
                    dve.wait_ge(var_n, 2 * t + 2)
                    V.tensor_scalar(into[:, 1:2], v, inv_var[:, bass.ds(t, 1)], RMS_EPS, ALU.mult,
                                    ALU.add).then_inc(stats_done, 1)

            dve.wait_ge(vec_turned, 1)
            step(V.tensor_copy(small[:, 48:64], bank[4][:, 64:80]))
            V.tensor_copy(vc[:, :], bank[4][:, 0:NV]).then_inc(vec_kept, 1)
            dve.wait_ge(vec_kept, 1)
            for c in range(DC):
                V.tensor_scalar(w_cen[:, c, 3 * D:YW], small[:, 48 + E * c:56 + E * c],
                                vc[:, FS_ + c:FS_ + c + 1], None, ALU.mult)
            step(V.tensor_tensor(small[:, 64:80], small[:, 48:64], small[:, 48:64], ALU.mult))
            gain, beta = vc[:, G_:G_ + 8], vc[:, BETA_:BETA_ + 8]
            sgn, mag, inv, lim, dead = (small[:, 8 * n:8 * n + 8] for n in range(5))
            spread = lambda col: col.unsqueeze(2).broadcast_to([P, col.shape[1], P])
            eye8 = lambda m, n: m[:, :].unsqueeze(1).broadcast_to([P, n, P])
            step(V.tensor_scalar(sgn, gain, 0.0, 2.0, ALU.is_ge, ALU.mult))
            step(V.tensor_scalar(sgn, sgn, -1.0, None, ALU.add))
            V.tensor_tensor(diag[:, :, :], eye8(ident, 8), spread(sgn), ALU.mult).then_inc(diag_made, 1)
            step(V.tensor_tensor(mag, gain, sgn, ALU.mult))
            step(V.tensor_scalar(mag, mag, 1e-30, None, ALU.max))
            step(V.reciprocal(inv, mag))
            step(V.tensor_scalar(lim, beta, -1.0, 1.0, ALU.mult, ALU.add))
            step(V.tensor_tensor(lim, lim, inv, ALU.mult))
            step(V.tensor_scalar(dead, gain, 0.0, 1e20, ALU.is_equal, ALU.mult))
            step(V.tensor_tensor(lim, lim, dead, ALU.subtract))
            step(V.tensor_scalar(lim, lim, 1.0 / 16, None, ALU.mult))
            dve.wait_ge(bias_mean, 1)
            step(V.tensor_copy(small[:, 88:96], bank[5][:, 0:8]))
            dve.wait_ge(rows_made, 1)
            V.tensor_tensor(diag[:, :, :], eye8(ident, 8), spread(lim), ALU.mult).then_inc(diag_made, 1)
            for h in range(2):
                last = V.tensor_copy(sgn_row[:, 2 * h:2 * h + 2, :].rearrange("p a n -> p (a n)"), bank[6 + h][:, :])
            step(last)
            for p in range(4):
                dve.wait_ge(w_turned, p + 1)
                last = V.tensor_reduce(small[:, 96 + 2 * p:98 + 2 * p],
                                       bank[p][:, :].rearrange("p (c n) -> p c n", c=DC), AX.X, ALU.add)
            step(last)
            step(V.tensor_scalar(small[:, 96:104], small[:, 96:104], 1.0 / D, None, ALU.mult))
            for p in range(4):
                at = p * D if p < 3 else YW
                for c in range(DC):
                    last = V.scalar_tensor_tensor(w_cen[:, c, at:at + D], bank[p][:, c * D:(c + 1) * D],
                                                  small[:, 96 + 2 * p + c:97 + 2 * p + c], sgn_row[:, p, :],
                                                  ALU.subtract, ALU.mult)
            last.then_inc(w_centred, 1)
            dve.wait_ge(rows_made, 2)
            for h in range(2):
                V.tensor_copy(thr[:, 512 * h:512 * h + 512], bank[4 + h][:, :])
            bm, bc = small[:, 104:108], small[:, 112:120]
            step(V.tensor_tensor(bm, small[:, 88:96:2], small[:, 89:96:2], ALU.add))
            step(V.tensor_tensor(bc.rearrange("p (a b) -> p a b", b=2),
                                 vc[:, B_:B_ + 8].rearrange("p (a b) -> p a b", b=2),
                                 bm.unsqueeze(2).broadcast_to([P, 4, 2]), ALU.subtract))
            step(V.tensor_tensor(bc, bc, sgn, ALU.mult))
            for part in range(3):
                step(V.tensor_copy(b16[:, 8 * part:8 * part + 8], bc))
                if part < 2:
                    step(V.tensor_tensor(bc, bc, b16[:, 8 * part:8 * part + 8], ALU.subtract))
            step(V.tensor_copy(ident16[:, :], ident[:, :]))
            for part in range(3):
                last = V.tensor_tensor(diag16[:, part, :, :], eye8(ident16, 8), spread(b16[:, 8 * part:8 * part + 8]),
                                       ALU.mult)
            last.then_inc(diag_made, 1)
            dve.wait_ge(rows_made, 3)
            step(V.tensor_copy(ny[:, :], bank[7][:, D:D + E]))
            dve.wait_ge(w_high, 2)
            V.tensor_tensor(w_lo[:, :, :], w_cen[:, :, 0:YW], w_hi[:, :, :].bitcast(F32), ALU.subtract)
            V.tensor_tensor(wo_lo[:, :, :], w_cen[:, :, YW:YW + D], wo_hi[:, :, :].bitcast(F32), ALU.subtract)
            dve.wait_ge(rows_made, 4)
            for h in range(2):
                last = V.tensor_copy(b_row[0:96, 512 * h:512 * h + 512], bank[4 + h][0:96, :])
            last.then_inc(setup_done, 1)

            V.memset(v_sp[:, 0:PAD, :], 0.0)
            step(V.memset(v_sp[:, PAD + NT:PAD + NT + PAD, :], 0.0))
            for k in range(8):
                stats(k, 0)

            def low_part(k, i):
                t, s = k + 4 * i, k % 2
                dve.wait_ge(hi_done, t + 1)
                dve.wait_ge(sq_done, t + 1)
                V.tensor_tensor(x_lo[s][:, :, :], bank[s][:, 0:D].rearrange("p (c n) -> p c n", c=DC),
                                x_hi[s][:, :, :].bitcast(F32), ALU.subtract).then_inc(lo_done, 1)

            def spikes(k, i, n):
                t, s = k + 4 * i, k % 2
                r = tile_of(rs, t)
                source = bank[2 + s][:, n * D:(n + 1) * D] if n < 2 else bank[4 + s][:, 0:D]
                V.scalar_tensor_tensor(tile_of((q_sp, k_sp, v_sp)[n], t + (PAD if n == 2 else 0)), source,
                                       r[:, n:n + 1], thr[:, n * D:(n + 1) * D], ALU.mult, ALU.is_ge).then_inc(spiked, 1)

            def keep_dots(k, i):
                V.tensor_copy(tile_of(dots, k + 4 * i), bank[4 + k % 2][:, D:D + E + 1]).then_inc(dots_done, 1)

            def keep_qt(k, i):
                t = k + 4 * i
                dve.wait_ge(qt_done, t + 1)
                V.tensor_copy(q_t[:, :, bass.ds(t * P, P)],
                              bank[7][:, 0:P].bitcast(BF16).rearrange("p (c n) -> p c n", c=DC)).then_inc(qt_kept, 1)

            def step_a(k, i, ahead):
                if k < NT:
                    low_part(k, i)
                if ahead:
                    stats(k + 8, i, 0)
                if ahead:
                    stats(k + 8, i, 1)
                if 0 <= k - 2 < NT:
                    dve.wait_ge(rs_done, k - 1 + 4 * i)
                for n in range(3):
                    if 0 <= k - 2 < NT:
                        spikes(k - 2, i, n)
                    if ahead:
                        stats(k + 8, i, n + 2)
                if 0 <= k - 2 < NT:
                    keep_dots(k - 2, i)
                if 0 <= k - 3 < NT:
                    keep_qt(k - 3, i)

            for k in range(4):
                step_a(k, 0, True)
            with dve.Fori(0, NT // 4 - 3) as i:
                for k in range(4, 8):
                    step_a(k, i, True)
            for k in range(NT - 8, NT + 3):
                step_a(k, 0, False)

            dve.wait_ge(sums_done, NT)
            V.tensor_copy(sc16[:, :], bank[6][:, D:2 * D]).then_inc(m_done, 1)
            dve.wait_ge(sv_done, 1)
            step(V.tensor_copy(sv_row[:, :], bank[7][:, 0:D]))
            step(V.scalar_tensor_tensor(m_f[:, :], bank[6][:, 0:D], 2.0, sv_row[:, :], ALU.mult, ALU.subtract))
            step(V.tensor_tensor(m_f[:, :].rearrange("p (c n) -> p c n", c=DC),
                                 m_f[:, :].rearrange("p (c n) -> p c n", c=DC),
                                 head.unsqueeze(1).broadcast_to([P, DC, P]), ALU.mult))
            step(V.tensor_copy(m_hi[:, :], m_f[:, :]))
            V.tensor_tensor(m_lo[:, :], m_f[:, :], m_hi[:, :], ALU.subtract).then_inc(m_done, 1)
            scale = vc[:, SCALE_:SCALE_ + 1]
            dve.wait_ge(cvec_done, 1)
            step(V.tensor_scalar(thr2[:, :], bank[7][:, 0:DC], scale, 0.5, ALU.mult, ALU.mult))
            step(V.tensor_scalar(thr2[:, :], thr2[:, :], 0.5, None, ALU.add))

            over_e = lambda m: m.unsqueeze(2).broadcast_to([P, NT, E])
            over_t = lambda m: m.unsqueeze(1).broadcast_to([P, NT, E])
            A, B, HOT = ra[:, :, :], rb[:, :, :], hot[:, :, :]
            nx, rms = (m.rearrange("p t a -> p (t a)") for m in (dots[:, :, E:E + 1], inv_std[:, :, 1:2]))
            dve.wait_ge(dots_done, NT)
            dve.wait_ge(tables_made, 4)
            step(V.tensor_tensor(A, dots[:, :, 0:E], over_e(rms), ALU.mult))
            step(V.tensor_tensor(rt[:, 0, :], nx, rms, ALU.mult))
            step(V.tensor_tensor(rt[:, 0, :], rt[:, 0, :], rms, ALU.mult))
            step(V.scalar_tensor_tensor(A, A, -2.0, over_t(ny[:, :]), ALU.mult, ALU.add))
            step(V.tensor_tensor(A, A, over_e(rt[:, 0, :]), ALU.add))
            step(V.tensor_reduce(rt[:, 1, :], A, AX.X, ALU.min))
            step(V.tensor_tensor(B, A, over_e(rt[:, 1, :]), ALU.is_equal))
            step(V.scalar_tensor_tensor(B, B, -float(E), over_t(eidx[:, :]), ALU.mult, ALU.add))
            step(V.tensor_reduce(rt[:, 1, :], B, AX.X, ALU.min))
            step(V.tensor_scalar(rt[:, 1, :], rt[:, 1, :], float(E), None, ALU.add))
            step(V.tensor_tensor(HOT, over_t(eidx[:, :]), over_e(rt[:, 1, :]), ALU.is_equal))
            V.tensor_copy(hot16[:, :, :], HOT).then_inc(hot_done, 1)
            def attention_spikes(k, i):
                c, s = k + 2 * i, k % 2
                after(dve, wo_done, 2 * (c - 1))
                for h in range(DC):
                    dve.wait_ge(at_done, DC * c + h + 1)
                    V.tensor_scalar(a_sp[s][:, h, :], bank[h][:, :], scale, thr2[:, h:h + 1], ALU.mult,
                                    ALU.is_ge).then_inc(at_spiked, 1)

            attention_spikes(0, 0)
            dve.wait_ge(ranks_done, 1)
            step(V.tensor_copy(A, bank[6][:, NT * E:2 * NT * E].rearrange("p (t e) -> p t e", e=E)))
            for e in range(E):
                last = V.tensor_tensor_scan(rb[:, :, e], ones32[:, 0:NT], ra[:, :, e], 0.0, ALU.mult, ALU.add)
            step(last)
            step(V.tensor_tensor(A, B, A, ALU.subtract))
            step(V.tensor_copy(r8[:, 0, :], rb[:, NT - 1, :]))
            step(V.tensor_tensor(A, bank[6][:, 0:NT * E].rearrange("p (t e) -> p t e", e=E), A, ALU.add))
            by_e = rb[:, :, :].rearrange("p t e -> p (t e)").rearrange("p (e t) -> p e t", e=E)
            step(V.tensor_tensor(by_e, r8[:, 0, :].unsqueeze(2).broadcast_to([P, E, NT]),
                                 lev[:, :].unsqueeze(1).broadcast_to([P, E, NT]), ALU.is_gt))
            step(V.tensor_reduce(r8[:, 1, :], by_e, AX.X, ALU.add))
            step(V.tensor_tensor_scan(r8[:, 2, :], ones32[:, 0:E], r8[:, 1, :], 0.0, ALU.mult, ALU.add))
            step(V.tensor_tensor(r8[:, 3, :], r8[:, 2, :], r8[:, 1, :], ALU.subtract))
            step(V.tensor_scalar(r8[:, 3, :], r8[:, 3, :], float(P), None, ALU.mult))
            step(V.tensor_tensor(A, A, over_t(r8[:, 3, :]), ALU.add))
            step(V.tensor_tensor(A, A, HOT, ALU.mult))
            step(V.tensor_reduce(rt[:, 2, :], A, AX.X, ALU.add))
            V.tensor_copy(pos[:, :], rt[:, 2, :]).then_inc(pos_done, 1)
            step(V.tensor_tensor(tcmp[:, :, :], r8[0:1, 2, :].unsqueeze(1).broadcast_to([1, ST, E]),
                                 tile_no[0:1, :].unsqueeze(2).broadcast_to([1, ST, E]), ALU.is_le))
            step(V.tensor_reduce(tex[:, :], tcmp[:, :, :], AX.X, ALU.add))
            V.tensor_scalar(expert[:, :], tex[:, :], float(E - 1), None, ALU.min).then_inc(pos_done, 1)

            def output_spikes(k, i):
                c, s = k + 2 * i, k % 2
                if c >= 2:
                    dve.wait_ge(s_put[s], 16 * (c // 2))
                for pair in range(2):
                    dve.wait_ge(wo_rs, 2 * c + pair + 1)
                    for n in range(2):
                        tl = 2 * pair + n
                        V.scalar_tensor_tensor(s_out[s][:, tl, :], bank[2 + 2 * s + pair][:, n * D:(n + 1) * D],
                                               tile_of(rs, c * CH + tl)[:, 3:4], thr[:, 3 * D:4 * D],
                                               ALU.mult, ALU.is_ge).then_inc(s_made, 1)

            def low_parts(c):
                for e, half in SPLITS[c]:
                    if (e, half) not in BY_POOL:
                        dve.wait_ge(up_high, SPLIT_ORDER.index((e, half)) + 1)
                        V.tensor_tensor(up_lo[:, e, half, :], up_raw[:, e, half, :],
                                        up_hi[:, e, half, :].bitcast(F32), ALU.subtract).then_inc(up_split, 1)

            for c in range(1, NCH):
                attention_spikes(c % 2, c // 2)
                output_spikes((c - 1) % 2, (c - 1) // 2)
                if c in SPLITS:
                    low_parts(c)
            output_spikes((NCH - 1) % 2, NCH // 2 - 1)
            low_parts(NCH)

            def step_c(k, i):
                s, b = k + 4 * i, k % 2
                if k < ST:
                    dve.wait_ge(ext_high, s + 1)
                    after(dve, up_done, 2 * (s - 1))
                    for c in range(DC):
                        last = V.scalar_tensor_tensor(e_xl[b][:, c, :], bank[4][:, c * P:(c + 1) * P],
                                                      vc[:, FS_ + c:FS_ + c + 1], e_xh[b][:, c, :].bitcast(F32),
                                                      ALU.mult, ALU.subtract)
                    last.then_inc(ext_kept, 1)
                if 0 <= k - 2 < ST:
                    dve.wait_ge(down_done, s - 1)
                    after(dve, g_done, s - 3)
                    V.tensor_tensor(e_z[b][:, :], bank[b][:, 0:D], row_a[(k - 2) % 4][:, 0:D], ALU.add).then_inc(z_done, 1)
                if 0 <= k - 1 < ST:
                    dve.wait_ge(eht_done, s)
                    after(dve, down_done, s - 2)
                    V.tensor_copy(e_ht[1 - b][:, :, :], bank[5][:, :].rearrange("p (c n) -> p c n", c=HC)).then_inc(eht_kept, 1)
                if 0 <= k - 2 < ST:
                    dve.wait_ge(g_done, s - 1)
                    if k - 2 >= 4:
                        dve.wait_ge(sent[(k - 2) % 4], 16 * ((k - 2) // 4 + i))
                    dve.wait_ge(got_s[(k - 2) % 4], 16 * ((k - 2) // 4 + i + 1))
                    o = e_o[(k - 2) % 4]
                    V.tensor_tensor(o[:, :], e_g[b][:, :], row_s[(k - 2) % 4][:, :], ALU.mult).then_inc(sg_done, 1)
                    dve.wait_ge(sg_done, s - 1)
                    V.tensor_tensor(o[:, :], o[:, :], row_a[(k - 2) % 4][:, D + 1:2 * D + 1], ALU.add).then_inc(o_done, 1)
                if k < ST:
                    dve.wait_ge(gate_done, s + 1)
                    dve.wait_ge(up_done, 2 * s + 2)
                    after(dve, eht_done, s - 1)
                    V.scalar_tensor_tensor(e_act[b][:, :], bank[2][:, :], row_a[k % 4][:, D:D + 1], e_gate[b][:, :],
                                           ALU.mult, ALU.mult).then_inc(act_done, 1)

            for k in range(4):
                step_c(k, 0)
            with dve.Fori(0, (ST - 4) // 4) as i:
                for k in range(4, 8):
                    step_c(k, i)
            for k in range(ST // 4 * 4, ST + 2):
                step_c(k, 0)

        @block.gpsimd
        def _(pool):
            G = nc.gpsimd
            step = chain(pool, pool_n)

            def held(s, count):
                after(pool, s, count)
                pool.sem_inc(pool_passed, 1)

            G.iota(none[:, :], [[0, P]], base=N, channel_multiplier=0).then_inc(none_made, 1)
            G.memset(eps3[:, :], D * LN_EPS)
            step(G.memset(half_neg[:, :, :], -0.5))
            G.iota(ids[:, :], [[P, NT]], base=0, channel_multiplier=1).then_inc(tables_made, 1)
            G.iota(eidx[:, :], [[1, E]], base=E, channel_multiplier=0, allow_small_or_imprecise_dtypes=True).then_inc(tables_made, 1)
            G.iota(lev[:, :], [[P, NT]], base=0, channel_multiplier=0, allow_small_or_imprecise_dtypes=True).then_inc(tables_made, 1)
            G.iota(tile_no[:, :], [[1, ST]], base=0, channel_multiplier=0, allow_small_or_imprecise_dtypes=True).then_inc(tables_made, 1)
            pool.wait_ge(ld_c, 16 * 4)
            G.tensor_scalar(neg16[:, :], sum_rows[:, 0:2], -16.0, None, ALU.mult).then_inc(neg_made, 1)

            def inverse_stds(pair):
                held(stats_done, 2 * (pair + 1))
                two = bass.ds(2 * pair, 2)
                G.tensor_tensor(inv_std[:, two, :], var_in[:, two, :], half_neg[:, :, :], ALU.pow).then_inc(group_n, 1)
                held(group_n, pair + 1)
                G.tensor_tensor(nmr[:, two], inv_std[:, two, 0:1].rearrange("p a b -> p (a b)"), neg_mean[:, two],
                                ALU.mult).then_inc(rstd_done, 1)

            def put_rms(k, i):
                t = k + 4 * i
                held(xn_done, t + 1)
                G.tensor_copy(xn[k % 4][:, D:D + 1],
                              inv_std[:, bass.ds(t, 1), 1:2].rearrange("p a b -> p (a b)")).then_inc(rms_put, 1)

            def norms(k, i):
                t, s = k + 4 * i, k % 2
                held(squared, 3 * (t + 1))
                held(rs_done, t - 1)
                G.tensor_tensor(pv[:, s, 0:3], tile_of(ss, t)[:, 0:3], eps3[:, :], ALU.add).then_inc(norm_n, 1)
                held(norm_n, t + 1)
                G.tensor_tensor(tile_of(rs, t)[:, 0:3], pv[:, s, 0:3], half_neg[:, :, :].rearrange("p a b -> p (a b)")[:, 0:3], ALU.pow).then_inc(rs_done, 1)

            def step_a(k, i, ahead):
                if k >= 1:
                    norms(k - 1, i)
                if k < NT:
                    put_rms(k, i)
                if ahead and k % 2 == 1:
                    inverse_stds(k // 2 + 2 * i + 3)

            for pair in range(3):
                inverse_stds(pair)
            for k in range(4):
                step_a(k, 0, True)
            with pool.Fori(0, NT // 4 - 3) as i:
                for k in range(4, 8):
                    step_a(k, i, True)
            for k in range(NT - 8, NT + 1):
                step_a(k, 0, k < NT - 6)

            def number(c0, c1):
                for t in range(c0, c1):
                    G.indirect_dma_start(slots, bass.IndirectOffsetOnAxis(ap=pos[:, t:t + 1], axis=0),
                                         ids[:, t:t + 1], None, bounds_check=ST * P - 1,
                                         oob_is_err=False).then_inc(id_put, 16)

            def norms_out(k, i):
                c = k + 2 * i
                for pair in range(2):
                    of = lambda buffer: buffer[:, bass.ds(c * CH + 2 * pair, 2), 3:4].rearrange("p a b -> p (a b)")
                    held(wo_sq, CH * c + 2 * pair + 2)
                    held(wo_rs, 2 * c + pair - 1)
                    G.tensor_tensor(pv[:, pair, 0:2], of(ss), eps3[:, 0:2], ALU.add).then_inc(out_n, 1)
                    held(out_n, 2 * c + pair + 1)
                    G.tensor_tensor(of(rs), pv[:, pair, 0:2], half_neg[:, 0, :], ALU.pow).then_inc(wo_rs, 1)

            for k in range(4):
                pool.wait_ge(row_put[k], 16 * NT // 4)
            pool.wait_ge(xt_done, NT)
            for k in range(4):
                G.memset(row_a[k][:, :], 0.0)
                last = G.memset(row_s[k][:, :], 0.0)
            last.then_inc(rows_clear, 1)
            def gather_a(k, i):
                s = k + 4 * i
                held(o_done, s - 3)
                G.tensor_copy(from_id[k % 4][:, :], slot_id[:, bass.ds(s, 1)]).then_inc(from_n, 1)
                held(from_n, s + 1)
                G.indirect_dma_start(row_a[k % 4][:, :], None, rows_a,
                                     bass.IndirectOffsetOnAxis(ap=from_id[k % 4][:, :], axis=0),
                                     bounds_check=N - 1, oob_is_err=False).then_inc(got_a[k % 4], 16)

            def gather_s(k):
                G.indirect_dma_start(row_s[k % 4][:, :], None, rows_s,
                                     bass.IndirectOffsetOnAxis(ap=from_id[k % 4][:, :], axis=0),
                                     bounds_check=N - 1, oob_is_err=False).then_inc(got_s[k % 4], 16)

            def gather(k, i):
                gather_a(k, i)
                gather_s(k)

            pool.wait_ge(pos_done, 1)
            pool.wait_ge(none_put, 16)
            done = 0
            for c in range(NCH):
                if c < 5:
                    upto = min(NT, 4 + 8 * c)
                    number(done, upto)
                    done = upto
                if c == 6:
                    pool.wait_ge(ids_back, 16)
                    pool.wait_ge(x_copied, 16)
                    pool.wait_ge(rows_clear, 1)
                    for k in range(4):
                        gather_a(k, 0)
                norms_out(c % 2, c // 2)
            for e, half in BY_POOL:
                pool.wait_ge(up_high, SPLIT_ORDER.index((e, half)) + 1)
                G.tensor_tensor(up_lo[:, e, half, :], up_raw[:, e, half, :], up_hi[:, e, half, :].bitcast(F32),
                                ALU.subtract).then_inc(pool_split, 1)
            for k in range(2):
                pool.wait_ge(s_put[k], 16 * NCH // 2)
            for k in range(4):
                gather_s(k)

            def scatter(k, i):
                s = k + 4 * i
                if k >= 4:
                    held(sent[k % 4], 16 * (k // 4 + i))
                G.tensor_copy(to_id[k % 4][:, :], slot_id[:, bass.ds(s, 1)]).then_inc(to_n, 1)
                held(to_n, s + 1)
                held(o_done, s + 1)
                G.indirect_dma_start(out, bass.IndirectOffsetOnAxis(ap=to_id[k % 4][:, :], axis=0),
                                     e_o[k % 4][:, :], None, bounds_check=N - 1,
                                     oob_is_err=False).then_inc(sent[k % 4], 16)

            for k in range(4, 8):
                scatter(k - 4, 0)
                gather(k, 0)
            with pool.Fori(0, (ST - 11) // 4) as i:
                for k in range(8, 12):
                    scatter(k - 4, i)
                    gather(k, i)
            for k in range(36, ST):
                scatter(k - 4, 0)
                gather(k, 0)
            for k in range(ST - 4, ST):
                scatter(k, 0)
            for k in range(4):
                pool.wait_ge(sent[k], 16 * ((ST - k + 3) // 4))


_NAMES = {"x": "L0_attn_query", "wq": "L0_attn_Wq", "wk": "L0_attn_Wk", "wv": "L0_attn_Wv", "wo": "L0_attn_Wo",
          "centroids": "L0_ffn_centroids", "up_w": "L0_ffn_up_w", "down_w": "L0_ffn_down_w"}
_VECTORS = ["L0_attn_gq", "L0_attn_gk", "L0_attn_gv", "L0_attn_go", "L0_attn_bq", "L0_attn_bk", "L0_attn_bv",
            "L0_attn_bo", "L0_attn_betaq", "L0_attn_betak", "L0_attn_betav", "L0_attn_betao", "L0_ffn_scale"]


def _shape_constants():
    import numpy as np

    def bias(dist):
        n = dist + 1
        level = 12 - np.floor(np.log2(n)).astype(np.int64)
        return np.where(n >= N - 1, 0, level)

    a, b = np.arange(P)[None, :], np.arange(P)[:, None]
    col = np.arange(3 * P)[None, :]
    near = bias(np.abs(col - P - b))
    tri = np.stack([(a - b <= -2), (b - a <= -2)], 1).reshape(P, 2 * P)
    pick = np.zeros((P, 64, 4))
    pick[:, 31, 0] = 1
    pick[0, 31, 1] = 1
    pick[P - 1, 31, 2] = 1
    pick[1, 0, 3] = 1
    pick[P - 2, 62, 3] = 1
    scan = (b < a)
    head = (a // 16 == b // 16)
    sums = np.broadcast_to(b % 4 == 0, (P, P))
    consts = np.concatenate([near, tri, pick.reshape(P, 256), scan, head, sums], 1)

    blocks = np.zeros((4, 32, NT, P))
    for r in range(32):
        j = 31 - r
        for t in range(NT):
            k = abs(t - j)
            if k >= 2:
                blocks[0, r, t, :] = 12 - int(np.floor(np.log2(P * k)))
            if k >= 2 and (k + 1) & k == 0:
                if t > j:
                    blocks[1, r, t, P - 1] = -1
                else:
                    blocks[2, r, t, 0] = -1
    blocks[1, 31, NT - 1, P - 2] = -1
    blocks[3, 0, NT - 1, P - 1] = -1
    blocks[2, 0, 0, 1] = -1
    blocks[3, 31, 0, 0] = -1
    bits = lambda m: np.ascontiguousarray(np.ascontiguousarray(m, np.float32).view(np.uint16)[:, 1::2])
    return bits(consts), bits(blocks.transpose(1, 0, 2, 3).reshape(P, N)), np.eye(P, dtype=np.float32)


def kernel(**inputs):
    import numpy as _np
    import concourse.bacc as _bacc
    from concourse import mybir as _mybir
    from concourse.bass_utils import run_bass_kernel_spmd as _run

    nc = _bacc.Bacc("TRN2", target_bir_lowering=False, num_devices=1)
    arrays = {k: _np.ascontiguousarray(inputs[v]) for k, v in _NAMES.items()}
    arrays["x"] = arrays["x"].reshape(N, D)
    rows = [_np.asarray(inputs[n]).reshape(DC, P) for n in _VECTORS]
    rows.append(_np.broadcast_to(_np.asarray(inputs["L0_attn_scale"]).reshape(1, 1), (1, P)))
    arrays["vectors"] = _np.ascontiguousarray(_np.concatenate(rows, 0))
    arrays["consts"], arrays["blocks"], arrays["eye"] = _shape_constants()
    order = ["x", "wq", "wk", "wv", "wo", "vectors", "centroids", "up_w", "down_w", "consts", "blocks", "eye"]
    args = [nc.dram_tensor(f"in_{k}", arrays[k].shape, _mybir.dt.from_np(arrays[k].dtype), kind="ExternalInput").ap()
            for k in order]
    out = nc.dram_tensor("out_x", (N, D), F32, kind="ExternalOutput").ap()
    build(nc, *args, out)
    r = _run(nc, [{f"in_{k}": arrays[k] for k in order}], core_ids=[0])
    return r.results[0]["out_x"].reshape(1, N, D)
```

```python
from contextlib import ExitStack

import concourse.bass as bass
from concourse import mybir

ALU = mybir.AluOpType
ACT = mybir.ActivationFunctionType
AX = mybir.AxisListType
F32 = mybir.dt.float32
F32R = mybir.dt.float32r
BF16 = mybir.dt.bfloat16
I32 = mybir.dt.int32
U16 = mybir.dt.uint16

P = 128
N = 4096
D = 256
DC = D // P
NT = N // P
E = 8
HID = 512
HC = HID // P
ST = NT + E - 1
PAD = 16
CH = 4
CT = CH * P
NCH = NT // CH
YW = 3 * D + E
ROWA = 2 * D + 1
LN_EPS = 1e-5
RMS_EPS = 1e-6

G_, B_, BETA_, FS_, SCALE_ = 0, 8, 16, 24, 26
NV = 27

C_NEAR, C_TRI, C_PICK, C_SCAN, C_HEAD, C_SUM, C_END = 0, 384, 640, 896, 1024, 1152, 1280

SPLITS = {4: [(0, 0), (0, 1), (1, 0)], 5: [(1, 1), (5, 0)], 6: [(6, 0), (7, 0), (2, 0)],
          7: [(2, 1), (3, 0), (3, 1)], 8: [(4, 0), (4, 1), (5, 1)], 9: [(6, 1), (7, 1)]}
SPLIT_ORDER = [unit for c in sorted(SPLITS) for unit in SPLITS[c]]


def build(nc, x, wq, wk, wv, wo, vectors, centroids, up_w, down_w, consts, blocks, eye, out):
    with ExitStack() as ctx:
        sem = lambda name: ctx.enter_context(nc.semaphore(name))
        block_arena = [(nc.sbuf_base + 63) // 64 * 64]

        def place(name, shape, dt, at=None):
            size = 4 if dt in (F32, F32R, I32) else 2
            for n in shape[1:]:
                size *= n
            size = (size + 31) // 32 * 32
            if at is None:
                at = block_arena[0]
                block_arena[0] += size
            return nc.alloc_sbuf_tensor_at(name, shape, dt, offset=at), at

        up_raw, at_up = place("up_raw", [P, E, DC, 2 * HID], F32)
        up_lo, _ = place("up_lo", [P, E, DC, 2 * HID], F32R, at=at_up)
        down_sb, at_down = place("down_sb", [P, E, HC, D], F32)
        xs, _ = place("xs", [P, NT, D], F32, at=at_up)
        q_sp, _ = place("q_sp", [P, NT, D], BF16, at=at_up + 4 * NT * D)
        k_sp, _ = place("k_sp", [P, NT, D], BF16, at=at_up + 6 * NT * D)
        w_raw, _ = place("w_raw", [P, 4, DC, D], F32, at=at_down)
        w_cen, _ = place("w_cen", [P, DC, YW + D], F32, at=at_down + 12288)
        sgn_row, _ = place("sgn_row", [P, 4, D], F32, at=at_down + 26880)

        up_hi, at_hi = place("up_hi", [P, E, DC, 2 * HID], F32R)
        block_arena[0] = at_hi + 8 * DC * HID
        assert (PAD * 2 * D, at_hi % 64) == (8 * DC * HID, 0)
        v_sp, at_v = place("v_sp", [P, PAD + NT + PAD, D], BF16)
        q_t, at_q = place("q_t", [P, DC, N], BF16)
        blk_tab, at_blk = place("blk_tab", [P, N], BF16)
        assert at_blk + 2 * N == at_hi + E * 8 * DC * HID
        w_hi, at_w = place("w_hi", [P, DC, YW], F32R)
        w_lo, at_w2 = place("w_lo", [P, DC, YW], F32R)
        a_sp = [place(f"a_sp{k}", [P, DC, CT], F32R, at=at_w + 4096 * k)[0] for k in range(2)]
        s_out = [place(f"s_out{k}", [P, CH, D], BF16, at=at_w + 8192 + 2048 * k)[0] for k in range(2)]
        assert at_w2 + 4 * DC * YW - at_w >= 12288
        wo_hi, _ = place("wo_hi", [P, DC, D], F32R)
        wo_lo, _ = place("wo_lo", [P, DC, D], F32R)
        thr, _ = place("thr", [P, 4 * D], F32)
        b_row, _ = place("b_row", [P, 4 * D], BF16)
        b_pick, _ = place("b_pick", [P, P], BF16)
        at_xh = [at_hi, at_hi + 1024]
        at_xl = [at_hi + 2048, at_hi + 3072]
        x_hi = [place(f"x_hi{k}", [P, DC, P], F32R, at=at_xh[k])[0] for k in range(2)]
        x_lo = [place(f"x_lo{k}", [P, DC, P], F32R, at=at_xl[k])[0] for k in range(2)]
        junk = [place(f"junk{k}", [P, D], BF16)[0] for k in range(4)]
        sq, at_sq = zip(*[place(f"sq{k}", [P, D], F32) for k in range(2)])
        fs_row, _ = place("fs_row", [P, D], F32)
        cst, _ = place("cst", [P, C_END], BF16)
        ident16, _ = place("ident16", [P, P], BF16)
        ones16, _ = place("ones16", [P, P], BF16)
        at_w_end = block_arena[0]

        xn, at_xn = zip(*[place(f"xn{k}", [P, D + 2], F32) for k in range(4)])

        ident, _ = place("ident", [P, P], F32)
        mean_w, _ = place("mean_w", [P, P], F32, at=at_hi + 4096)
        ones32, _ = place("ones32", [P, P], F32)
        zeros16, _ = place("zeros16", [P, CT], BF16, at=at_q)
        vec_raw, _ = place("vec_raw", [NV, P], F32, at=at_q + 1024)
        vc, _ = place("vc", [P, NV], F32)
        cen_raw, _ = place("cen_raw", [E, D], F32, at=at_q + 2048)
        small, _ = place("small", [P, 128], F32)
        b16, _ = place("b16", [P, 24], BF16)
        eps3, _ = place("eps3", [P, 3], F32)
        half_neg, _ = place("half_neg", [P, 2, 2], F32)
        st6, _ = place("st6", [P, 4, 6], F32)
        mv2, _ = place("mv2", [P, 4, 2], F32)
        neg_mean, _ = place("neg_mean", [P, NT], F32)
        inv_var, _ = place("inv_var", [P, NT], F32)
        var_in, _ = place("var_in", [P, NT, 2], F32)
        inv_std, _ = place("inv_std", [P, NT, 2], F32)
        pv, _ = place("pv", [P, 2, 4], F32)
        nmr, _ = place("nmr", [P, NT], F32)
        ss, _ = place("ss", [P, NT, 4], F32)
        rs, _ = place("rs", [P, NT, 4], F32)
        ny, _ = place("ny", [P, E], F32)
        dots, _ = place("dots", [P, NT, E + 1], F32, at=at_hi + 6912)
        ra, _ = place("ra", [P, NT, E], F32, at=at_xh[0])
        rb, _ = place("rb", [P, NT, E], F32, at=at_xh[1])
        hot, _ = place("hot", [P, NT, E], F32, at=at_xl[0])
        hot16, _ = place("hot16", [P, NT, E], BF16, at=at_hi + 4608)
        eidx, _ = place("eidx", [P, E], F32)
        lev, _ = place("lev", [P, NT], F32)
        rt, _ = place("rt", [P, 4, NT], F32)
        r8, _ = place("r8", [P, 6, E], F32)
        pos, _ = place("pos", [P, NT], I32)
        ids, _ = place("ids", [P, NT], I32)
        tile_no, _ = place("tile_no", [P, ST], F32)
        tcmp, _ = place("tcmp", [1, ST, E], F32, at=at_hi + 5632)
        tex, _ = place("tex", [1, ST], F32)
        expert, _ = place("expert", [1, ST], I32)
        none, _ = place("none", [ST, P], I32, at=at_hi + 5120)
        slot_id, _ = place("slot_id", [P, ST], I32)
        from_id = [place(f"from_id{k}", [P, 1], I32)[0] for k in range(4)]
        to_id = [place(f"to_id{k}", [P, 1], I32)[0] for k in range(4)]
        from_n, to_n = sem("from_n"), sem("to_n")
        pool_passed, dve_passed = sem("pool_passed"), sem("dve_passed")
        sc16, _ = place("sc16", [P, D], BF16)
        sv_row, _ = place("sv_row", [P, D], F32, at=at_sq[0])
        m_f, _ = place("m_f", [P, D], F32, at=at_xl[1])
        m_hi, _ = place("m_hi", [P, D], BF16, at=at_sq[1])
        m_lo, _ = place("m_lo", [P, D], BF16, at=at_sq[1] + 2 * D)
        neg16, _ = place("neg16", [P, 2], BF16)
        thr2, _ = place("thr2", [P, 2], F32)

        row_a = [place(f"row_a{k}", [P, ROWA], F32, at=at_xn[2 * k] if k < 2 else None)[0] for k in range(4)]
        row_s = [place(f"row_s{k}", [P, D], BF16)[0] for k in range(4)]
        over = [at_w]

        def over_weights(name, n, shape, dt=F32):
            made = []
            for k in range(n):
                made.append(place(f"{name}{k}", shape, dt, at=over[0])[0])
                over[0] += 4 * shape[1] * (shape[2] if len(shape) > 2 else 1)
            return made

        e_xh, e_xl = over_weights("e_xh", 2, [P, DC, P], F32R), over_weights("e_xl", 2, [P, DC, P], F32R)
        e_hh = over_weights("e_hh", 2, [P, HC, P], F32R)
        e_o = over_weights("e_o", 4, [P, D])
        e_hl = over_weights("e_hl", 2, [P, HC, P], F32R)
        e_h, e_z = over_weights("e_h", 2, [P, HID]), over_weights("e_z", 2, [P, D])
        (d_hi,), (d_lo,) = over_weights("d_hi", 1, [P, HC, D], F32R), over_weights("d_lo", 1, [P, HC, D], F32R)
        assert over[0] <= at_w_end, (over[0], at_w_end)
        assert block_arena[0] <= nc.sbuf_usable_end, (block_arena[0], nc.sbuf_usable_end)

        bank = [ctx.enter_context(nc.psum_tensor(f"bank{k}", [P, 512], F32)) for k in range(8)]
        rows_a = nc.dram_tensor("rows_a", (N, ROWA), F32, kind="Internal").ap()
        rows_s = nc.dram_tensor("rows_s", (N, D), BF16, kind="Internal").ap()
        slots = nc.dram_tensor("slots", (ST * P, 1), I32, kind="Internal").ap()

        near = cst[:, C_NEAR:C_TRI]
        tri = cst[:, C_TRI:C_PICK].rearrange("p (a b) -> p a b", a=2)
        pick = cst[:, C_PICK:C_SCAN]
        scan_tri = cst[:, C_SCAN:C_HEAD]
        head = cst[:, C_HEAD:C_SUM]
        sum_rows = cst[:, C_SUM:C_END]

        ld_w = [sem(f"ld_w{p}") for p in range(4)]
        ld_c, ld_t, ld_b, x_loaded = sem("ld_c"), sem("ld_t"), sem("ld_b"), sem("x_loaded")
        x_copied, up_loaded, down_loaded = sem("x_copied"), sem("up_loaded"), sem("down_loaded")
        consts_set = sem("consts_set")
        vec_turned, w_turned, vec_kept, bias_mean = sem("vec_turned"), sem("w_turned"), sem("vec_kept"), sem("bias_mean")
        cols_made, rows_made, w_centred, w_high = sem("cols_made"), sem("rows_made"), sem("w_centred"), sem("w_high")
        sgn_kept, thr_kept, b_kept, cen_summed = sem("sgn_kept"), sem("thr_kept"), sem("b_kept"), sem("cen_summed")
        pads_cleared, ny_kept = sem("pads_cleared"), sem("ny_kept")
        sgn, lim = small[:, 0:8], small[:, 24:32]
        setup_done, none_made, tables_made = sem("setup_done"), sem("none_made"), sem("tables_made")
        dve_n, pool_n = sem("dve_n"), sem("pool_n")
        group_n, aggr_done, norm_n, sq_done = sem("group_n"), sem("aggr_done"), sem("norm_n"), sem("sq_done")
        out_n, neg_made, rows_clear = sem("out_n"), sem("neg_made"), sem("rows_clear")
        stats_done, rstd_done, xn_done, rms_put = sem("stats_done"), sem("rstd_done"), sem("xn_done"), sem("rms_put")
        xt_done, hi_done, lo_done = sem("xt_done"), sem("hi_done"), sem("lo_done")
        row_put = [sem(f"row_put{k}") for k in range(4)]
        qk_done, v_done, squared, rs_done = sem("qk_done"), sem("v_done"), sem("squared"), sem("rs_done")
        spiked, dots_done, var_n, st_n = sem("spiked"), sem("dots_done"), sem("var_n"), sem("st_n")
        inv_n, nx_done, table_read = sem("inv_n"), sem("nx_done"), sem("table_read")
        sums_done, qt_done, qt_kept = sem("sums_done"), sem("qt_done"), sem("qt_kept")
        hot_done, ranks_done, pos_done, none_put, id_put, ids_back = (
            sem("hot_done"), sem("ranks_done"), sem("pos_done"), sem("none_put"), sem("id_put"), sem("ids_back"))
        m_done, cvec_done, sv_done = sem("m_done"), sem("cvec_done"), sem("sv_done")
        at_done, at_spiked, wo_done, wo_sq, wo_rs, s_made = (sem("at_done"), sem("at_spiked"), sem("wo_done"),
                                                            sem("wo_sq"), sem("wo_rs"), sem("s_made"))
        s_put = [sem(f"s_put{k}") for k in range(2)]
        got_a, got_s = ([sem(f"{name}{k}") for k in range(4)] for name in ("got_a", "got_s"))
        sent = [sem(f"sent{k}") for k in range(4)]
        ext_done, ext_kept, up_done, gate_done, act_done = (sem("ext_done"), sem("ext_kept"), sem("up_done"),
                                                          sem("gate_done"), sem("act_done"))
        up_high, up_ready, ext_high = sem("up_high"), sem("up_ready"), sem("ext_high")
        hid_high, d_high, d_low = sem("hid_high"), sem("d_high"), sem("d_low")
        eht_done, eht_kept, down_done, z_done, g_done, sg_done, o_done = (
            sem("eht_done"), sem("eht_kept"), sem("down_done"), sem("z_done"), sem("g_done"), sem("sg_done"), sem("o_done"))

        def after(eng, s, count):
            if not isinstance(count, int) or count > 0:
                eng.wait_ge(s, count)

        def tile_of(buffer, t):
            return buffer[:, bass.ds(t, 1), :].rearrange("p a n -> p (a n)")

        def chain(eng, s):
            count = [0]

            def step(ins):
                count[0] += 1
                ins.then_inc(s, 1)
                eng.wait_ge(s, count[0])
            return step

        block = ctx.enter_context(nc.Block())

        @block.sync
        def _(sp):
            for p, w in enumerate((wq, wk, wv, wo)):
                sp.dma_start(w_raw[:, p, :, :], w.rearrange("(c p) n -> p c n", p=P)).then_inc(ld_w[p], 16)
            for g in range(NT // 4):
                if g:
                    sp.wait_ge(x_loaded, 16 * g)
                sp.dma_start(xs[:, 4 * g:4 * g + 4, :],
                             x[512 * g:512 * g + 512, :].rearrange("(t p) n -> p t n", p=P)).then_inc(x_loaded, 16)
            sp.wait_ge(none_made, 1)
            sp.dma_start(slots.rearrange("(s p) a -> s (p a)", p=P), none[:, :]).then_inc(none_put, 16)
            sp.wait_ge(setup_done, 1)
            sp.wait_ge(b_kept, 1)
            for t in range(NT):
                sp.wait_ge(rms_put, t + 1)
                sp.dma_start(rows_a[t * P:(t + 1) * P, 0:D + 1], xn[t % 4][:, 0:D + 1]).then_inc(row_put[t % 4], 16)
                if t == NT // 2:
                    sp.dma_start(blk_tab[:, :].bitcast(U16), blocks).then_inc(ld_b, 16)
                if t % 4 == 2:
                    rows = slice((t - 2) * P, (t + 2) * P)
                    sp.dma_start(rows_a[rows, D + 1:2 * D + 1], x[rows, :]).then_inc(x_copied, 16)
                if t % 4 == 0:
                    e = t // 4
                    sp.dma_start(down_sb[:, e, :, :], down_w[e].rearrange("(c p) n -> p c n", p=P)) \
                        .then_inc(down_loaded, 16)
            sp.wait_ge(xn_done, NT)
            sp.wait_ge(stats_done, NT)
            sp.wait_ge(sums_done, NT)
            sp.wait_ge(qt_done, NT)
            for e in range(E):
                sp.dma_start(up_raw[:, e, :, :], up_w[e].rearrange("(c p) n -> p c n", p=P)).then_inc(up_loaded, 16)
            for c in range(NCH):
                if c == 5:
                    sp.wait_ge(id_put, 16 * NT)
                    sp.dma_start(slot_id[:, :], slots.rearrange("(s p) a -> p (s a)", p=P),
                                 allow_slow_non_contiguous=True).then_inc(ids_back, 16)
                sp.wait_ge(s_made, CH * (c + 1))
                sp.dma_start(rows_s[c * CT:(c + 1) * CT, :].rearrange("(t p) n -> p t n", p=P),
                             s_out[c % 2][:, :, :]).then_inc(s_put[c % 2], 16)

        @block.tensor
        def _(pe):
            pe.wait_ge(consts_set, 5)
            pe.wait_ge(ld_c, 16 * 3)
            pe.transpose(bank[4][0:P, 0:NV], vec_raw[:, :], ident[0:NV, 0:NV])
            for c in range(DC):
                last = pe.transpose(bank[4][:, 64 + E * c:64 + E * c + E], cen_raw[:, c * P:(c + 1) * P],
                                    ident[0:E, 0:E])
            last.then_inc(vec_turned, 1)
            pe.wait_ge(vec_kept, 1)
            pe.matmul(bank[5][:, 0:8], mean_w[:, :], vc[:, B_:B_ + 8], start=True, stop=True).then_inc(bias_mean, 1)
            for p in range(4):
                pe.wait_ge(ld_w[p], 16)
                for ic in range(DC):
                    for oc in range(DC):
                        last = pe.transpose(bank[p][:, ic * D + oc * P:ic * D + (oc + 1) * P],
                                            w_raw[:, p, oc, ic * P:(ic + 1) * P], ident[:, :])
                last.then_inc(w_turned, 1)

            def rows_from(cols, where):
                for n in range(8):
                    last = pe.matmul(bank[where + n // 4][:, n % 4 * P:(n % 4 + 1) * P],
                                     cols[:, n:n + 1].broadcast_to([P, P]), ident[:, :], start=True, stop=True)
                last.then_inc(rows_made, 1)

            pe.wait_ge(cols_made, 1)
            rows_from(sgn, 6)
            pe.wait_ge(cols_made, 2)
            rows_from(lim, 4)
            pe.wait_ge(sgn_kept, 1)
            for c in range(DC):
                pe.matmul(bank[7][:, c * P:(c + 1) * P], vc[:, FS_ + c:FS_ + c + 1].broadcast_to([P, P]),
                          ident[:, :], start=True, stop=True)
            for c in range(DC):
                last = pe.matmul(bank[7][:, D:D + E], ones32[:, :], small[:, 64 + E * c:64 + E * c + E],
                                 start=(c == 0), stop=(c == DC - 1))
            last.then_inc(cen_summed, 1)
            pe.matmul(bank[6][:, :], zeros16[:, 0:P], zeros16[:, :], start=True, stop=True)
            pe.wait_ge(cols_made, 3)
            pe.wait_ge(thr_kept, 1)
            for n in range(8):
                for part in range(3):
                    last = pe.matmul(bank[4 + n // 4][32 * part:32 * part + 32, n % 4 * P:(n % 4 + 1) * P],
                                     b16[:, 8 * part + n:8 * part + n + 1].broadcast_to([P, 32]), ident16[:, :],
                                     start=True, stop=True)
            last.then_inc(rows_made, 1)
            pe.wait_ge(w_centred, 1)
            pe.wait_ge(ny_kept, 2)
            pe.wait_ge(ld_t, 16)

            def transpose_x(k, i):
                t, s = k + 4 * i, k % 2
                pe.wait_ge(xn_done, t + 1)
                for c in range(DC):
                    last = pe.transpose(bank[s][:, c * P:(c + 1) * P], xn[k % 4][:, c * P:(c + 1) * P], ident[:, :])
                last.then_inc(xt_done, 1)

            def project(k, i):
                t, s = k + 4 * i, k % 2
                if k == 0:
                    pe.wait_ge(setup_done, 1)
                    pe.wait_ge(b_kept, 1)
                pe.wait_ge(lo_done, t + 1)
                for b, c0, c1, done in ((2 + s, 0, 2 * D, qk_done), (4 + s, 2 * D, YW, v_done)):
                    if done is qk_done:
                        after(pe, spiked, 3 * (t - 1) - 1)
                    else:
                        after(pe, dots_done, t - 1)
                    first = True
                    for left, right in ((x_hi, w_hi), (x_hi, w_lo), (x_lo, w_hi)):
                        for c in range(DC):
                            pe.matmul(bank[b][:, 0:c1 - c0], left[s][:, c, :], right[:, c, c0:c1],
                                      start=first, stop=False)
                            first = False
                    cb = min(c1, 3 * D)
                    pe.matmul(bank[b][:, 0:cb - c0], b_pick[0:96, :], b_row[0:96, c0:cb],
                              start=False, stop=True).then_inc(done, 1)

            def accumulate(k, i):
                t = k + 4 * i
                pe.wait_ge(spiked, 3 * (t + 1))
                after(pe, qt_kept, t)
                for c in range(DC):
                    last = pe.transpose(bank[7][:, 64 * c:64 * c + 64].bitcast(BF16),
                                        tile_of(q_sp, t)[:, c * P:(c + 1) * P], ident16[:, :])
                last.then_inc(qt_done, 1)
                for c in range(DC):
                    pe.matmul(bank[6][:, c * P:(c + 1) * P], tile_of(k_sp, t)[:, c * P:(c + 1) * P],
                              tile_of(v_sp, t + PAD)[:, c * P:(c + 1) * P], start=False, stop=False,
                              skip_group_check=True)
                pe.matmul(bank[6][:, D:2 * D], pick[:, bass.ds(4 * t, P)], tile_of(v_sp, t + PAD),
                          start=False, stop=False, skip_group_check=True).then_inc(sums_done, 1)

            def step_a(k, i):
                if k < NT:
                    transpose_x(k, i)
                if 0 <= k - 1 < NT:
                    project(k - 1, i)
                if 0 <= k - 3 < NT:
                    accumulate(k - 3, i)

            for k in range(4):
                step_a(k, 0)
            with pe.Fori(0, NT // 4 - 1) as i:
                for k in range(4, 8):
                    step_a(k, i)
            for k in range(NT, NT + 3):
                step_a(k, 0)

            pe.wait_ge(pads_cleared, 1)

            def attend_near(k, i, h):
                c, ps, hs = k + 2 * i, bank[h], slice(h * P, (h + 1) * P)
                after(pe, at_spiked, DC * (c - 1) + h + 1)
                for b in range(CH):
                    for n, d in enumerate((2, 4, 8, 16)):
                        for side in range(2):
                            at = PAD + b + (d if side else -d)
                            pe.matmul(ps[:, b * P:(b + 1) * P], tile_of(v_sp, CH * c + at)[:, hs],
                                      tri[:, side, :], start=(b == 0 and n == 0 and side == 0), stop=False)
                for j in range(-1, CH + 1):
                    a, b = max(0, j - 1), min(CH, j + 2)
                    pe.matmul(ps[:, a * P:b * P], tile_of(v_sp, CH * c + (PAD + j))[:, hs],
                              near[:, (a - j + 1) * P:(b - j + 1) * P], start=False, stop=False)

            def attend_sums(k, i, h):
                c, ps, hs = k + 2 * i, bank[h], slice(h * P, (h + 1) * P)
                pe.matmul(ps[:, :], sc16[:, hs], blk_tab[:, bass.ds(c * CT, CT)], start=False, stop=False)
                for part in (m_hi, m_lo):
                    last = pe.matmul(ps[:, :], part[:, hs], q_t[:, h, bass.ds(c * CT, CT)], start=False,
                                     stop=(part is m_lo))
                last.then_inc(at_done, 1)

            def attend(k, i):
                for h in range(DC):
                    attend_near(k, i, h)
                    attend_sums(k, i, h)

            def project_out(k, i):
                c, s = k + 2 * i, k % 2
                pe.wait_ge(at_spiked, DC * (c + 1))
                for pair in range(2):
                    ps = bank[2 + 2 * s + pair]
                    after(pe, s_made, CH * (c - 2) + 2 * pair + 2)
                    for n in range(2):
                        tl = 2 * pair + n
                        o = ps[:, n * D:(n + 1) * D]
                        for m, w in enumerate((wo_hi, wo_lo)):
                            for h in range(DC):
                                pe.matmul(o, a_sp[s][:, h, tl * P:(tl + 1) * P], w[:, h, :],
                                          start=(m == 0 and h == 0), stop=False)
                        last = pe.matmul(o, b_pick[0:96, :], b_row[0:96, 3 * D:4 * D], start=False, stop=True)
                    last.then_inc(wo_done, 1)

            pe.wait_ge(m_done, 1)
            pe.wait_ge(qt_kept, NT)
            pe.matmul(bank[7][:, 0:D], sum_rows, sc16[:, :], start=True, stop=True).then_inc(sv_done, 1)
            for h in range(DC):
                attend_near(0, 0, h)
            pe.wait_ge(m_done, 2)
            pe.wait_ge(neg_made, 1)
            for c in range(DC):
                cs = slice(c * P, (c + 1) * P)
                pe.matmul(bank[7][:, c:c + 1], m_hi[:, cs], ones16[:, 0:1], start=True, stop=False)
                pe.matmul(bank[7][:, c:c + 1], m_lo[:, cs], ones16[:, 0:1], start=False, stop=False)
                last = pe.matmul(bank[7][:, c:c + 1], sc16[:, cs], neg16[:, 0:1], start=False, stop=True)
            last.then_inc(cvec_done, 1)
            pe.wait_ge(ld_b, 16)
            for h in range(DC):
                attend_sums(0, 0, h)
            pe.wait_ge(hot_done, 1)
            pe.matmul(bank[6][:, 0:NT * E], scan_tri, hot16[:, :, :], start=True, stop=True)
            pe.matmul(bank[6][:, NT * E:2 * NT * E], ones16[:, :], hot16[:, :, :], start=True, stop=True) \
                .then_inc(ranks_done, 1)
            for k in range(1, 4):
                attend(k, 0)
                project_out(k - 1, 0)
            with pe.Fori(0, NCH // 2 - 2) as i:
                for k in range(4, 6):
                    attend(k, i)
                    project_out(k - 1, i)
            project_out(NCH - 1, 0)

            def turn_rows(k, i):
                s = k + 4 * i
                pe.wait_ge(got_a[k % 4], 16 * (k // 4 + i + 1))
                after(pe, ext_kept, s)
                for c in range(DC):
                    last = pe.transpose(bank[7][:, c * P:(c + 1) * P], row_a[k % 4][:, c * P:(c + 1) * P], ident[:, :])
                last.then_inc(ext_done, 1)

            def turn_hidden(k, i):
                s = k + 4 * i
                if k == 0:
                    pe.wait_ge(s_made, NT)
                pe.wait_ge(act_done, s + 1)
                after(pe, eht_kept, s)
                for c in range(HC):
                    last = pe.transpose(bank[5][:, c * P:(c + 1) * P], e_h[k % 2][:, c * P:(c + 1) * P], ident[:, :])
                last.then_inc(eht_done, 1)

            def expert_up(k, i, e):
                s = k + 4 * i
                if k == 0:
                    pe.wait_ge(s_made, NT - CH)
                pe.wait_ge(up_ready, e + 1)
                pe.wait_ge(ext_high, s + 1)
                after(pe, act_done, s)
                hi, lo = (w[:, bass.ds(e, 1), :, :].rearrange("p a c n -> p (a c) n") for w in (up_hi, up_lo))
                for half in (1, 0):
                    for n, (left, w) in enumerate(((e_xh, hi), (e_xh, lo), (e_xl, hi))):
                        if half == 1 and n == 2:
                            pe.wait_ge(ext_kept, s + 1)
                        for c in range(DC):
                            last = pe.matmul(bank[2 + half][:, :], left[k % 2][:, c, :],
                                             w[:, c, half * HID:(half + 1) * HID],
                                             start=(n == 0 and c == 0), stop=(n == 2 and c == DC - 1))
                    last.then_inc(up_done, 1)

            def expert_down(k, i):
                s = k + 4 * i
                after(pe, z_done, s - 1)
                for n, (left, w) in enumerate(((e_hh, d_hi), (e_hl, d_hi), (e_hh, d_lo))):
                    if n == 0:
                        pe.wait_ge(d_high, s + 1)
                        pe.wait_ge(hid_high, s + 1)
                    else:
                        pe.wait_ge((eht_kept, d_low)[n - 1], s + 1)
                    for c in range(HC):
                        last = pe.matmul(bank[k % 2][:, 0:D], left[k % 2][:, c, :], w[:, c, :],
                                         start=(n == 0 and c == 0), stop=(n == 2 and c == HC - 1))
                last.then_inc(down_done, 1)

            def step_c(k, i):
                if k < ST:
                    e = pe.value_load(expert[0:1, bass.ds(k + 4 * i, 1)], min_val=0, max_val=E - 1)
                    turn_rows(k, i)
                if 0 <= k - 2 < ST:
                    expert_down(k - 2, i)
                if 0 <= k - 1 < ST:
                    turn_hidden(k - 1, i)
                if k < ST:
                    expert_up(k, i, e)

            pe.wait_ge(pos_done, 2)
            for k in range(4):
                step_c(k, 0)
            with pe.Fori(0, (ST - 4) // 4) as i:
                for k in range(4, 8):
                    step_c(k, i)
            for k in range(ST // 4 * 4, ST + 2):
                step_c(k, 0)

        @block.scalar
        def _(act):
            act.dma_start(ident[:, :], eye).then_inc(ld_c, 16)
            act.dma_start(vec_raw[:, :], vectors).then_inc(ld_c, 16)
            act.dma_start(cen_raw[:, :], centroids).then_inc(ld_c, 16)
            act.dma_start(cst[:, :].bitcast(U16), consts).then_inc(ld_t, 16)
            act.wait_ge(consts_set, 5)
            act.activation(junk[0][:, 0:1], ones16[:, 0:1], ACT.Silu).then_inc(table_read, 1)
            def normalize(k, i):
                t = k + 4 * i
                act.wait_ge(rstd_done, k // 2 + 2 * i + 1)
                act.wait_ge(x_loaded, 16 * (k // 4 + i + 1))
                if k >= 4:
                    act.wait_ge(xt_done, t - 3)
                    act.wait_ge(sq_done, t - 3)
                    act.wait_ge(row_put[k % 4], 16 * (k // 4 + i))
                act.activation(xn[k % 4][:, 0:D], tile_of(xs, t), ACT.Identity, bias=nmr[:, bass.ds(t, 1)],
                               scale=inv_std[:, bass.ds(t, 1), 0:1].rearrange("p a b -> p (a b)")).then_inc(xn_done, 1)

            act.wait_ge(rows_made, 1)
            for h in range(2):
                last = act.activation(sgn_row[:, 2 * h:2 * h + 2, :].rearrange("p a n -> p (a n)"), bank[6 + h][:, :],
                                      ACT.Copy)
            last.then_inc(sgn_kept, 1)
            act.wait_ge(rows_made, 2)
            for h in range(2):
                last = act.activation(thr[:, 512 * h:512 * h + 512], bank[4 + h][:, :], ACT.Copy)
            last.then_inc(thr_kept, 1)
            normalize(0, 0)
            act.wait_ge(w_centred, 1)
            act.activation(w_hi[:, :, :], w_cen[:, :, 0:YW], ACT.Copy).then_inc(w_high, 1)
            act.activation(wo_hi[:, :, :], w_cen[:, :, YW:YW + D], ACT.Copy).then_inc(w_high, 1)
            act.wait_ge(rows_made, 3)
            for h in range(2):
                last = act.activation(b_row[0:96, 512 * h:512 * h + 512], bank[4 + h][0:96, :], ACT.Copy)
            last.then_inc(b_kept, 1)

            def step_a(k, i):
                t, s = k + 4 * i, k % 2
                if k < NT:
                    act.wait_ge(xt_done, t + 1)
                    act.activation(x_hi[s][:, :, :], bank[s][:, 0:D].rearrange("p (c n) -> p c n", c=DC),
                                   ACT.Copy).then_inc(hi_done, 1)
                if k + 1 < NT:
                    normalize(k + 1, i)
                if k >= 1:
                    u, su = t - 1, (k - 1) % 2
                    act.wait_ge(qk_done, u + 1)
                    if k == 1:
                        act.wait_ge(table_read, 1)
                    for n in range(3):
                        if n == 2:
                            act.wait_ge(v_done, u + 1)
                        after(act, squared, 3 * (u - 1) + n + 1)
                        src = bank[2 + su][:, n * D:(n + 1) * D] if n < 2 else bank[4 + su][:, 0:D]
                        act.activation(junk[n][:, :], src, ACT.Square,
                                       accum_out=tile_of(ss, u)[:, n:n + 1]).then_inc(squared, 1)
                    act.wait_ge(sq_done, u + 1)
                    after(act, nx_done, u)
                    act.activation(junk[3][:, :], sq[su][:, :], ACT.Square,
                                   accum_out=tile_of(dots, u)[:, E:E + 1]).then_inc(nx_done, 1)

            for k in range(4):
                step_a(k, 0)
            with act.Fori(0, NT // 4 - 2) as i:
                for k in range(4, 8):
                    step_a(k, i)
            for k in range(NT - 4, NT + 1):
                step_a(k, 0)

            def squares_out(k, i):
                c, s = k + 2 * i, k % 2
                for pair in range(2):
                    act.wait_ge(wo_done, 2 * c + pair + 1)
                    for n in range(2):
                        m = 2 * pair + n
                        after(act, wo_sq, CH * (c - 1) + m + 1)
                        act.activation(junk[m][:, :], bank[2 + 2 * s + pair][:, n * D:(n + 1) * D], ACT.Square,
                                       accum_out=ss_out(c, m)).then_inc(wo_sq, 1)

            def ss_out(c, n):
                return ss[:, bass.ds(c * CH + n, 1), 3:4].rearrange("p a b -> p (a b)")

            def high_parts(c):
                for e, half in SPLITS[c]:
                    act.activation(up_hi[:, e, half, :], up_raw[:, e, half, :], ACT.Copy,
                                   scale=vc[:, FS_ + half:FS_ + half + 1]).then_inc(up_high, 1)

            for c in range(NCH):
                if c == NCH - 2:
                    act.wait_ge(at_done, DC * NCH)
                    high_parts(c + 1)
                squares_out(c % 2, c // 2)
                if c == 3:
                    act.wait_ge(up_loaded, 16 * E)
                    act.wait_ge(pos_done, 2)
                    act.wait_ge(none_put, 16)
                if 3 <= c < NCH - 2:
                    act.wait_ge(at_done, DC * (c + 1))
                    high_parts(c + 1)
                if c == NCH - 2:
                    high_parts(c + 2)

            def turned_high(k, i):
                s = k + 4 * i
                act.wait_ge(ext_done, s + 1)
                after(act, up_done, 2 * (s - 1))
                act.activation(e_xh[k % 2][:, :, :], bank[7][:, 0:D].rearrange("p (c n) -> p c n", c=DC),
                               ACT.Copy).then_inc(ext_high, 1)

            turned_high(0, 0)
            high_parts(NCH + 1)

            def step_c(k, i):
                s, b = k + 4 * i, k % 2
                if 0 < k < ST:
                    turned_high(k, i)
                if 0 <= k - 1 < ST:
                    e = act.value_load(expert[0:1, bass.ds(s - 1, 1)], min_val=0, max_val=E - 1)
                if 0 <= k - 1 < ST:
                    after(act, down_done, s - 1)
                    act.activation(d_hi[:, :, :], down_sb[:, bass.ds(e, 1), :, :].rearrange("p a c n -> p (a c) n"),
                                   ACT.Copy).then_inc(d_high, 1)
                if k >= 2:
                    act.wait_ge(z_done, s - 1)
                    act.activation(e_z[b][:, :], e_z[b][:, :], ACT.Silu).then_inc(g_done, 1)
                if 0 <= k - 1 < ST:
                    act.wait_ge(eht_done, s)
                    act.activation(e_hh[1 - b][:, :, :], bank[5][:, :].rearrange("p (c n) -> p c n", c=HC),
                                   ACT.Copy).then_inc(hid_high, 1)
                if k < ST:
                    act.wait_ge(up_done, 2 * s + 1)
                    after(act, eht_done, s - 1)
                    act.activation(e_h[b][:, :], bank[3][:, :], ACT.Silu,
                                   scale=row_a[k % 4][:, D:D + 1]).then_inc(gate_done, 1)

            act.wait_ge(down_loaded, 16 * E)
            for k in range(4):
                step_c(k, 0)
            with act.Fori(0, (ST - 4) // 4) as i:
                for k in range(4, 8):
                    step_c(k, i)
            for k in range(ST // 4 * 4, ST + 2):
                step_c(k, 0)

        @block.vector
        def _(dve):
            V = nc.vector
            step = chain(dve, dve_n)
            for m, val in ((ones32, 1.0), (ones16, 1.0), (mean_w, 1.0 / D), (zeros16, 0.0)):
                V.memset(m[:, :], val).then_inc(consts_set, 1)
            step(V.memset(b_pick[:, :], 0.0))
            for part in range(3):
                last = V.memset(b_pick[32 * part:32 * part + 1, :], 1.0)
            last.then_inc(consts_set, 1)

            def stats(k, i, part):
                t = k + 4 * i
                m, v, into = mv2[:, k % 4, 0:1], mv2[:, k % 4, 1:2], tile_of(var_in, t)
                if part == 0:
                    dve.wait_ge(x_loaded, 16 * (k // 4 + i + 1))
                    V.bn_stats(st6[:, k % 4, :], tile_of(xs, t)).then_inc(st_n, 1)
                if part == 1:
                    dve.wait_ge(st_n, t + 1)
                    dve.sem_inc(dve_passed, 1)
                    V.bn_aggr(mv2[:, k % 4, :], st6[:, k % 4, :]).then_inc(aggr_done, 1)
                if part == 2:
                    dve.wait_ge(aggr_done, t + 1)
                    V.tensor_scalar(into[:, 0:1], v, LN_EPS, None, ALU.add).then_inc(var_n, 1)
                    V.tensor_scalar(neg_mean[:, bass.ds(t, 1)], m, -1.0, None, ALU.mult)
                if part == 3:
                    dve.wait_ge(var_n, t + 1)
                    V.reciprocal(inv_var[:, bass.ds(t, 1)], into[:, 0:1]).then_inc(inv_n, 1)
                if part == 4:
                    dve.wait_ge(inv_n, t + 1)
                    V.tensor_scalar(into[:, 1:2], v, inv_var[:, bass.ds(t, 1)], RMS_EPS, ALU.mult,
                                    ALU.add).then_inc(stats_done, 1)

            def low_part(k, i):
                t, s = k + 4 * i, k % 2
                dve.wait_ge(hi_done, t + 1)
                V.tensor_tensor(x_lo[s][:, :, :], bank[s][:, 0:D].rearrange("p (c n) -> p c n", c=DC),
                                x_hi[s][:, :, :].bitcast(F32), ALU.subtract).then_inc(lo_done, 1)

            dve.wait_ge(vec_turned, 1)
            step(V.tensor_copy(small[:, 48:64], bank[4][:, 64:80]))
            V.tensor_copy(vc[:, :], bank[4][:, 0:NV]).then_inc(vec_kept, 1)
            dve.wait_ge(vec_kept, 1)
            gain, beta = vc[:, G_:G_ + 8], vc[:, BETA_:BETA_ + 8]
            mag, inv, dead = (small[:, 8 * n:8 * n + 8] for n in (1, 2, 4))
            step(V.tensor_scalar(sgn, gain, 0.0, 2.0, ALU.is_ge, ALU.mult))
            step(V.tensor_tensor(small[:, 64:80], small[:, 48:64], small[:, 48:64], ALU.mult))
            V.tensor_scalar(sgn, sgn, -1.0, None, ALU.add).then_inc(cols_made, 1)
            for c in range(DC):
                V.tensor_scalar(w_cen[:, c, 3 * D:YW], small[:, 48 + E * c:56 + E * c],
                                vc[:, FS_ + c:FS_ + c + 1], None, ALU.mult)
            dve.wait_ge(cols_made, 1)
            step(V.tensor_tensor(mag, gain, sgn, ALU.mult))
            step(V.tensor_scalar(mag, mag, 1e-30, None, ALU.max))
            step(V.reciprocal(inv, mag))
            step(V.tensor_scalar(lim, beta, -1.0, 1.0, ALU.mult, ALU.add))
            step(V.tensor_tensor(lim, lim, inv, ALU.mult))
            step(V.tensor_scalar(dead, gain, 0.0, 1e20, ALU.is_equal, ALU.mult))
            dve.wait_ge(bias_mean, 1)
            step(V.tensor_copy(small[:, 88:96], bank[5][:, 0:8]))
            step(V.tensor_tensor(lim, lim, dead, ALU.subtract))
            V.tensor_scalar(lim, lim, 1.0 / 16, None, ALU.mult).then_inc(cols_made, 1)
            for p in range(4):
                dve.wait_ge(w_turned, p + 1)
                last = V.tensor_reduce(small[:, 96 + 2 * p:98 + 2 * p],
                                       bank[p][:, :].rearrange("p (c n) -> p c n", c=DC), AX.X, ALU.add)
            step(last)
            step(V.tensor_scalar(small[:, 96:104], small[:, 96:104], 1.0 / D, None, ALU.mult))
            for part in range(5):
                for k in range(4):
                    stats(k, 0, part)
            dve.wait_ge(sgn_kept, 1)
            for p in range(4):
                at = p * D if p < 3 else YW
                for c in range(DC):
                    last = V.scalar_tensor_tensor(w_cen[:, c, at:at + D], bank[p][:, c * D:(c + 1) * D],
                                                  small[:, 96 + 2 * p + c:97 + 2 * p + c], sgn_row[:, p, :],
                                                  ALU.subtract, ALU.mult)
            last.then_inc(w_centred, 1)
            bm, bc = small[:, 104:108], small[:, 112:120]
            step(V.tensor_tensor(bm, small[:, 88:96:2], small[:, 89:96:2], ALU.add))
            step(V.tensor_tensor(bc.rearrange("p (a b) -> p a b", b=2),
                                 vc[:, B_:B_ + 8].rearrange("p (a b) -> p a b", b=2),
                                 bm.unsqueeze(2).broadcast_to([P, 4, 2]), ALU.subtract))
            step(V.tensor_tensor(bc, bc, sgn, ALU.mult))
            step(V.tensor_copy(ident16[:, :], ident[:, :]))
            for part in range(3):
                last = V.tensor_copy(b16[:, 8 * part:8 * part + 8], bc)
                if part < 2:
                    step(last)
                    step(V.tensor_tensor(bc, bc, b16[:, 8 * part:8 * part + 8], ALU.subtract))
            last.then_inc(cols_made, 1)
            dve.wait_ge(cen_summed, 1)
            V.tensor_copy(fs_row[:, :], bank[7][:, 0:D]).then_inc(ny_kept, 1)
            V.tensor_copy(ny[:, :], bank[7][:, D:D + E]).then_inc(ny_kept, 1)
            dve.wait_ge(w_high, 2)
            V.tensor_tensor(w_lo[:, :, :], w_cen[:, :, 0:YW], w_hi[:, :, :].bitcast(F32), ALU.subtract)
            V.tensor_tensor(wo_lo[:, :, :], w_cen[:, :, YW:YW + D], wo_hi[:, :, :].bitcast(F32),
                            ALU.subtract).then_inc(setup_done, 1)
            low_part(0, 0)
            for part in range(5):
                for k in range(4, 8):
                    stats(k, 0, part)
            dve.wait_ge(thr_kept, 1)

            def spikes(k, i, n):
                t, s = k + 4 * i, k % 2
                r = tile_of(rs, t)
                source = bank[2 + s][:, n * D:(n + 1) * D] if n < 2 else bank[4 + s][:, 0:D]
                V.scalar_tensor_tensor(tile_of((q_sp, k_sp, v_sp)[n], t + (PAD if n == 2 else 0)), source,
                                       r[:, n:n + 1], thr[:, n * D:(n + 1) * D], ALU.mult, ALU.is_ge).then_inc(spiked, 1)

            def keep_dots(k, i):
                V.tensor_copy(tile_of(dots, k + 4 * i)[:, 0:E], bank[4 + k % 2][:, D:D + E]).then_inc(dots_done, 1)

            def keep_qt(k, i):
                t = k + 4 * i
                dve.wait_ge(qt_done, t + 1)
                V.tensor_copy(q_t[:, :, bass.ds(t * P, P)],
                              bank[7][:, 0:P].bitcast(BF16).rearrange("p (c n) -> p c n", c=DC)).then_inc(qt_kept, 1)

            def step_a(k, i, ahead):
                if 0 < k < NT:
                    low_part(k, i)
                if ahead:
                    stats(k + 8, i, 0)
                if ahead:
                    stats(k + 8, i, 1)
                if 0 <= k - 2 < NT:
                    dve.wait_ge(rs_done, k - 1 + 4 * i)
                for n in range(3):
                    if 0 <= k - 2 < NT:
                        spikes(k - 2, i, n)
                    if ahead:
                        stats(k + 8, i, n + 2)
                if 0 <= k - 2 < NT:
                    keep_dots(k - 2, i)
                if 0 <= k - 3 < NT:
                    keep_qt(k - 3, i)

            for k in range(4):
                step_a(k, 0, True)
            with dve.Fori(0, NT // 4 - 3) as i:
                for k in range(4, 8):
                    step_a(k, i, True)
            for k in range(NT - 8, NT + 3):
                step_a(k, 0, False)

            dve.wait_ge(sums_done, NT)
            V.tensor_copy(sc16[:, :], bank[6][:, D:2 * D]).then_inc(m_done, 1)
            dve.wait_ge(sv_done, 1)
            dve.wait_ge(nx_done, NT)
            step(V.tensor_copy(sv_row[:, :], bank[7][:, 0:D]))
            step(V.scalar_tensor_tensor(m_f[:, :], bank[6][:, 0:D], 2.0, sv_row[:, :], ALU.mult, ALU.subtract))
            step(V.tensor_tensor(m_f[:, :].rearrange("p (c n) -> p c n", c=DC),
                                 m_f[:, :].rearrange("p (c n) -> p c n", c=DC),
                                 head.unsqueeze(1).broadcast_to([P, DC, P]), ALU.mult))
            step(V.tensor_copy(m_hi[:, :], m_f[:, :]))
            V.tensor_tensor(m_lo[:, :], m_f[:, :], m_hi[:, :], ALU.subtract).then_inc(m_done, 1)

            over_e = lambda m: m.unsqueeze(2).broadcast_to([P, NT, E])
            over_t = lambda m: m.unsqueeze(1).broadcast_to([P, NT, E])
            A, B, HOT = ra[:, :, :], rb[:, :, :], hot[:, :, :]
            nx, rms = (m.rearrange("p t a -> p (t a)") for m in (dots[:, :, E:E + 1], inv_std[:, :, 1:2]))
            dve.wait_ge(dots_done, NT)
            dve.wait_ge(nx_done, NT)
            dve.wait_ge(tables_made, 4)
            step(V.tensor_tensor(A, dots[:, :, 0:E], over_e(rms), ALU.mult))
            step(V.tensor_tensor(rt[:, 0, :], nx, rms, ALU.mult))
            step(V.tensor_tensor(rt[:, 0, :], rt[:, 0, :], rms, ALU.mult))
            step(V.scalar_tensor_tensor(A, A, -2.0, over_t(ny[:, :]), ALU.mult, ALU.add))
            step(V.tensor_tensor(A, A, over_e(rt[:, 0, :]), ALU.add))
            step(V.tensor_reduce(rt[:, 1, :], A, AX.X, ALU.min))
            step(V.tensor_tensor(B, A, over_e(rt[:, 1, :]), ALU.is_equal))
            step(V.scalar_tensor_tensor(B, B, -float(E), over_t(eidx[:, :]), ALU.mult, ALU.add))
            step(V.tensor_reduce(rt[:, 1, :], B, AX.X, ALU.min))
            step(V.tensor_scalar(rt[:, 1, :], rt[:, 1, :], float(E), None, ALU.add))
            step(V.tensor_tensor(HOT, over_t(eidx[:, :]), over_e(rt[:, 1, :]), ALU.is_equal))
            V.tensor_copy(hot16[:, :, :], HOT).then_inc(hot_done, 1)
            def attention_spikes(k, i):
                c, s = k + 2 * i, k % 2
                after(dve, wo_done, 2 * (c - 1))
                for h in range(DC):
                    dve.wait_ge(at_done, DC * c + h + 1)
                    V.tensor_scalar(a_sp[s][:, h, :], bank[h][:, :], scale, thr2[:, h:h + 1], ALU.mult,
                                    ALU.is_ge).then_inc(at_spiked, 1)

            scale = vc[:, SCALE_:SCALE_ + 1]
            dve.wait_ge(cvec_done, 1)
            step(V.tensor_scalar(thr2[:, :], bank[7][:, 0:DC], scale, 0.5, ALU.mult, ALU.mult))
            step(V.tensor_scalar(thr2[:, :], thr2[:, :], 0.5, None, ALU.add))
            attention_spikes(0, 0)
            dve.wait_ge(ranks_done, 1)
            step(V.tensor_copy(A, bank[6][:, NT * E:2 * NT * E].rearrange("p (t e) -> p t e", e=E)))
            for e in range(E):
                last = V.tensor_tensor_scan(rb[:, :, e], ones32[:, 0:NT], ra[:, :, e], 0.0, ALU.mult, ALU.add)
            step(last)
            step(V.tensor_tensor(A, B, A, ALU.subtract))
            step(V.tensor_copy(r8[:, 0, :], rb[:, NT - 1, :]))
            step(V.tensor_tensor(A, bank[6][:, 0:NT * E].rearrange("p (t e) -> p t e", e=E), A, ALU.add))
            by_e = rb[:, :, :].rearrange("p t e -> p (t e)").rearrange("p (e t) -> p e t", e=E)
            step(V.tensor_tensor(by_e, r8[:, 0, :].unsqueeze(2).broadcast_to([P, E, NT]),
                                 lev[:, :].unsqueeze(1).broadcast_to([P, E, NT]), ALU.is_gt))
            step(V.tensor_reduce(r8[:, 1, :], by_e, AX.X, ALU.add))
            step(V.tensor_tensor_scan(r8[:, 2, :], ones32[:, 0:E], r8[:, 1, :], 0.0, ALU.mult, ALU.add))
            step(V.tensor_tensor(r8[:, 3, :], r8[:, 2, :], r8[:, 1, :], ALU.subtract))
            step(V.tensor_scalar(r8[:, 3, :], r8[:, 3, :], float(P), None, ALU.mult))
            step(V.tensor_tensor(A, A, over_t(r8[:, 3, :]), ALU.add))
            step(V.tensor_tensor(A, A, HOT, ALU.mult))
            step(V.tensor_reduce(rt[:, 2, :], A, AX.X, ALU.add))
            V.tensor_copy(pos[:, :], rt[:, 2, :]).then_inc(pos_done, 1)
            step(V.tensor_tensor(tcmp[:, :, :], r8[0:1, 2, :].unsqueeze(1).broadcast_to([1, ST, E]),
                                 tile_no[0:1, :].unsqueeze(2).broadcast_to([1, ST, E]), ALU.is_le))
            step(V.tensor_reduce(tex[:, :], tcmp[:, :, :], AX.X, ALU.add))
            V.tensor_scalar(expert[:, :], tex[:, :], float(E - 1), None, ALU.min).then_inc(pos_done, 1)

            def output_spikes(k, i):
                c, s = k + 2 * i, k % 2
                if c >= 2:
                    dve.wait_ge(s_put[s], 16 * (c // 2))
                for pair in range(2):
                    dve.wait_ge(wo_rs, 2 * c + pair + 1)
                    for n in range(2):
                        tl = 2 * pair + n
                        V.scalar_tensor_tensor(s_out[s][:, tl, :], bank[2 + 2 * s + pair][:, n * D:(n + 1) * D],
                                               tile_of(rs, c * CH + tl)[:, 3:4], thr[:, 3 * D:4 * D],
                                               ALU.mult, ALU.is_ge).then_inc(s_made, 1)

            def low_parts(c):
                for e, half in SPLITS[c]:
                    dve.wait_ge(up_high, SPLIT_ORDER.index((e, half)) + 1)
                    last = V.scalar_tensor_tensor(up_lo[:, e, half, :], up_raw[:, e, half, :],
                                                  vc[:, FS_ + half:FS_ + half + 1],
                                                  up_hi[:, e, half, :].bitcast(F32), ALU.mult, ALU.subtract)
                    if half == 1:
                        last.then_inc(up_ready, 1)

            for c in range(1, NCH):
                attention_spikes(c % 2, c // 2)
                if c == NCH - 1:
                    low_parts(c)
                output_spikes((c - 1) % 2, (c - 1) // 2)
                if c in SPLITS and c < NCH - 1:
                    low_parts(c)
            low_parts(NCH)

            def turned_low(k, i):
                s = k + 4 * i
                dve.wait_ge(ext_high, s + 1)
                after(dve, up_done, 2 * (s - 1))
                V.tensor_tensor(e_xl[k % 2][:, :, :], bank[7][:, 0:D].rearrange("p (c n) -> p c n", c=DC),
                                e_xh[k % 2][:, :, :].bitcast(F32), ALU.subtract).then_inc(ext_kept, 1)

            turned_low(0, 0)
            output_spikes((NCH - 1) % 2, NCH // 2 - 1)
            low_parts(NCH + 1)

            def step_c(k, i):
                s, b = k + 4 * i, k % 2
                if 0 < k < ST:
                    turned_low(k, i)
                if 0 <= k - 1 < ST:
                    e = dve.value_load(expert[0:1, bass.ds(s - 1, 1)], min_val=0, max_val=E - 1)
                if 0 <= k - 2 < ST:
                    dve.wait_ge(down_done, s - 1)
                    after(dve, sg_done, s - 3)
                    V.tensor_tensor(e_z[b][:, :], bank[b][:, 0:D], row_a[(k - 2) % 4][:, 0:D], ALU.add).then_inc(z_done, 1)
                if 0 <= k - 1 < ST:
                    dve.wait_ge(d_high, s)
                    V.tensor_tensor(d_lo[:, :, :], down_sb[:, bass.ds(e, 1), :, :].rearrange("p a c n -> p (a c) n"),
                                    d_hi[:, :, :].bitcast(F32), ALU.subtract).then_inc(d_low, 1)
                    dve.wait_ge(hid_high, s)
                    V.tensor_tensor(e_hl[1 - b][:, :, :], bank[5][:, :].rearrange("p (c n) -> p c n", c=HC),
                                    e_hh[1 - b][:, :, :].bitcast(F32), ALU.subtract).then_inc(eht_kept, 1)
                if 0 <= k - 2 < ST:
                    dve.wait_ge(g_done, s - 1)
                    if k - 2 >= 4:
                        dve.wait_ge(sent[(k - 2) % 4], 16 * ((k - 2) // 4 + i))
                    dve.wait_ge(got_s[(k - 2) % 4], 16 * ((k - 2) // 4 + i + 1))
                    o = e_o[(k - 2) % 4]
                    V.tensor_tensor(o[:, :], e_z[b][:, :], row_s[(k - 2) % 4][:, :], ALU.mult).then_inc(sg_done, 1)
                    dve.wait_ge(sg_done, s - 1)
                    V.tensor_tensor(o[:, :], o[:, :], row_a[(k - 2) % 4][:, D + 1:2 * D + 1], ALU.add).then_inc(o_done, 1)
                if k < ST:
                    dve.wait_ge(gate_done, s + 1)
                    dve.wait_ge(up_done, 2 * s + 2)
                    V.scalar_tensor_tensor(e_h[b][:, :], bank[2][:, :], row_a[k % 4][:, D:D + 1], e_h[b][:, :],
                                           ALU.mult, ALU.mult).then_inc(act_done, 1)

            for k in range(4):
                step_c(k, 0)
            with dve.Fori(0, (ST - 4) // 4) as i:
                for k in range(4, 8):
                    step_c(k, i)
            for k in range(ST // 4 * 4, ST + 2):
                step_c(k, 0)

        @block.gpsimd
        def _(pool):
            G = nc.gpsimd
            step = chain(pool, pool_n)

            def held(s, count):
                after(pool, s, count)
                pool.sem_inc(pool_passed, 1)

            G.iota(none[:, :], [[0, P]], base=N, channel_multiplier=0).then_inc(none_made, 1)
            G.memset(eps3[:, :], D * LN_EPS)
            step(G.memset(half_neg[:, :, :], -0.5))
            G.iota(ids[:, :], [[P, NT]], base=0, channel_multiplier=1).then_inc(tables_made, 1)
            G.iota(eidx[:, :], [[1, E]], base=E, channel_multiplier=0,
                   allow_small_or_imprecise_dtypes=True).then_inc(tables_made, 1)
            G.iota(lev[:, :], [[P, NT]], base=0, channel_multiplier=0,
                   allow_small_or_imprecise_dtypes=True).then_inc(tables_made, 1)
            G.iota(tile_no[:, :], [[1, ST]], base=0, channel_multiplier=0,
                   allow_small_or_imprecise_dtypes=True).then_inc(tables_made, 1)
            for first in (0, PAD + NT):
                last = G.memset(v_sp[:, first:first + PAD, :], 0.0)
            last.then_inc(pads_cleared, 1)
            pool.wait_ge(ld_t, 16)
            G.tensor_scalar(neg16[:, :], sum_rows[:, 0:2], -16.0, None, ALU.mult).then_inc(neg_made, 1)

            def inverse_stds(pair):
                held(stats_done, 2 * (pair + 1))
                two = bass.ds(2 * pair, 2)
                G.tensor_tensor(inv_std[:, two, :], var_in[:, two, :], half_neg[:, :, :], ALU.pow).then_inc(group_n, 1)
                held(group_n, pair + 1)
                G.tensor_tensor(nmr[:, two], inv_std[:, two, 0:1].rearrange("p a b -> p (a b)"), neg_mean[:, two],
                                ALU.mult).then_inc(rstd_done, 1)

            def put_rms(k, i):
                t = k + 4 * i
                held(xn_done, t + 1)
                G.tensor_copy(xn[k % 4][:, D:D + 1],
                              inv_std[:, bass.ds(t, 1), 1:2].rearrange("p a b -> p (a b)")).then_inc(rms_put, 1)

            def norms(k, i):
                t, s = k + 4 * i, k % 2
                held(squared, 3 * (t + 1))
                held(rs_done, t - 1)
                G.tensor_tensor(pv[:, s, 0:3], tile_of(ss, t)[:, 0:3], eps3[:, :], ALU.add).then_inc(norm_n, 1)
                held(norm_n, t + 1)
                halves = half_neg[:, :, :].rearrange("p a b -> p (a b)")[:, 0:3]
                G.tensor_tensor(tile_of(rs, t)[:, 0:3], pv[:, s, 0:3], halves, ALU.pow).then_inc(rs_done, 1)

            def scaled(k, i):
                t = k + 4 * i
                held(nx_done, t - 1)
                G.tensor_tensor(sq[k % 2][:, :], xn[k % 4][:, 0:D], fs_row[:, :], ALU.mult).then_inc(sq_done, 1)

            def step_a(k, i, ahead):
                if k >= 1:
                    norms(k - 1, i)
                if k < NT:
                    put_rms(k, i)
                    scaled(k, i)
                if ahead and k % 2 == 1:
                    inverse_stds(k // 2 + 2 * i + 3)

            for pair in range(3):
                inverse_stds(pair)
            pool.wait_ge(ny_kept, 2)
            for k in range(4):
                step_a(k, 0, True)
            with pool.Fori(0, NT // 4 - 3) as i:
                for k in range(4, 8):
                    step_a(k, i, True)
            for k in range(NT - 8, NT + 1):
                step_a(k, 0, k < NT - 6)

            def number(c0, c1):
                for t in range(c0, c1):
                    G.indirect_dma_start(slots, bass.IndirectOffsetOnAxis(ap=pos[:, t:t + 1], axis=0),
                                         ids[:, t:t + 1], None, bounds_check=ST * P - 1,
                                         oob_is_err=False).then_inc(id_put, 16)

            def norms_out(k, i):
                c = k + 2 * i
                for pair in range(2):
                    of = lambda buffer: buffer[:, bass.ds(c * CH + 2 * pair, 2), 3:4].rearrange("p a b -> p (a b)")
                    held(wo_sq, CH * c + 2 * pair + 2)
                    held(wo_rs, 2 * c + pair - 1)
                    G.tensor_tensor(pv[:, pair, 0:2], of(ss), eps3[:, 0:2], ALU.add).then_inc(out_n, 1)
                    held(out_n, 2 * c + pair + 1)
                    G.tensor_tensor(of(rs), pv[:, pair, 0:2], half_neg[:, 0, :], ALU.pow).then_inc(wo_rs, 1)

            for k in range(4):
                pool.wait_ge(row_put[k], 16 * NT // 4)
            pool.wait_ge(xt_done, NT)
            for k in range(4):
                G.memset(row_a[k][:, :], 0.0)
                last = G.memset(row_s[k][:, :], 0.0)
            last.then_inc(rows_clear, 1)
            def gather_a(k, i):
                s = k + 4 * i
                if k >= 4:
                    held(got_a[k % 4], 16 * (k // 4 + i))
                    held(got_s[k % 4], 16 * (k // 4 + i))
                G.tensor_copy(from_id[k % 4][:, :], slot_id[:, bass.ds(s, 1)]).then_inc(from_n, 1)
                held(from_n, s + 1)
                held(o_done, s - 3)
                G.indirect_dma_start(row_a[k % 4][:, :], None, rows_a,
                                     bass.IndirectOffsetOnAxis(ap=from_id[k % 4][:, :], axis=0),
                                     bounds_check=N - 1, oob_is_err=False).then_inc(got_a[k % 4], 16)

            def gather_s(k):
                G.indirect_dma_start(row_s[k % 4][:, :], None, rows_s,
                                     bass.IndirectOffsetOnAxis(ap=from_id[k % 4][:, :], axis=0),
                                     bounds_check=N - 1, oob_is_err=False).then_inc(got_s[k % 4], 16)

            def gather(k, i):
                gather_a(k, i)
                gather_s(k)

            pool.wait_ge(pos_done, 1)
            pool.wait_ge(none_put, 16)
            done = 0
            for c in range(NCH):
                if c < 6:
                    upto = min(NT, 5 + 6 * c)
                    number(done, upto)
                    done = upto
                if c == 6:
                    pool.wait_ge(ids_back, 16)
                    pool.wait_ge(x_copied, 16 * NT // 4)
                    pool.wait_ge(rows_clear, 1)
                    for k in range(4):
                        gather_a(k, 0)
                norms_out(c % 2, c // 2)
            for k in range(2):
                pool.wait_ge(s_put[k], 16 * NCH // 2)
            for k in range(4):
                gather_s(k)

            def scatter(k, i):
                s = k + 4 * i
                if k >= 4:
                    held(sent[k % 4], 16 * (k // 4 + i))
                G.tensor_copy(to_id[k % 4][:, :], slot_id[:, bass.ds(s, 1)]).then_inc(to_n, 1)
                held(to_n, s + 1)
                held(o_done, s + 1)
                G.indirect_dma_start(out, bass.IndirectOffsetOnAxis(ap=to_id[k % 4][:, :], axis=0),
                                     e_o[k % 4][:, :], None, bounds_check=N - 1,
                                     oob_is_err=False).then_inc(sent[k % 4], 16)

            for k in range(4, 8):
                gather(k, 0)
                scatter(k - 4, 0)
            with pool.Fori(0, (ST - 11) // 4) as i:
                for k in range(8, 12):
                    gather(k, i)
                    scatter(k - 4, i)
            for k in range(36, ST):
                gather(k, 0)
                scatter(k - 4, 0)
            for k in range(ST - 4, ST):
                scatter(k, 0)
            for k in range(4):
                pool.wait_ge(sent[k], 16 * ((ST - k + 3) // 4))


_NAMES = {"x": "L0_attn_query", "wq": "L0_attn_Wq", "wk": "L0_attn_Wk", "wv": "L0_attn_Wv", "wo": "L0_attn_Wo",
          "centroids": "L0_ffn_centroids", "up_w": "L0_ffn_up_w", "down_w": "L0_ffn_down_w"}
_VECTORS = ["L0_attn_gq", "L0_attn_gk", "L0_attn_gv", "L0_attn_go", "L0_attn_bq", "L0_attn_bk", "L0_attn_bv",
            "L0_attn_bo", "L0_attn_betaq", "L0_attn_betak", "L0_attn_betav", "L0_attn_betao", "L0_ffn_scale"]


def _shape_constants():
    import numpy as np

    def bias(dist):
        n = dist + 1
        level = 12 - np.floor(np.log2(n)).astype(np.int64)
        return np.where(n >= N - 1, 0, level)

    a, b = np.arange(P)[None, :], np.arange(P)[:, None]
    col = np.arange(3 * P)[None, :]
    near = bias(np.abs(col - P - b))
    tri = np.stack([(a - b <= -2), (b - a <= -2)], 1).reshape(P, 2 * P)
    pick = np.zeros((P, 64, 4))
    pick[:, 31, 0] = 1
    pick[0, 31, 1] = 1
    pick[P - 1, 31, 2] = 1
    pick[1, 0, 3] = 1
    pick[P - 2, 62, 3] = 1
    scan = (b < a)
    head = (a // 16 == b // 16)
    sums = np.broadcast_to(b % 4 == 0, (P, P))
    consts = np.concatenate([near, tri, pick.reshape(P, 256), scan, head, sums], 1)

    blocks = np.zeros((4, 32, NT, P))
    for r in range(32):
        j = 31 - r
        for t in range(NT):
            k = abs(t - j)
            if k >= 2:
                blocks[0, r, t, :] = 12 - int(np.floor(np.log2(P * k)))
            if k >= 2 and (k + 1) & k == 0:
                if t > j:
                    blocks[1, r, t, P - 1] = -1
                else:
                    blocks[2, r, t, 0] = -1
    blocks[1, 31, NT - 1, P - 2] = -1
    blocks[3, 0, NT - 1, P - 1] = -1
    blocks[2, 0, 0, 1] = -1
    blocks[3, 31, 0, 0] = -1
    bits = lambda m: np.ascontiguousarray(np.ascontiguousarray(m, np.float32).view(np.uint16)[:, 1::2])
    return bits(consts), bits(blocks.transpose(1, 0, 2, 3).reshape(P, N)), np.eye(P, dtype=np.float32)


def kernel(**inputs):
    import numpy as _np
    import concourse.bacc as _bacc
    from concourse import mybir as _mybir
    from concourse.bass_utils import run_bass_kernel_spmd as _run

    nc = _bacc.Bacc("TRN2", target_bir_lowering=False, num_devices=1)
    arrays = {k: _np.ascontiguousarray(inputs[v]) for k, v in _NAMES.items()}
    arrays["x"] = arrays["x"].reshape(N, D)
    rows = [_np.asarray(inputs[n]).reshape(DC, P) for n in _VECTORS]
    rows.append(_np.broadcast_to(_np.asarray(inputs["L0_attn_scale"]).reshape(1, 1), (1, P)))
    arrays["vectors"] = _np.ascontiguousarray(_np.concatenate(rows, 0))
    arrays["consts"], arrays["blocks"], arrays["eye"] = _shape_constants()
    order = ["x", "wq", "wk", "wv", "wo", "vectors", "centroids", "up_w", "down_w", "consts", "blocks", "eye"]
    args = [nc.dram_tensor(f"in_{k}", arrays[k].shape, _mybir.dt.from_np(arrays[k].dtype), kind="ExternalInput").ap()
            for k in order]
    out = nc.dram_tensor("out_x", (N, D), F32, kind="ExternalOutput").ap()
    build(nc, *args, out)
    r = _run(nc, [{f"in_{k}": arrays[k] for k in order}], core_ids=[0])
    return r.results[0]["out_x"].reshape(1, N, D)
```
